# Optimizing a Trainium2 kernel written in Bass

```python
import numpy as np
import jax
import jax.numpy as jnp

def _softmax(x, axis=-1):
    return jax.nn.softmax(x, axis=axis)

def _gelu(x):
    return jax.nn.gelu(x, approximate=True)

def _silu(x):
    return jax.nn.silu(x)

def _sigmoid(x):
    return jax.nn.sigmoid(x)

def _layernorm(x, axis=-1, eps=1e-05):
    m = jnp.mean(x, axis=axis, keepdims=True)
    v = jnp.var(x, axis=axis, keepdims=True)
    return (x - m) / jnp.sqrt(v + eps)

def _scatter_add(tgt, idx, src, axis=0):
    return tgt.at[idx].add(src)

def _segment_sum(src, seg, n):
    return jax.ops.segment_sum(src, seg, n)
kernel_name = 'mk_flamingo_gated_d2_seqx_r8_eb0f34'

def setup_inputs(seed: int=0):
    np.random.seed(seed)
    _w = jnp.asarray

    def _rec_inputs():
        import jax
        import jax.numpy as jnp
        _rk = jax.random.key(seed)
        x = 7.22e-05 + 1 * jax.random.normal(jax.random.fold_in(_rk, 1), (64, 64, 256), jnp.float32)
        _lenS = 64 - jax.random.randint(jax.random.fold_in(_rk, 7), (64,), 0, max(1, 64 // 4) + 1, jnp.int32)
        _lenS2 = 64 - jax.random.randint(jax.random.fold_in(_rk, 8), (64,), 0, max(1, 64 // 4) + 1, jnp.int32)
        _ctx_1024P = jax.random.normal(jax.random.fold_in(_rk, 11), (64, 16, 128), jnp.float32)
        _ctx_1024c = jax.random.dirichlet(jax.random.fold_in(_rk, 511), 0.3 * jnp.ones((16,), jnp.float32), (64, 64))
        _ctx_1024t = jnp.einsum('bsk,bkd->bsd', _ctx_1024c, _ctx_1024P)
        _ctx_1024t = _ctx_1024t * jax.lax.rsqrt(jnp.mean(jnp.square(_ctx_1024t)) + 1e-12) * 0.953939
        ctx_1024 = -1.39393e-06 + 0.999914 * (_ctx_1024t + 0.3 * jax.random.normal(jax.random.fold_in(_rk, 611), (64, 64, 128), jnp.float32))
        fside_BxSx2_0 = jax.random.uniform(jax.random.fold_in(_rk, 12), (64, 64, 2), jnp.float32, 0.0, 0.999707)
        _validS = jnp.arange(64)[None, :] < _lenS[:, None]
        _validS2 = jnp.arange(64)[None, :] < _lenS2[:, None]
        _causal = jnp.tril(jnp.ones((64, 64), dtype=bool))
        mask_BxS2_bf1 = jnp.ones((64, 64), dtype=bool)
        _g = jax.random.normal(jax.random.fold_in(_rk, 9001), (2, 2), jnp.float32)
        _g = jnp.sign(_g) * jnp.maximum(jnp.abs(_g), 1.0) + (_g == 0) * 1.0
        g_xattn = _g[0]
        g_ffn = _g[1]
        return (x, ctx_1024, fside_BxSx2_0, mask_BxS2_bf1, g_xattn, g_ffn)
    x, ctx_1024, fside_BxSx2_0, mask_BxS2_bf1, g_xattn, g_ffn = _rec_inputs()

    def _L0_xattn_setup():
        import jax, jax.numpy as jnp
        import numpy as np
        DIM = 256
        CTX_DIM = 128
        N_HEADS = 32
        HEAD_DIM = DIM // N_HEADS
        POS_DIM = 2
        B, N, CTXN = (2, 256, 256)
        ROPE_BASE = 10000.0

        def apply_axial_rope(x, pos):
            b, n, h, d = x.shape
            p = pos.shape[-1]
            dpa = d // p
            half = dpa // 2
            freqs = ROPE_BASE ** (-jnp.arange(half, dtype=x.dtype) / half)
            ang = pos[..., :, None] * freqs
            cos = jnp.cos(ang)[:, :, None, :, :]
            sin = jnp.sin(ang)[:, :, None, :, :]
            xr = x.reshape(b, n, h, p, half, 2)
            x1, x2 = (xr[..., 0], xr[..., 1])
            out = jnp.stack([x1 * cos - x2 * sin, x1 * sin + x2 * cos], axis=-1)
            return out.reshape(b, n, h, d)
        key = jax.random.key(seed)
        ks = jax.random.split(key, 8)
        x = jax.random.normal(ks[0], (B, N, DIM), jnp.float32)
        ctx = jax.random.normal(ks[1], (B, CTXN, CTX_DIM), jnp.float32)
        pos_map = jax.random.uniform(ks[2], (B, N, POS_DIM), jnp.float32)
        ctx_pos_map = jax.random.uniform(ks[3], (B, CTXN, POS_DIM), jnp.float32)
        Wq = jax.random.normal(ks[4], (DIM, DIM), jnp.float32) / np.sqrt(DIM)
        Wkv = jax.random.normal(ks[5], (CTX_DIM, 2 * DIM), jnp.float32) / np.sqrt(CTX_DIM)
        Wout = jax.random.normal(ks[6], (DIM, DIM), jnp.float32) / np.sqrt(DIM)
        bout = jnp.zeros((DIM,), jnp.float32)
        return {'x': x, 'ctx': ctx, 'pos_map': pos_map, 'ctx_pos_map': ctx_pos_map, 'Wq': Wq, 'Wkv': Wkv, 'Wout': Wout, 'bout': bout}
    _L0_xattn_all = _L0_xattn_setup()
    _L0_xattn_in = {k: v for k, v in _L0_xattn_all.items() if k in ('Wq', 'Wkv', 'Wout', 'bout')}
    del _L0_xattn_all

    def _L0_ffn_setup():
        import jax, jax.numpy as jnp
        import numpy as np
        E = 8
        TOP_K = 2
        H = 256
        I_MOE = 176
        I_SH = 704
        B, S = (2, 256)

        def _moe_forward(hidden_states, router_weight, gate_up_proj, down_proj, sh_gate_w, sh_up_w, sh_down_w, shared_gate_w):
            b, s, h = hidden_states.shape
            x = hidden_states.reshape(-1, h)
            shared = jnp.einsum('ti,hi->th', jax.nn.silu(x @ sh_gate_w.T) * (x @ sh_up_w.T), sh_down_w)
            logits = x @ router_weight.T
            probs = jax.nn.softmax(logits.astype(jnp.float32), axis=-1)
            top_v, top_i = jax.lax.top_k(probs, TOP_K)
            top_v = top_v / top_v.sum(axis=-1, keepdims=True)
            combine = (jax.nn.one_hot(top_i, E, dtype=top_v.dtype) * top_v[..., None]).sum(axis=1)
            out = jnp.zeros_like(x)
            for e in range(E):
                gu = x @ gate_up_proj[e].T
                gate, up = (gu[:, :I_MOE], gu[:, I_MOE:])
                cur = jax.nn.silu(gate) * up @ down_proj[e].T
                out = out + cur * combine[:, e:e + 1]
            out = out + jax.nn.sigmoid(x @ shared_gate_w.T) * shared
            return out.reshape(b, s, h)
        key = jax.random.key(seed)
        ks = jax.random.split(key, 8)
        scale = 0.02
        return {'hidden_states': jax.random.normal(ks[0], (B, S, H), dtype=jnp.float32), 'router_weight': jax.random.normal(ks[1], (E, H), dtype=jnp.float32) * scale, 'gate_up_proj': jax.random.normal(ks[2], (E, 2 * I_MOE, H), dtype=jnp.float32) * scale, 'down_proj': jax.random.normal(ks[3], (E, H, I_MOE), dtype=jnp.float32) * scale, 'sh_gate_w': jax.random.normal(ks[4], (I_SH, H), dtype=jnp.float32) * scale, 'sh_up_w': jax.random.normal(ks[5], (I_SH, H), dtype=jnp.float32) * scale, 'sh_down_w': jax.random.normal(ks[6], (H, I_SH), dtype=jnp.float32) * scale, 'shared_gate_w': jax.random.normal(ks[7], (1, H), dtype=jnp.float32) * scale}
    _L0_ffn_all = _L0_ffn_setup()
    _L0_ffn_in = {k: v for k, v in _L0_ffn_all.items() if k in ('router_weight', 'gate_up_proj', 'down_proj', 'sh_gate_w', 'sh_up_w', 'sh_down_w', 'shared_gate_w')}
    del _L0_ffn_all

    def _L1_xattn_setup():
        import jax, jax.numpy as jnp
        import numpy as np
        N_HEADS = 16
        N_KV_HEADS = 8
        HEAD_DIM = 128
        D_TEXT = 256
        D_VISION = 128
        GROUPS = N_HEADS // N_KV_HEADS
        key = jax.random.key(seed)
        ks = jax.random.split(key, 6)
        B, T_text, T_vis = (4, 256, 72)
        text_hidden = jax.random.normal(ks[0], (B, T_text, D_TEXT), dtype=jnp.float32)
        vision_tokens = jax.random.normal(ks[1], (B, T_vis, D_VISION), dtype=jnp.float32)
        vision_mask = jnp.ones((B, T_vis), dtype=bool)
        s = 0.02
        Wq = jax.random.normal(ks[2], (D_TEXT, N_HEADS * HEAD_DIM), dtype=jnp.float32) * s
        Wk = jax.random.normal(ks[3], (D_VISION, N_KV_HEADS * HEAD_DIM), dtype=jnp.float32) * s
        Wv = jax.random.normal(ks[4], (D_VISION, N_KV_HEADS * HEAD_DIM), dtype=jnp.float32) * s
        Wo = jax.random.normal(ks[5], (N_HEADS * HEAD_DIM, D_TEXT), dtype=jnp.float32) * s
        return {'text_hidden': text_hidden, 'vision_tokens': vision_tokens, 'vision_mask': vision_mask, 'Wq': Wq, 'Wk': Wk, 'Wv': Wv, 'Wo': Wo}
    _L1_xattn_all = _L1_xattn_setup()
    _L1_xattn_in = {k: v for k, v in _L1_xattn_all.items() if k in ('Wq', 'Wk', 'Wv', 'Wo')}
    del _L1_xattn_all

    def _L1_ffn_setup():
        import jax, jax.numpy as jnp
        import numpy as np
        D = 256
        H_TOTAL = 1024
        E = 8
        K = 2
        HE = H_TOTAL // E
        B, S = (2, 256)
        key = jax.random.key(seed)
        ks = jax.random.split(key, 8)
        scale_up = 1.0 / np.sqrt(D)
        scale_dn = 1.0 / np.sqrt(HE)
        return {'x': jax.random.normal(ks[0], (B, S, D), dtype=jnp.float32), 'Wg1': jax.random.normal(ks[1], (E, D), dtype=jnp.float32) * 0.02, 'Wg2': jax.random.normal(ks[2], (E, E), dtype=jnp.float32) * 0.2, 'Wup': jax.random.uniform(ks[3], (E, HE, D), dtype=jnp.float32, minval=-scale_up, maxval=scale_up), 'bup': jax.random.uniform(ks[4], (E, HE), dtype=jnp.float32, minval=-scale_up, maxval=scale_up), 'Wdown': jax.random.uniform(ks[5], (E, D, HE), dtype=jnp.float32, minval=-scale_dn, maxval=scale_dn), 'bdown': jax.random.uniform(ks[6], (E, D), dtype=jnp.float32, minval=-scale_dn, maxval=scale_dn)}
    _L1_ffn_all = _L1_ffn_setup()
    _L1_ffn_in = {k: v for k, v in _L1_ffn_all.items() if k in ('Wg1', 'Wg2', 'Wup', 'bup', 'Wdown', 'bdown')}
    del _L1_ffn_all
    return {'x': x, 'ctx_1024': ctx_1024, 'fside_BxSx2_0': fside_BxSx2_0, 'mask_BxS2_bf1': mask_BxS2_bf1, 'g_xattn': g_xattn, 'g_ffn': g_ffn, 'L0_xattn_Wq': _L0_xattn_in['Wq'], 'L0_xattn_Wkv': _L0_xattn_in['Wkv'], 'L0_xattn_Wout': _L0_xattn_in['Wout'], 'L0_xattn_bout': _L0_xattn_in['bout'], 'L0_ffn_router_weight': _L0_ffn_in['router_weight'], 'L0_ffn_gate_up_proj': _L0_ffn_in['gate_up_proj'], 'L0_ffn_down_proj': _L0_ffn_in['down_proj'], 'L0_ffn_sh_gate_w': _L0_ffn_in['sh_gate_w'], 'L0_ffn_sh_up_w': _L0_ffn_in['sh_up_w'], 'L0_ffn_sh_down_w': _L0_ffn_in['sh_down_w'], 'L0_ffn_shared_gate_w': _L0_ffn_in['shared_gate_w'], 'L1_xattn_Wq': _L1_xattn_in['Wq'], 'L1_xattn_Wk': _L1_xattn_in['Wk'], 'L1_xattn_Wv': _L1_xattn_in['Wv'], 'L1_xattn_Wo': _L1_xattn_in['Wo'], 'L1_ffn_Wg1': _L1_ffn_in['Wg1'], 'L1_ffn_Wg2': _L1_ffn_in['Wg2'], 'L1_ffn_Wup': _L1_ffn_in['Wup'], 'L1_ffn_bup': _L1_ffn_in['bup'], 'L1_ffn_Wdown': _L1_ffn_in['Wdown'], 'L1_ffn_bdown': _L1_ffn_in['bdown']}

def reference(x, ctx_1024, fside_BxSx2_0, mask_BxS2_bf1, g_xattn, g_ffn, L0_xattn_Wq, L0_xattn_Wkv, L0_xattn_Wout, L0_xattn_bout, L0_ffn_router_weight, L0_ffn_gate_up_proj, L0_ffn_down_proj, L0_ffn_sh_gate_w, L0_ffn_sh_up_w, L0_ffn_sh_down_w, L0_ffn_shared_gate_w, L1_xattn_Wq, L1_xattn_Wk, L1_xattn_Wv, L1_xattn_Wo, L1_ffn_Wg1, L1_ffn_Wg2, L1_ffn_Wup, L1_ffn_bup, L1_ffn_Wdown, L1_ffn_bdown):
    import jax
    import jax.numpy as jnp

    def _L0_xattn_ref(x, ctx, pos_map, ctx_pos_map, Wq, Wkv, Wout, bout):
        import jax, jax.numpy as jnp
        import numpy as np
        DIM = 256
        CTX_DIM = 128
        N_HEADS = 32
        HEAD_DIM = DIM // N_HEADS
        POS_DIM = 2
        B, N, CTXN = (2, 256, 256)
        ROPE_BASE = 10000.0

        def apply_axial_rope(x, pos):
            b, n, h, d = x.shape
            p = pos.shape[-1]
            dpa = d // p
            half = dpa // 2
            freqs = ROPE_BASE ** (-jnp.arange(half, dtype=x.dtype) / half)
            ang = pos[..., :, None] * freqs
            cos = jnp.cos(ang)[:, :, None, :, :]
            sin = jnp.sin(ang)[:, :, None, :, :]
            xr = x.reshape(b, n, h, p, half, 2)
            x1, x2 = (xr[..., 0], xr[..., 1])
            out = jnp.stack([x1 * cos - x2 * sin, x1 * sin + x2 * cos], axis=-1)
            return out.reshape(b, n, h, d)
        b, n, _ = x.shape
        ctx_n = ctx.shape[1]
        q = (x @ Wq).reshape(b, n, N_HEADS, HEAD_DIM)
        k, v = jnp.split(ctx @ Wkv, 2, axis=-1)
        k = k.reshape(b, ctx_n, N_HEADS, HEAD_DIM)
        v = v.reshape(b, ctx_n, N_HEADS, HEAD_DIM)
        q = apply_axial_rope(q, pos_map)
        k = apply_axial_rope(k, ctx_pos_map)
        scale = 1.0 / np.sqrt(HEAD_DIM).astype(np.float32)
        logits = jnp.einsum('bqhd,bkhd->bhqk', q, k) * scale
        w = jax.nn.softmax(logits, axis=-1)
        attn = jnp.einsum('bhqk,bkhd->bqhd', w, v)
        attn = attn.reshape(b, n, N_HEADS * HEAD_DIM)
        return attn @ Wout + bout

    def _L0_ffn_ref(hidden_states, router_weight, gate_up_proj, down_proj, sh_gate_w, sh_up_w, sh_down_w, shared_gate_w):
        import jax, jax.numpy as jnp
        import numpy as np
        E = 8
        TOP_K = 2
        H = 256
        I_MOE = 176
        I_SH = 704
        B, S = (2, 256)

        def _moe_forward(hidden_states, router_weight, gate_up_proj, down_proj, sh_gate_w, sh_up_w, sh_down_w, shared_gate_w):
            b, s, h = hidden_states.shape
            x = hidden_states.reshape(-1, h)
            shared = jnp.einsum('ti,hi->th', jax.nn.silu(x @ sh_gate_w.T) * (x @ sh_up_w.T), sh_down_w)
            logits = x @ router_weight.T
            probs = jax.nn.softmax(logits.astype(jnp.float32), axis=-1)
            top_v, top_i = jax.lax.top_k(probs, TOP_K)
            top_v = top_v / top_v.sum(axis=-1, keepdims=True)
            combine = (jax.nn.one_hot(top_i, E, dtype=top_v.dtype) * top_v[..., None]).sum(axis=1)
            out = jnp.zeros_like(x)
            for e in range(E):
                gu = x @ gate_up_proj[e].T
                gate, up = (gu[:, :I_MOE], gu[:, I_MOE:])
                cur = jax.nn.silu(gate) * up @ down_proj[e].T
                out = out + cur * combine[:, e:e + 1]
            out = out + jax.nn.sigmoid(x @ shared_gate_w.T) * shared
            return out.reshape(b, s, h)
        return _moe_forward(hidden_states, router_weight, gate_up_proj, down_proj, sh_gate_w, sh_up_w, sh_down_w, shared_gate_w)

    def _L1_xattn_ref(text_hidden, vision_tokens, vision_mask, Wq, Wk, Wv, Wo):
        import jax, jax.numpy as jnp
        import numpy as np
        N_HEADS = 16
        N_KV_HEADS = 8
        HEAD_DIM = 128
        D_TEXT = 256
        D_VISION = 128
        GROUPS = N_HEADS // N_KV_HEADS
        B, T_text, _ = text_hidden.shape
        T_vis = vision_tokens.shape[1]
        scale = jnp.float32(np.sqrt(HEAD_DIM))
        q = (text_hidden @ Wq).reshape(B, T_text, N_HEADS, HEAD_DIM).transpose(0, 2, 1, 3)
        k = (vision_tokens @ Wk).reshape(B, T_vis, N_KV_HEADS, HEAD_DIM).transpose(0, 2, 1, 3)
        v = (vision_tokens @ Wv).reshape(B, T_vis, N_KV_HEADS, HEAD_DIM).transpose(0, 2, 1, 3)
        k = jnp.repeat(k, GROUPS, axis=1)
        v = jnp.repeat(v, GROUPS, axis=1)
        scores = jnp.einsum('bhtd,bhsd->bhts', q, k) / scale
        mask = vision_mask[:, None, None, :]
        scores = jnp.where(mask, scores, -jnp.inf)
        attn = jax.nn.softmax(scores, axis=-1)
        attn = jnp.nan_to_num(attn, nan=0.0)
        out = jnp.einsum('bhts,bhsd->bhtd', attn, v)
        out = out.transpose(0, 2, 1, 3).reshape(B, T_text, N_HEADS * HEAD_DIM)
        return out @ Wo

    def _L1_ffn_ref(x, Wg1, Wg2, Wup, bup, Wdown, bdown):
        import jax, jax.numpy as jnp
        import numpy as np
        D = 256
        H_TOTAL = 1024
        E = 8
        K = 2
        HE = H_TOTAL // E
        B, S = (2, 256)
        Bd, Sd, Dd = x.shape
        T = Bd * Sd
        xt = x.reshape(T, Dd)
        logits = jnp.tanh(xt @ Wg1.T) @ Wg2.T
        _, top_idx = jax.lax.top_k(logits, K)
        top_logits = jnp.take_along_axis(logits, top_idx, axis=1)
        top_scores = jax.nn.softmax(top_logits.astype(jnp.float32), axis=1).astype(logits.dtype)
        rows = jnp.arange(T)[:, None]
        scores = jnp.zeros_like(logits).at[rows, top_idx].set(top_scores)
        up = jnp.einsum('td,ehd->teh', xt, Wup) + bup
        h = jax.nn.silu(up)
        down = jnp.einsum('teh,eoh->teo', h, Wdown) + bdown
        out = jnp.einsum('te,teo->to', scores, down)
        return out.reshape(Bd, Sd, Dd)
    x = x + jnp.tanh(g_xattn[0]) * _L0_xattn_ref(_layernorm(x, axis=-1), ctx_1024, fside_BxSx2_0, fside_BxSx2_0, L0_xattn_Wq, L0_xattn_Wkv, L0_xattn_Wout, L0_xattn_bout)
    x = x + jnp.tanh(g_ffn[0]) * _L0_ffn_ref(_layernorm(x, axis=-1), L0_ffn_router_weight, L0_ffn_gate_up_proj, L0_ffn_down_proj, L0_ffn_sh_gate_w, L0_ffn_sh_up_w, L0_ffn_sh_down_w, L0_ffn_shared_gate_w)
    x = x + jnp.tanh(g_xattn[1]) * _L1_xattn_ref(_layernorm(x, axis=-1), ctx_1024, mask_BxS2_bf1, L1_xattn_Wq, L1_xattn_Wk, L1_xattn_Wv, L1_xattn_Wo)
    x = x + jnp.tanh(g_ffn[1]) * _L1_ffn_ref(_layernorm(x, axis=-1), L1_ffn_Wg1, L1_ffn_Wg2, L1_ffn_Wup, L1_ffn_bup, L1_ffn_Wdown, L1_ffn_bdown)
    return x

_drawn_inputs = setup_inputs


def setup_inputs(seed=0):
    import zlib

    import numpy as np

    out = dict(_drawn_inputs(seed))
    spreads = {'g_ffn': (-1.0, 0.6), 'L0_xattn_bout': (0.0, 0.1)}
    factors = {'L0_ffn_router_weight': 6.306,
     'L0_ffn_gate_up_proj': 5.19,
     'L0_ffn_down_proj': 5.194,
     'L0_ffn_sh_gate_w': 4.173,
     'L0_ffn_sh_up_w': 4.071,
     'L0_ffn_sh_down_w': 4.237,
     'L0_ffn_shared_gate_w': 8.0,
     'L1_xattn_Wq': 8.0,
     'L1_xattn_Wk': 8.0,
     'L1_ffn_bup': 8.0,
     'L1_ffn_bdown': 3.578}
    for name, (base, spread) in spreads.items():
        noise = np.random.default_rng([zlib.crc32(name.encode()), seed]).standard_normal(out[name].shape)
        drawn = base * np.exp(spread * noise) if base else spread * noise
        out[name] = jnp.asarray(drawn.astype(out[name].dtype))
    for name, factor in factors.items():
        out[name] = (out[name] * factor).astype(out[name].dtype)
    return out
```

```python
import concourse.bass as bass
from concourse import mybir
from contextlib import ExitStack
import numpy as np

F32 = mybir.dt.float32
FR = mybir.dt.float32r
I32 = mybir.dt.int32
U32 = mybir.dt.uint32
U8 = mybir.dt.uint8
ALU = mybir.AluOpType
ACT = mybir.ActivationFunctionType
AX_X = mybir.AxisListType.X
P = 128
ds = bass.ds

B, S, D = 64, 64, 256
CD = 128
T = B * S
NT = T // P
KT = D // P
H0, HD0 = 32, 8
HG = 4
H1, G1 = 16, 8
E = 8
I_MOE, I_SH = 176, 704
HID0 = E * I_MOE + I_SH
NC0 = -(-HID0 // P)
HID1 = 1024
NC1 = HID1 // P
LN_EPS = 1e-5
ROPE_BASE = 10000.0
MASKED = -(2.0 ** 100)
LOW = 32
KC = LOW + E + 1

ONE = 1
NA = 16
NF = 8
FT = NT // NF


class Steps:

    def __init__(self, eng, sem):
        self.eng, self.sem, self.base, self.n, self.per, self.i = eng, sem, 0, 0, None, 0

    def loop(self, i, per):
        self.base, self.n, self.per, self.i = self.base + self.n, 0, per, i

    def end(self, rounds):
        assert self.n == self.per, f"steps a round: {self.n}"
        self.base, self.n, self.per, self.i = self.base + rounds * self.per, 0, None, 0

    def done(self, ins):
        ins.then_inc(self.sem, 1)
        self.n += 1
        return self.value()

    def value(self):
        if self.per is None:
            return self.base + self.n
        return self.i * self.per + (self.base + self.n)

    def wait(self, value=None):
        self.eng.wait_ge(self.sem, self.value() if value is None else value)


def build(nc, a, out):
    with ExitStack() as ctx:
        def sem(name):
            return ctx.enter_context(nc.semaphore(name))

        FIRST = -(-nc.sbuf_base // 32) * 32
        WORDS = (nc.sbuf_top - FIRST) // 4

        class Region:

            def __init__(self, at):
                self.at = self.last = at

            def take(self, name, *shape, dtype=F32, over=False):
                n = int(np.prod(shape))
                at = self.last if over else self.at
                t = nc.alloc_sbuf_tensor_at(name, [P, n], dtype, offset=FIRST + 4 * at)
                self.last, self.at = at, max(self.at, at + -(-n // 8) * 8)
                assert self.at <= WORDS, (name, self.at, WORDS)
                v = t[:, :]
                if len(shape) == 1:
                    return v
                names = "abcdef"[:len(shape)]
                return v.rearrange(f"p ({' '.join(names)}) -> p {' '.join(names)}",
                                   **{k: m for k, m in zip(names, shape)})

            def split(self, name, *shape):
                raw = self.take(name + "_raw", *shape)
                lo = self.take(name + "_lo", *shape, dtype=FR, over=True)
                return self.take(name + "_hi", *shape, dtype=FR), lo, raw

            def halves(self, name, *shape):
                return self.take(name + "_hi", *shape, dtype=FR), self.take(name + "_lo", *shape, dtype=FR)

        keep = Region(0)
        x = keep.take("x", NT, D)
        ident = keep.take("ident", P)
        headmask = keep.take("headmask", E)
        ownbatch = keep.take("ownbatch", P)
        gates = keep.take("gates", 4)
        tiny = keep.take("freqs", 4)
        iota8 = keep.take("iota8", E)
        bn = keep.take("bn", NT, 6)
        mv = keep.take("mean_var", NT, 2)
        sd = keep.take("sd", NT)
        rstd = keep.take("rstd", NT)
        nmr = keep.take("nmr", NT)
        gbout = keep.take("gbout", D)
        validb = keep.take("validb", B)
        bup = keep.take("bup", NC1)
        maskraw = keep.take("maskraw", S // 4)
        wide = keep.at
        w0 = Region(wide)
        W0N = (2 * KT * NC0 + 2 * NC0) * P
        w0_hi, w0_lo, w0_raw = w0.split("w0", W0N)
        local = w0.at

        def ffn0_view(w):
            n = KT * NC0 * P
            gate = w[:, 0:n].rearrange("p (k m) -> p k m", k=KT)
            up = w[:, n:2 * n].rearrange("p (k m) -> p k m", k=KT)
            down = w[:, 2 * n:].rearrange("p (c n) -> p c n", n=D)
            return gate, up, down

        w1 = Region(wide)
        m_hi, m_lo = w1.halves("m", H1, KT, P)
        n_hi, n_lo = w1.halves("n", H1, D)
        w1_hi, w1_lo, w1_raw = w1.split("w1", KT * HID1 + NC1 * D)
        valid = w1.take("valid", P)
        ctxT_b = w1.take("ctxT_b", 4, S)
        mrow_raw = w1.take("mrow_raw", 4 * S)
        mrow = w1.take("mrow", 4 * S, dtype=FR)
        ones_raw = w1.take("ones_raw", P)
        ones = w1.take("ones", P, dtype=FR)
        maskrow = w1.take("maskrow", S)
        assert w1.at <= w0.at

        def ffn1_view(w):
            return w[:, 0:KT * HID1].rearrange("p (k m) -> p k m", k=KT), \
                w[:, KT * HID1:].rearrange("p (c n) -> p c n", n=D)

        r = Region(local)
        cosT = r.take("cosT", NT, S)
        sinT = r.take("sinT", NT, S)
        wq0 = r.take("wq0", KT, D)
        wk0 = r.take("wk0", D)
        wv0 = r.take("wv0", 2, P)
        wo0 = r.take("wo0", HG, D)
        xn_a = r.take("xn_a", 2, D)
        xnT_a = r.take("xnT_a", KT, 2, P)
        ctxT_a = r.take("ctxT_a", 2, P)
        ks_a, kw_a, qs_a, qw_a = (r.take(n, HG, 2, S) for n in ("ks_a", "kw_a", "qs_a", "qw_a"))
        q_bd = r.take("q_bd", HG, 2, 2, S)
        k_rot = r.take("k_rot", HG, 2, S)
        v_bd = r.take("v_bd", 2, 16, 2, 2, HD0)
        NK = 3
        k_hd = [r.take(f"k_hd{n}", E, S) for n in range(NK)]
        NP = 4
        probs_a = [r.take(f"probs_a{n}", E, S) for n in range(NP)]
        pT_a = [r.take(f"pT_a{n}", 4, P) for n in range(2)]
        oT_a = r.take("oT_a", 2, HG, P)
        rm_a = r.take("rm_a", 2, E)
        rs_a = r.take("rs_a", 4, E)
        pos = qs_a.rearrange("p a b c -> p (a b c)")[:, 0:256]
        ang = ks_a.rearrange("p a b c -> p (a b c)")
        turn = kw_a.rearrange("p a b c -> p (a b c)")
        trig = qw_a.rearrange("p a b c -> p (a b c)")

        def ffn_region(n, chunks):
            r = Region(local)
            f = {}
            f["sel"] = r.take(f"sel{n}", chunks, P, dtype=FR)
            f["xn"] = r.take(f"xn{n}", FT, D)
            f["xh"], f["xl"] = r.halves(f"xT{n}", KT, FT * P)
            f["s"] = [r.take(f"s{n}{m}", FT * P) for m in range(2)]
            f["act"] = [r.take(f"act{n}{m}", FT * P) for m in range(3)]
            f["hh"] = [r.take(f"hh{n}{m}", FT * P, dtype=FR) for m in range(3)]
            f["hl"] = [r.take(f"hl{n}{m}", FT * P, dtype=FR) for m in range(3)]
            f["cT"] = r.take(f"cT{n}", FT * P, dtype=FR)
            for k, shape in (("lT", (FT * P,)), ("lg", (FT, E + 1)), ("m8", (FT, E)), ("ix", (FT, E)), ("ixf", (FT, 2)),
                             ("dl", (FT, 2)), ("ed", (FT, 2)), ("wt", (FT, 2)), ("comb", (FT, E + 1)), ("c2", (FT, E)),
                             ("wg2", (E,))):
                f[k] = r.take(f"{k}{n}", *shape)
            f["rw_hi"], f["rw_lo"], f["rw_raw"] = r.split(f"rw{n}", KT, E + 2)
            f["bd_hi"], f["bd_lo"], f["bd_raw"] = r.split(f"bd{n}", D)
            return f, r

        f0, r0 = ffn_region(0, NC0)
        f1, _ = ffn_region(1, NC1)

        r = r0
        q1_raw = r.take("q1_raw", H1, D)
        k1_raw = r.take("k1_raw", G1, CD)
        r = Region(local)
        o1_raw = r.take("o1_raw", H1, D)
        v1_raw = r.take("v1_raw", G1, CD)
        r = Region(local)
        xn_b = r.take("xn_b", 2, D)
        xh_b, xl_b = r.halves("xT_b", KT, 2 * P)
        qT = r.take("qT", 4, H1, S)
        cx_hi, cx_lo, cx_raw = r.split("cx", 4, CD)
        probs_b = [r.take(f"probs_b{n}", G1, S) for n in range(2)]
        pTh, pTl = zip(*(r.halves(f"pT_b{n}", 4 * P) for n in range(2)))
        oTh, oTl = r.halves("oT_b", 4, 2, 2, 2 * P)
        rm_b = w1.take("rm_b", 2, G1)
        rs_b = w1.take("rs_b", 2, G1)
        assert w1.at <= w0.at

        bank = [ctx.enter_context(nc.psum_tensor(f"bank{n}", [P, 512], F32)) for n in range(8)]

        tab = {k: nc.dram_tensor(f"{k}_table", (16, NT * S), F32).ap() for k in ("cos", "sin")}

        biases = nc.dram_tensor("mask_biases", (1, B * S), F32).ap()

        names = """x_loaded const_loaded w0x_loaded w0f_loaded pos_loaded tables_stored tables_loaded
        gates_ready sd_wanted sd_ready stats_ready zeros_ready bout_ready trig_wanted trig_ready
        a_xn_ready a_xnT_psum a_xnT_ready a_ctx_loaded a_q_psum a_k_psum a_v_psum a_ks_ready a_qs_ready
        a_v_ready a_k_ready a_q_ready a_khd_ready a_scores a_centred a_exp a_recip a_probs a_pT_psum a_pT_ready
        a_o_psum a_oT_ready a_y_psum a_resid a_loop_done
        sel0_loaded sel1_loaded sel0_cast sel1_cast w1_loaded o1_loaded m_psum m_copied n_psum n_copied w1_split rw_split
        mask_loaded mask_ready biases_stored valid_psum valid_ready ones_ready
        b_xn_ready b_xnT_psum b_xh_ready b_xl_ready b_ctx_loaded b_q_psum b_q_ready b_cxh b_cxl b_scores b_centred
        b_exp b_recip b_probs b_pT_psum b_pTh b_pTl b_o_psum b_oTh b_oTl b_y_psum b_resid b_mrow
        vector_steps scalar_steps out_stored vector_passed tensor_passed""".split()
        s = {n: sem(n) for n in names}
        for ph in ("f0", "f1"):
            for n in """xn_ready xnT_psum xh_ready xl_ready logit_psum logit_copied logitT_psum delta_ready exp_ready
                    comb_ready combT_psum cTh_ready cTl_ready gu_psum silu act_ready scaled cb_psum hh_ready hl_ready
                    down_done resid loop_done""".split():
                s[f"{ph}_{n}"] = sem(f"{ph}_{n}")

        started = dict(
            tensor="""a_xnT_psum a_q_psum a_k_psum a_v_psum a_scores a_pT_psum a_o_psum a_y_psum
                b_xnT_psum b_q_psum b_scores b_pT_psum b_o_psum b_y_psum
                f_xnT_psum f_logit_psum f_logitT_psum f_combT_psum f_gu_psum f_cb_psum f_down_done""",
            scalar="""a_xnT_ready a_ks_ready a_qs_ready a_v_ready a_exp a_pT_ready
                b_xh_ready b_cxh b_q_ready b_exp b_pTh b_oTh
                f_xh_ready f_logit_copied f_exp_ready f_silu f_cTh_ready f_hh_ready""",
            gpsimd="a_khd_ready a_probs b_probs",
            vector="""a_xn_ready a_k_ready a_q_ready a_centred a_recip a_oT_ready a_resid
                b_xn_ready b_xl_ready b_cxl b_mrow b_centred b_recip b_pTl b_oTl b_resid
                f_xn_ready f_xl_ready f_delta_ready f_comb_ready f_cTl_ready f_act_ready f_scaled f_hl_ready f_resid""")

        def start(eng, name):
            for n in started[name].split():
                for ph in ("f0", "f1") if n.startswith("f_") else (None,):
                    eng.sem_inc(s[n if ph is None else ph + n[1:]], ONE)

        block = ctx.enter_context(nc.Block())

        @block.sync
        def _(sp):
            sp.sem_inc(s["w0f_loaded"], 16)
            xs = a["x"].rearrange("(t p) d -> p t d", p=P)
            sp.dma_start(pos, a["pos"]).then_inc(s["pos_loaded"], 16)
            for n, (dst, src) in enumerate(((tiny[:, 0:4], "freq"), (gates, "gates"), (ident, "ident"), (headmask, "headmask"),
                                            (ownbatch, "ownbatch"), (iota8, "iota8"), (gbout, "bout"), (bup, "bup"))):
                sp.dma_start(dst, a[src]).then_inc(s["const_loaded"], 16)
            for n in range(4):
                sp.dma_start(x[:, 8 * n:8 * n + 8, :], xs[:, 8 * n:8 * n + 8, :]).then_inc(s["x_loaded"], 16)
            for dst, src in ((wq0.rearrange("p k n -> p (k n)"), "wq0"), (wk0, "wk0"),
                             (wv0.rearrange("p k n -> p (k n)"), "wv0"), (wo0.rearrange("p k n -> p (k n)"), "wo0")):
                sp.dma_start(dst, a[src]).then_inc(s["w0x_loaded"], 16)
            sp.dma_start(maskraw.bitcast(U8)[0:B, :], a["mask"]).then_inc(s["mask_loaded"], 16)
            for n, k in enumerate(("sin", "cos")):
                sp.wait_ge(s["trig_ready"], n + 1)
                sp.dma_start(tab[k].rearrange("r (g c) -> (r g) c", c=256), trig[:, 256 * n:256 * n + 256]).then_inc(
                    s["tables_stored"], 16)
            sp.wait_ge(s["tables_stored"], 32)
            for k, dst in (("cos", cosT), ("sin", sinT)):
                for b in range(2):
                    for h in range(8):
                        sp.dma_start(dst[64 * b + 8 * h:64 * b + 8 * h + 8, :, :].rearrange("p t c -> p (t c)"),
                                     tab[k][8 * b:8 * b + 8, :]).then_inc(s["tables_loaded"], 16)
            with sp.Fori(0, NA) as i:
                sp.wait_ge(s["a_v_psum"], ONE + i)
                sp.dma_start(ctxT_a.rearrange("p a b -> p (a b)"), a["ctxT"][:, ds(i * 256, 256)]).then_inc(s["a_ctx_loaded"], 16)
                sp.wait_ge(s["w0f_loaded"], i * 16 + 16)
                sp.dma_start(w0_raw[:, ds(i * (W0N // NA), W0N // NA)], a["w0"][:, ds(i * (W0N // NA), W0N // NA)]).then_inc(
                    s["w0f_loaded"], 16)
            sp.wait_ge(s["a_loop_done"], 3)
            sp.dma_start(f0["rw_raw"].rearrange("p k m -> p (k m)"), a["rw0"]).then_inc(s["sel0_loaded"], 16)
            for dst, src in ((q1_raw, "wq1"), (k1_raw, "wk1")):
                sp.dma_start(dst.rearrange("p k n -> p (k n)"), a[src]).then_inc(s["w1_loaded"], 16)
            sp.wait_ge(s["f0_loop_done"], 2)
            sp.dma_start(o1_raw.rearrange("p k n -> p (k n)"), a["wo1"]).then_inc(s["o1_loaded"], 16)
            sp.dma_start(v1_raw.rearrange("p k n -> p (k n)"), a["wv1"]).then_inc(s["o1_loaded"], 16)
            sp.dma_start(w1_raw, a["w1"]).then_inc(s["o1_loaded"], 16)
            sp.wait_ge(s["n_psum"], H1 // 2)
            sp.wait_ge(s["mask_ready"], 1)
            sp.dma_start(biases.rearrange("a (b k) -> (a b) k", b=B), maskrow[0:B, :]).then_inc(s["biases_stored"], 16)
            sp.wait_ge(s["biases_stored"], 16)
            with sp.Fori(0, NA) as i:
                sp.wait_ge(s["b_o_psum"], ONE + i * 8)
                sp.dma_start(ctxT_b.rearrange("p a b -> p (a b)"), a["ctxT"][:, ds(i * 256, 256)]).then_inc(s["b_ctx_loaded"], 16)
                sp.dma_start(mrow_raw[0:1, :], biases[:, ds(i * 256, 256)]).then_inc(s["b_ctx_loaded"], 16)
                for half in range(2):
                    sp.dma_start(cx_raw[64 * half:64 * half + 64, :, :],
                                 a["ctx"][ds(i * 4, 4), :, :].rearrange("b k c -> k b c")).then_inc(s["b_ctx_loaded"], 16)
            sp.wait_ge(s["b_resid"], ONE + NA * 2)
            sp.dma_start(f1["rw_raw"].rearrange("p k m -> p (k m)"), a["rw1"]).then_inc(s["sel1_loaded"], 16)
            sp.dma_start(f1["wg2"][0:E, :], a["wg2"]).then_inc(s["sel1_loaded"], 16)
            sp.dma_start(f1["bd_raw"][0:KC, :], a["bdown"]).then_inc(s["sel1_loaded"], 16)
            os_ = out.rearrange("(t p) d -> p t d", p=P)
            with sp.Fori(0, NF) as i:
                sp.wait_ge(s["f1_resid"], ONE + i + 1)
                sp.dma_start(os_[:, ds(i * FT, FT), :], x[:, ds(i * FT, FT), :]).then_inc(s["out_stored"], 16)
            sp.wait_ge(s["out_stored"], 16 * NF)
            for n, v in (("const_loaded", 128), ("tables_loaded", 512), ("w0f_loaded", 16 * NA + 16), ("x_loaded", 64)):
                sp.wait_ge(s[n], v)

        @block.tensor
        def _(pe):
            start(pe, "tensor")

            def split3(dst, lhs, rhs, start, stop):
                (lh, ll), (rh, rl) = lhs, rhs
                pe.matmul(dst, lh, rh, start=start, stop=False, skip_group_check=True)
                pe.matmul(dst, ll, rh, start=False, stop=False, skip_group_check=True)
                return pe.matmul(dst, lh, rl, start=False, stop=stop, skip_group_check=True)

            pe.wait_ge(s["const_loaded"], 128)
            pe.wait_ge(s["w0x_loaded"], 64)
            pe.wait_ge(s["zeros_ready"], 2)
            NS = 8
            with pe.Fori(0, NA) as i:
                pe.wait_ge(s["a_xn_ready"], ONE + i + 1)
                pe.wait_ge(s["a_v_ready"], ONE + i * 4)
                trb = bank[6][:, :].rearrange("p (k t c) -> p k t c", k=KT, t=2)
                for t in range(2):
                    for k in range(KT):
                        m = pe.transpose(trb[:, k, t, :], xn_a[:, t, k * P:(k + 1) * P], ident)
                m.then_inc(s["a_xnT_psum"], 1)
                pe.wait_ge(s["a_ctx_loaded"], i * 16 + 16)
                pe.wait_ge(s["a_resid"], ONE + i * 2)
                kb = bank[5][:, :].rearrange("p (g t k) -> p g t k", g=HG, t=2)
                for b in range(2):
                    for g in range(HG):
                        m = pe.matmul(kb[64 * b:64 * b + 64, g], wk0[:, 64 * g:64 * g + 64], ctxT_a[:, :, 64 * b:64 * b + 64],
                                      start=True, stop=True)
                m.then_inc(s["a_k_psum"], 1)
                pe.wait_ge(s["a_xnT_ready"], ONE + i + 1)
                qb = bank[7][:, :].rearrange("p (g t k) -> p g t k", g=HG, t=2)
                for b in range(2):
                    for g in range(HG):
                        for k in range(KT):
                            m = pe.matmul(qb[64 * b:64 * b + 64, g], wq0[:, k, 64 * g:64 * g + 64],
                                          xnT_a[:, k, :, 64 * b:64 * b + 64], start=(k == 0), stop=(k == KT - 1))
                m.then_inc(s["a_q_psum"], 1)
                vb = bank[6][:, :].rearrange("p (b n) -> p b n", b=4)
                for par in range(2):
                    for b in range(4):
                        m = pe.matmul(vb[64 * par:64 * par + 64, b], ctxT_a[:, b // 2, 64 * (b % 2):64 * (b % 2) + 64],
                                      wv0[:, par, :], start=True, stop=True)
                m.then_inc(s["a_v_psum"], 1)
                for t in range(NS + 4):
                    if t < NS:
                        pe.wait_ge(s["a_khd_ready"], ONE + i * NS + t + 1)
                        if t == 0:
                            pe.wait_ge(s["a_q_ready"], ONE + i + 1)
                        if t >= 2:
                            pe.wait_ge(s["a_centred"], ONE + i * NS + t - 1)
                        pe.matmul(bank[t % 2][:, :], q_bd[:, t % 4, t // 4].rearrange("p b q -> p (b q)"),
                                  k_hd[t % NK].rearrange("p h k -> p (h k)"), start=True, stop=True).then_inc(s["a_scores"], 1)
                    n = t - 2
                    if 0 <= n < NS:
                        pe.wait_ge(s["a_probs"], ONE + i * NS + n + 1)
                        if n >= 2:
                            pe.wait_ge(s["a_pT_ready"], ONE + i * NS + n - 1)
                        for j in range(4):
                            m = pe.transpose(bank[2 + n % 2][:, j * P:(j + 1) * P],
                                             probs_a[n % NP].rearrange("p h k -> p (h k)")[:, j * P:(j + 1) * P], ident)
                        m.then_inc(s["a_pT_psum"], 1)
                    n = t - 3
                    if 0 <= n < NS:
                        pe.wait_ge(s["a_pT_ready"], ONE + i * NS + n + 1)
                        if n == 0:
                            pe.wait_ge(s["a_v_ready"], ONE + i * 4 + 4)
                        if n >= 1:
                            pe.wait_ge(s["a_oT_ready"], ONE + i * NS + n)
                        for j in range(4):
                            m = pe.matmul(bank[4][32 * j:32 * j + 32, 0:P],
                                          v_bd[:, n // 4, 4 * (n % 4) + j].rearrange("p b r d -> p (b r d)"),
                                          pT_a[n % 2][:, j, :], start=True, stop=True)
                        m.then_inc(s["a_o_psum"], 1)
                    n = t - 4
                    if 0 <= n < NS:
                        pe.wait_ge(s["a_oT_ready"], ONE + i * NS + n + 1)
                        if n == 4:
                            pe.wait_ge(s["a_resid"], ONE + i * 2 + 1)
                        if n == 0:
                            pe.wait_ge(s["a_k_ready"], ONE + i + 1)
                        m = pe.matmul(bank[5][:, 0:D], oT_a[:, n // 4, n % 4, :], wo0[:, n % 4, :],
                                      start=(n % 4 == 0), stop=(n % 4 == 3))
                        if n % 4 == 3:
                            m.then_inc(s["a_y_psum"], 1)
            pe.wait_ge(s["a_resid"], ONE + NA * 2)
            pe.sem_inc(s["a_loop_done"], 1)

            def ffn(ph, f, chunks, hidden, gate, up, down, rows_last):
                gated = gate is not None
                last = {c: (hidden - c * P if (c + 1) * P > hidden else P) for c in range(chunks)}
                NL = E + 1 if gated else E
                with pe.Fori(0, NF) as i:
                    pe.wait_ge(s[f"{ph}_xn_ready"], ONE + i + 1)
                    pe.wait_ge(s[f"{ph}_silu"], ONE + i * chunks)
                    if gated:
                        pe.wait_ge(s[f"{ph}_act_ready"], ONE + i * chunks)
                    for k in range(KT):
                        for t in range(FT):
                            m = pe.transpose(bank[k][:, t * P:(t + 1) * P], f["xn"][:, t, k * P:(k + 1) * P], ident)
                    m.then_inc(s[f"{ph}_xnT_psum"], 1)
                    pe.wait_ge(s[f"{ph}_xh_ready"], ONE + i * KT + KT)
                    pe.wait_ge(s[f"{ph}_xl_ready"], ONE + i * KT + KT)
                    for k in range(KT):
                        m = split3(bank[6][0:NL, :], (f["rw_hi"][:, k, 0:NL], f["rw_lo"][:, k, 0:NL]),
                                   (f["xh"][:, k, :], f["xl"][:, k, :]), k == 0, k == KT - 1)
                    m.then_inc(s[f"{ph}_logit_psum"], 1)

                    def gate_up(c):
                        M = last[c]
                        cols = slice(c * P, c * P + M)
                        if c >= 2:
                            pe.wait_ge(s[f"{ph}_silu"], ONE + i * chunks + c - 1)
                            if gated:
                                pe.wait_ge(s[f"{ph}_act_ready"], ONE + i * chunks + c - 1)
                        for w, b in ((gate, 0), (up, 2)) if gated else ((up, 0),):
                            for k in range(KT):
                                m = split3(bank[b + c % 2][0:M, :], (w[0][:, k, cols], w[1][:, k, cols]),
                                           (f["xh"][:, k, :], f["xl"][:, k, :]), k == 0, k == KT - 1)
                        m.then_inc(s[f"{ph}_gu_psum"], 1)

                    def spread(c):
                        if c == 0:
                            pe.wait_ge(s[f"{ph}_cTh_ready"], ONE + i + 1)
                            pe.wait_ge(s[f"{ph}_cTl_ready"], ONE + i + 1)
                        if c >= 1:
                            pe.wait_ge(s[f"{ph}_scaled"], ONE + i * chunks + c)
                        M = last[c]
                        pe.sem_inc(s["tensor_passed"], 1)
                        pe.matmul(bank[4][0:M, :], f["sel"][0:KC, c, 0:M], f["cT"][0:KC, :],
                                  start=True, stop=True, skip_group_check=True).then_inc(s[f"{ph}_cb_psum"], 1)

                    def down_part(c):
                        M = last[c]
                        pe.wait_ge(s[f"{ph}_hh_ready"], ONE + i * chunks + c + 1)
                        pe.wait_ge(s[f"{ph}_hl_ready"], ONE + i * chunks + c + 1)
                        if c == 0:
                            pe.wait_ge(s[f"{ph}_resid"], ONE + i)
                            if not gated:
                                for t in range(FT):
                                    y = bank[5 + 2 * (t // 2)][:, (t % 2) * D:(t % 2 + 1) * D]
                                    cols = f["cT"][0:KC, t * P:(t + 1) * P]
                                    pe.matmul(y, cols, f["bd_hi"][0:KC, :], start=(t % 2 == 0), stop=False,
                                              skip_group_check=True)
                                    pe.matmul(y, cols, f["bd_lo"][0:KC, :], start=False, stop=False,
                                              skip_group_check=True)
                        for t in range(FT):
                            y = bank[5 + 2 * (t // 2)][:, (t % 2) * D:(t % 2 + 1) * D]
                            m = split3(y, (f["hh"][c % 3][0:M, t * P:(t + 1) * P], f["hl"][c % 3][0:M, t * P:(t + 1) * P]),
                                       (down[0][0:M, c, :], down[1][0:M, c, :]),
                                       gated and c == 0 and t % 2 == 0, c == chunks - 1)
                        m.then_inc(s[f"{ph}_down_done"], 1)

                    gate_up(0)
                    if not gated:
                        pe.wait_ge(s[f"{ph}_logit_copied"], ONE + i + 1)
                        pe.sem_inc(s["tensor_passed"], 1)
                        for t in range(FT):
                            m = pe.matmul(bank[6][:, t * 16:t * 16 + E], f["lT"][0:E, t * P:(t + 1) * P], f["wg2"][0:E, :],
                                          start=True, stop=True)
                    else:
                        pe.wait_ge(s[f"{ph}_logit_copied"], ONE + i + 1)
                        pe.sem_inc(s["tensor_passed"], 1)
                        for t in range(FT):
                            m = pe.transpose(bank[6][:, t * 16:t * 16 + NL], f["lT"][0:NL, t * P:(t + 1) * P], ident[0:NL, 0:NL])
                    m.then_inc(s[f"{ph}_logitT_psum"], 1)
                    gate_up(1)
                    pe.wait_ge(s[f"{ph}_comb_ready"], ONE + i + 1)
                    for t in range(FT):
                        m = pe.transpose(bank[6][0:NL, t * P:(t + 1) * P], f["comb"][:, t, 0:NL], ident)
                    m.then_inc(s[f"{ph}_combT_psum"], 1)
                    for t in range(1, chunks + 3):
                        if 2 <= t < chunks:
                            gate_up(t)
                        if 0 <= t - 1 < chunks:
                            spread(t - 1)
                        if 0 <= t - 3 < chunks:
                            down_part(t - 3)
                pe.wait_ge(s[f"{ph}_resid"], ONE + NF)
                pe.sem_inc(s[f"{ph}_loop_done"], 1)

            pe.wait_ge(s["sel0_cast"], 16)
            pe.wait_ge(s["rw_split"], 1)
            hi, lo = ffn0_view(w0_hi), ffn0_view(w0_lo)
            ffn("f0", f0, NC0, HID0, (hi[0], lo[0]), (hi[1], lo[1]), (hi[2], lo[2]), None)

            pe.wait_ge(s["w1_loaded"], 32)
            for h in range(H1):
                if h >= 2:
                    pe.wait_ge(s["m_copied"], h - 1)
                for k in range(KT):
                    m = pe.matmul(bank[h % 2][:, k * P:(k + 1) * P], q1_raw[:, h, k * P:(k + 1) * P], k1_raw[:, h // 2, :],
                                  start=True, stop=True)
                m.then_inc(s["m_psum"], 1)
            pe.wait_ge(s["o1_loaded"], 48)
            for c in range(H1 // 2):
                if c >= 2:
                    pe.wait_ge(s["n_copied"], c - 1)
                for u in range(2):
                    m = pe.matmul(bank[2 + c % 2][:, u * D:(u + 1) * D], v1_raw[:, c, :], o1_raw[:, 2 * c + u, :],
                                  start=True, stop=True)
                m.then_inc(s["n_psum"], 1)
            pe.wait_ge(s["mask_ready"], 1)
            pe.wait_ge(s["m_copied"], H1)
            pe.matmul(bank[0][:, 0:B], valid[0:B, :], ident[0:B, 0:B], start=True, stop=True).then_inc(s["valid_psum"], 1)
            pe.wait_ge(s["valid_ready"], 1)
            pe.wait_ge(s["n_copied"], H1 // 2)
            pe.wait_ge(s["ones_ready"], 1)
            NB = 4
            with pe.Fori(0, NA) as i:
                pe.wait_ge(s["b_xn_ready"], ONE + i + 1)
                pe.wait_ge(s["b_o_psum"], ONE + i * NB)
                pe.wait_ge(s["b_oTh"], ONE + i * NB * 2)
                pe.wait_ge(s["b_oTl"], ONE + i * NB * 2)
                trb = bank[4][:, :].rearrange("p (k t c) -> p k t c", k=KT, t=2)
                for t in range(2):
                    for k in range(KT):
                        m = pe.transpose(trb[:, k, t, :], xn_b[:, t, k * P:(k + 1) * P], ident)
                m.then_inc(s["b_xnT_psum"], 1)
                pe.wait_ge(s["b_xh_ready"], ONE + i + 1)
                pe.wait_ge(s["b_xl_ready"], ONE + i + 1)
                for c in range(H1 // 2):
                    if c >= 2:
                        pe.wait_ge(s["b_q_ready"], ONE + i * 8 + c - 1)
                    for u in range(2):
                        for k in range(KT):
                            m = split3(bank[6 + c % 2][:, u * 256:(u + 1) * 256], (m_hi[:, 2 * c + u, k, :], m_lo[:, 2 * c + u, k, :]),
                                       (xh_b[:, k, :], xl_b[:, k, :]), u == 0 and k == 0, k == KT - 1)
                    m.then_inc(s["b_q_psum"], 1)
                pe.wait_ge(s["b_q_ready"], ONE + i * 8 + 8)
                pe.wait_ge(s["b_ctx_loaded"], i * 64 + 64)
                pe.wait_ge(s["b_mrow"], ONE + i + 1)

                def scores(b):
                    if b >= 2:
                        pe.wait_ge(s["b_centred"], ONE + i * NB + b - 1)
                    pe.matmul(bank[b % 2][:, :].rearrange("p (g k) -> p g k", g=G1), ones[0:1, :],
                              mrow[0:1, b * S:(b + 1) * S].unsqueeze(1).broadcast_to([1, G1, S]),
                              start=True, stop=False, skip_group_check=True)
                    for g in range(G1):
                        m = pe.matmul(bank[b % 2][:, g * S:(g + 1) * S], qT[:, b, 2 * g:2 * g + 2, :].rearrange("p h q -> p (h q)"),
                                      ctxT_b[:, b, :], start=False, stop=(g == G1 - 1), skip_group_check=True)
                    m.then_inc(s["b_scores"], 1)

                def probsT(b):
                    pe.wait_ge(s["b_probs"], ONE + i * NB + b + 1)
                    if b >= 2:
                        pe.wait_ge(s["b_pTh"], ONE + i * NB + b - 1)
                        pe.wait_ge(s["b_pTl"], ONE + i * NB + b - 1)
                    for j in range(4):
                        m = pe.transpose(bank[2 + b % 2][:, j * P:(j + 1) * P],
                                         probs_b[b % 2].rearrange("p g k -> p (g k)")[:, j * P:(j + 1) * P], ident)
                    m.then_inc(s["b_pT_psum"], 1)

                def outputs(b):
                    pe.wait_ge(s["b_pTh"], ONE + i * NB + b + 1)
                    pe.wait_ge(s["b_pTl"], ONE + i * NB + b + 1)
                    if b == 0:
                        pe.wait_ge(s["b_cxh"], ONE + i + 1)
                        pe.wait_ge(s["b_cxl"], ONE + i + 1)
                        pe.wait_ge(s["b_q_ready"], ONE + i * 8 + 8)
                        pe.wait_ge(s["b_y_psum"], ONE + i * 2)
                    for par in range(2):
                        if b >= 1:
                            pe.wait_ge(s["b_oTh"], ONE + i * NB * 2 + 2 * b - 1 + par)
                            pe.wait_ge(s["b_oTl"], ONE + i * NB * 2 + 2 * b - 1 + par)
                        rows = slice(64 * par, 64 * par + 64)
                        split3(bank[4 + par][:, :], (cx_hi[rows, b, :], cx_lo[rows, b, :]), (pTh[b % 2][rows, :], pTl[b % 2][rows, :]),
                               True, True).then_inc(s["b_o_psum"], 1)

                def project(t):
                    pe.wait_ge(s["b_oTh"], ONE + i * NB * 2 + 4 * t + 4)
                    pe.wait_ge(s["b_oTl"], ONE + i * NB * 2 + 4 * t + 4)
                    pe.wait_ge(s["b_resid"], ONE + i * 2 + t)
                    for h in range(H1):
                        j, par, u = h // 4, (h // 2) % 2, h % 2
                        m = split3(bank[6][:, 0:D], (oTh[:, j, par, u, t * P:(t + 1) * P], oTl[:, j, par, u, t * P:(t + 1) * P]),
                                   (n_hi[:, h, :], n_lo[:, h, :]), h == 0, h == H1 - 1)
                    m.then_inc(s["b_y_psum"], 1)

                scores(0)
                scores(1)
                probsT(0)
                scores(2)
                probsT(1)
                outputs(0)
                scores(3)
                outputs(1)
                probsT(2)
                project(0)
                probsT(3)
                outputs(2)
                outputs(3)
                project(1)
                pe.wait_ge(s["b_resid"], ONE + i * 2 + 2)
            pe.wait_ge(s["sel1_cast"], 16)
            pe.wait_ge(s["sel1_loaded"], 48)
            pe.wait_ge(s["rw_split"], 2)
            pe.wait_ge(s["w1_split"], 1)
            hi, lo = ffn1_view(w1_hi), ffn1_view(w1_lo)
            ffn("f1", f1, NC1, HID1, None, (hi[0], lo[0]), (hi[1], lo[1]), None)

        @block.scalar
        def _(act):
            start(act, "scalar")
            act.wait_ge(s["const_loaded"], 128)
            act.activation(gates, gates, ACT.Tanh).then_inc(s["gates_ready"], 1)
            for n in range(2):
                act.wait_ge(s["trig_wanted"], n + 1)
                act.activation(trig[:, 256 * n:256 * n + 256], ang[:, 256 * n:256 * n + 256], ACT.Sin).then_inc(s["trig_ready"], 1)

            def root(n):
                act.wait_ge(s["sd_wanted"], n + 1)
                act.activation(sd, sd, ACT.Sqrt).then_inc(s["sd_ready"], 1)

            root(0)
            NS = 8
            SCALE0 = float(HD0) ** -0.5
            act.wait_ge(s["tables_stored"], 32)
            act.wait_ge(s["zeros_ready"], 2)
            with act.Fori(0, NA) as i:
                act.wait_ge(s["a_k_psum"], ONE + i + 1)
                act.wait_ge(s["a_k_ready"], ONE + i)
                act.activation(ks_a.rearrange("p g t k -> p (g t k)"), bank[5][:, :], ACT.Copy).then_inc(s["a_ks_ready"], 1)
                act.wait_ge(s["a_xnT_psum"], ONE + i + 1)
                act.wait_ge(s["a_q_psum"], ONE + i)
                act.activation(xnT_a.rearrange("p k t c -> p (k t c)"), bank[6][:, :], ACT.Copy).then_inc(s["a_xnT_ready"], 1)
                act.wait_ge(s["a_q_psum"], ONE + i + 1)
                act.wait_ge(s["a_q_ready"], ONE + i)
                act.activation(qs_a.rearrange("p g t k -> p (g t k)"), bank[7][:, :], ACT.Copy).then_inc(s["a_qs_ready"], 1)
                act.wait_ge(s["a_v_psum"], ONE + i + 1)
                act.wait_ge(s["a_o_psum"], ONE + i * NS)
                vb = bank[6][:, :].rearrange("p (t b j d) -> p t b j d", t=2, b=2, j=16)
                for par in range(2):
                    for t in range(2):
                        rows = slice(64 * par, 64 * par + 64)
                        act.activation(v_bd[rows, t, :, :, par, :].rearrange("p j b d -> p b j d"), vb[rows, t],
                                       ACT.Copy).then_inc(s["a_v_ready"], 1)
                for t in range(NS + 3):
                    if t < NS:
                        act.wait_ge(s["a_centred"], ONE + i * NS + t + 1)
                        act.activation(probs_a[t % NP], probs_a[t % NP], ACT.Exp, scale=SCALE0).then_inc(s["a_exp"], 1)
                    n = t - 2
                    if 0 <= n < NS:
                        act.wait_ge(s["a_pT_psum"], ONE + i * NS + n + 1)
                        if n >= 2:
                            act.wait_ge(s["a_o_psum"], ONE + i * NS + n - 1)
                        act.activation(pT_a[n % 2].rearrange("p j c -> p (j c)"), bank[2 + n % 2][:, :], ACT.Copy).then_inc(
                            s["a_pT_ready"], 1)

            def ffn(ph, f, chunks, hidden, gated):
                last = {c: (hidden - c * P if (c + 1) * P > hidden else P) for c in range(chunks)}
                NL = E + 1 if gated else E
                with act.Fori(0, NF) as i:
                    act.wait_ge(s[f"{ph}_xnT_psum"], ONE + i + 1)
                    act.wait_ge(s[f"{ph}_gu_psum"], ONE + i * chunks)
                    for k in range(KT):
                        act.activation(f["xh"][:, k, :], bank[k][:, :], ACT.Copy).then_inc(s[f"{ph}_xh_ready"], 1)
                    act.wait_ge(s[f"{ph}_logit_psum"], ONE + i + 1)
                    act.activation(f["lT"][0:NL, :], bank[6][0:NL, :], ACT.Copy if gated else ACT.Tanh).then_inc(
                        s[f"{ph}_logit_copied"], 1)

                    def silu(c):
                        M = last[c]
                        act.wait_ge(s[f"{ph}_gu_psum"], ONE + i * chunks + c + 1)
                        if c >= 2:
                            act.wait_ge(s[f"{ph}_act_ready" if gated else f"{ph}_scaled"], ONE + i * chunks + c - 1)
                        act.activation(f["s"][c % 2][0:M, :], bank[c % 2][0:M, :], ACT.Silu,
                                       **({} if gated else {"bias": bup[:, c:c + 1]})).then_inc(s[f"{ph}_silu"], 1)

                    def high(c):
                        M = last[c]
                        act.wait_ge(s[f"{ph}_scaled"], ONE + i * chunks + c + 1)
                        if c >= 3:
                            act.wait_ge(s[f"{ph}_down_done"], ONE + i * chunks + c - 2)
                        else:
                            act.wait_ge(s[f"{ph}_down_done"], ONE + i * chunks)
                        act.activation(f["hh"][c % 3][0:M, :], f["act"][c % 3][0:M, :], ACT.Copy).then_inc(
                            s[f"{ph}_hh_ready"], 1)

                    act.wait_ge(s[f"{ph}_delta_ready"], ONE + i + 1)
                    act.activation(f["ed"], f["dl"], ACT.Exp).then_inc(s[f"{ph}_exp_ready"], 1)
                    silu(0)
                    silu(1)
                    act.wait_ge(s[f"{ph}_combT_psum"], ONE + i + 1)
                    act.activation(f["cT"][0:NL, :], bank[6][0:NL, :], ACT.Copy).then_inc(s[f"{ph}_cTh_ready"], 1)
                    for t in range(1, chunks + 1):
                        if 2 <= t < chunks:
                            silu(t)
                        high(t - 1)

            root(1)
            ffn("f0", f0, NC0, HID0, True)
            root(2)
            for h in range(H1):
                act.wait_ge(s["m_psum"], h + 1)
                act.activation(m_hi[:, h].rearrange("p k c -> p (k c)"), bank[h % 2][:, 0:256], ACT.Copy).then_inc(
                    s["scalar_steps"], 1)
            for c in range(H1 // 2):
                act.wait_ge(s["n_psum"], c + 1)
                act.activation(n_hi[:, 2 * c:2 * c + 2, :].rearrange("p u n -> p (u n)"), bank[2 + c % 2][:, :],
                               ACT.Copy).then_inc(s["scalar_steps"], 1)
            NB = 4
            SCALE1 = float(CD) ** -0.5
            with act.Fori(0, NA) as i:
                act.wait_ge(s["b_xnT_psum"], ONE + i + 1)
                act.activation(xh_b.rearrange("p k t -> p (k t)"), bank[4][:, :], ACT.Copy).then_inc(s["b_xh_ready"], 1)
                act.wait_ge(s["b_ctx_loaded"], i * 64 + 64)
                act.wait_ge(s["b_o_psum"], ONE + i * 8)
                act.activation(cx_hi, cx_raw, ACT.Copy).then_inc(s["b_cxh"], 1)
                for c in range(H1 // 2):
                    act.wait_ge(s["b_q_psum"], ONE + i * 8 + c + 1)
                    act.activation(qT[:, :, 2 * c:2 * c + 2, :].rearrange("p b h q -> p h b q"),
                                   bank[6 + c % 2][:, :].rearrange("p (h b q) -> p h b q", h=2, b=4), ACT.Copy).then_inc(
                        s["b_q_ready"], 1)

                def expo(b):
                    act.wait_ge(s["b_centred"], ONE + i * NB + b + 1)
                    act.activation(probs_b[b % 2], probs_b[b % 2], ACT.Exp, scale=SCALE1).then_inc(s["b_exp"], 1)

                def pth(b):
                    act.wait_ge(s["b_pT_psum"], ONE + i * NB + b + 1)
                    if b >= 2:
                        act.wait_ge(s["b_o_psum"], ONE + i * NB * 2 + 2 * b - 2)
                    act.activation(pTh[b % 2], bank[2 + b % 2][:, :], ACT.Copy).then_inc(s["b_pTh"], 1)

                def oth(b):
                    for par in range(2):
                        act.wait_ge(s["b_o_psum"], ONE + i * NB * 2 + 2 * b + par + 1)
                        if b == 0:
                            act.wait_ge(s["b_y_psum"], ONE + i * 2)
                        act.activation(oTh[:, :, par, :, b * S:(b + 1) * S],
                                       bank[4 + par][:, :].rearrange("p (j u q) -> p j u q", j=4, u=2), ACT.Copy).then_inc(
                            s["b_oTh"], 1)

                expo(0)
                expo(1)
                pth(0)
                expo(2)
                pth(1)
                oth(0)
                expo(3)
                oth(1)
                pth(2)
                pth(3)
                oth(2)
                oth(3)
            root(3)
            ffn("f1", f1, NC1, HID1, False)

        @block.gpsimd
        def _(pool):
            start(pool, "gpsimd")
            pool.memset(v_bd, 0.0).then_inc(s["zeros_ready"], 1)
            pool.wait_ge(s["const_loaded"], 128)
            NS = 8
            with pool.Fori(0, NA) as i:
                def heads(n):
                    if n == 0:
                        pool.wait_ge(s["a_k_ready"], ONE + i + 1)
                    if n >= NK:
                        pool.wait_ge(s["a_scores"], ONE + i * NS + n - NK + 1)
                    else:
                        pool.wait_ge(s["a_scores"], ONE + i * NS)
                    pool.tensor_tensor(k_hd[n % NK], k_rot[:, n % 4, n // 4, :].unsqueeze(1).broadcast_to([P, E, S]),
                                       headmask.unsqueeze(2).broadcast_to([P, E, S]), ALU.mult).then_inc(s["a_khd_ready"], 1)

                for n in range(NK):
                    heads(n)
                for n in range(NS):
                    pool.wait_ge(s["a_recip"], ONE + i * NS + n + 1)
                    pool.tensor_tensor(probs_a[n % NP], probs_a[n % NP], rs_a[:, n % 4, :].unsqueeze(2).broadcast_to([P, E, S]),
                                       ALU.mult).then_inc(s["a_probs"], 1)
                    if n + NK < NS:
                        heads(n + NK)
            pool.sem_inc(s["a_loop_done"], 1)
            pool.wait_ge(s["a_loop_done"], 3)
            pool.dma_start(f0["sel"][0:KC].rearrange("p c m -> p (c m)"), a["sel0"]).then_inc(s["sel0_cast"], 16)
            NB = 4
            with pool.Fori(0, NA) as i:
                for b in range(NB):
                    pool.wait_ge(s["b_recip"], ONE + i * NB + b + 1)
                    pool.tensor_tensor(probs_b[b % 2], probs_b[b % 2], rs_b[:, b % 2, :].unsqueeze(2).broadcast_to([P, G1, S]),
                                       ALU.mult).then_inc(s["b_probs"], 1)
            pool.wait_ge(s["b_resid"], ONE + NA * 2)
            pool.dma_start(f1["sel"][0:KC].rearrange("p c m -> p (c m)"), a["sel1"]).then_inc(s["sel1_cast"], 16)

        @block.vector
        def _(ve):
            start(ve, "vector")
            st = Steps(ve, s["vector_steps"])

            TWO_PI, PI = float(2 * np.pi), 3.14159250
            ROUND = 1.5 * 2.0 ** 23
            ve.wait_ge(s["pos_loaded"], 16)
            ve.wait_ge(s["const_loaded"], 128)
            for n in range(2):
                w = slice(256 * n, 256 * n + 256)
                st.done(ve.tensor_scalar(ang[:, w], pos, tiny[:, n:n + 1], tiny[:, 2 + n:3 + n], ALU.mult, ALU.add))
                st.wait()
                st.done(ve.tensor_scalar(turn[:, w], ang[:, w], 1.0 / TWO_PI, ROUND, ALU.mult, ALU.add))
                st.wait()
                st.done(ve.tensor_scalar(turn[:, w], turn[:, w], ROUND, -TWO_PI, ALU.subtract, ALU.mult))
                st.wait()
                st.done(ve.tensor_tensor(ang[:, w], ang[:, w], turn[:, w], ALU.add))
                st.wait()
                ve.tensor_scalar(ang[:, w], ang[:, w], PI, -PI, ALU.min, ALU.max).then_inc(s["trig_wanted"], 1)
            ve.memset(q_bd, 0.0).then_inc(s["zeros_ready"], 1)
            ve.wait_ge(s["gates_ready"], 1)
            st.done(ve.tensor_scalar(gbout, gbout, gates[:, 0:1], None, ALU.mult))

            for n in range(4):
                ve.wait_ge(s["x_loaded"], 64)
                for t in range(8 * n, 8 * n + 8):
                    st.done(ve.bn_stats(bn[:, t, :], x[:, t, :]))
            st.wait()

            def stats(n):
                for t in range(NT):
                    st.done(ve.bn_aggr(mv[:, t, :], bn[:, t, :]))
                st.wait()
                ve.tensor_scalar(sd, mv[:, :, 1], LN_EPS, None, ALU.add).then_inc(s["sd_wanted"], 1)
                ve.wait_ge(s["sd_ready"], n + 1)
                st.done(ve.reciprocal(rstd, sd))
                st.wait()
                st.done(ve.scalar_tensor_tensor(out=nmr, in0=mv[:, :, 0], scalar=-1.0, in1=rstd, op0=ALU.mult, op1=ALU.mult))
                st.wait()

            def normalise(dst, tile):
                return ve.tensor_scalar(dst, x[:, ds(tile, 1), :], rstd[:, ds(tile, 1)], nmr[:, ds(tile, 1)], ALU.mult, ALU.add)

            stats(0)
            NS = 8
            WS = W0N // NA
            ve.wait_ge(s["tables_loaded"], 512)
            with ve.Fori(0, NA) as i:
                st.loop(i, 42)
                ve.wait_ge(s["a_xnT_psum"], ONE + i)
                normalise(xn_a[:, 0:1, :], i * 2)
                st.done(normalise(xn_a[:, 1:2, :], i * 2 + 1))
                st.wait()
                ve.sem_inc(s["a_xn_ready"], 1)
                st.done(ve.tensor_tensor(x[:, ds(i * 2, 2), :], x[:, ds(i * 2, 2), :],
                                         gbout.unsqueeze(1).broadcast_to([P, 2, D]), ALU.add))

                def rope(src, swapped, sums):
                    c = cosT[:, ds(i * 2, 2), :].unsqueeze(1).broadcast_to([P, HG, 2, S])
                    sn = sinT[:, ds(i * 2, 2), :].unsqueeze(1).broadcast_to([P, HG, 2, S])
                    ve.sem_inc(s["vector_passed"], 1)
                    st.done(ve.stream_shuffle(swapped.rearrange("p g t k -> p (g t k)"), src.rearrange("p g t k -> p (g t k)"),
                                              [j ^ 1 for j in range(32)]))
                    st.wait()
                    for g in range(HG):
                        st.done(ve.tensor_tensor(src[:, g], src[:, g], cosT[:, ds(i * 2, 2), :], ALU.mult))
                        st.done(ve.tensor_tensor(swapped[:, g], swapped[:, g], sinT[:, ds(i * 2, 2), :], ALU.mult))
                    st.wait()
                    for dst, x0, x1, ready in sums:
                        m = ve.tensor_tensor(dst, x0, x1, ALU.add)
                    m.then_inc(s[ready], 1)

                ve.wait_ge(s["a_ks_ready"], ONE + i + 1)
                ve.wait_ge(s["a_khd_ready"], ONE + i * NS)
                rope(ks_a, kw_a, [(k_rot, ks_a, kw_a, "a_k_ready")])
                ve.wait_ge(s["a_qs_ready"], ONE + i + 1)
                ve.wait_ge(s["a_scores"], ONE + i * NS)
                halves = []
                for b in range(2):
                    rows = slice(64 * b, 64 * b + 64)
                    halves.append((q_bd[rows, :, :, b, :], qs_a[rows], qw_a[rows], "a_q_ready"))
                rope(qs_a, qw_a, halves)
                for t in range(NS + 4):
                    if t < NS:
                        ve.wait_ge(s["a_scores"], ONE + i * NS + t + 1)
                        sc = bank[t % 2][:, :].rearrange("p (h k) -> p h k", h=E)
                        st.done(ve.tensor_reduce(rm_a[:, t % 2, :], sc, AX_X, ALU.max))
                        if t < NP:
                            ve.wait_ge(s["a_pT_psum"], ONE + i * NS)
                        else:
                            ve.wait_ge(s["a_pT_psum"], ONE + i * NS + t - NP + 1)
                        st.wait()
                        ve.tensor_tensor(probs_a[t % NP], sc, rm_a[:, t % 2, :].unsqueeze(2).broadcast_to([P, E, S]),
                                         ALU.subtract).then_inc(s["a_centred"], 1)
                    n = t - 1
                    if 0 <= n < NS:
                        ve.wait_ge(s["a_exp"], ONE + i * NS + n + 1)
                        st.done(ve.tensor_reduce(rs_a[:, n % 4, :], probs_a[n % NP], AX_X, ALU.add))
                        st.wait()
                        ve.reciprocal(rs_a[:, n % 4, :], rs_a[:, n % 4, :]).then_inc(s["a_recip"], 1)
                    n = t - 3
                    if 0 <= n < NS:
                        ve.wait_ge(s["a_o_psum"], ONE + i * NS + n + 1)
                        ve.tensor_tensor(oT_a[:, n // 4, n % 4, :], bank[4][:, 0:P], ownbatch, ALU.mult).then_inc(s["a_oT_ready"], 1)
                    n = t - 4
                    if n in (3, 7):
                        u = n // 4
                        ve.wait_ge(s["a_y_psum"], ONE + i * 2 + u + 1)
                        xt = x[:, ds(i * 2 + u, 1), :].rearrange("p a d -> p (a d)")
                        st.done(ve.scalar_tensor_tensor(out=xt, in0=bank[5][:, 0:D], scalar=gates[:, 0:1], in1=xt,
                                                        op0=ALU.mult, op1=ALU.add))
                        st.wait()
                        ve.sem_inc(s["a_resid"], 1)
                        st.done(ve.bn_stats(bn[:, ds(i * 2 + u, 1), :].rearrange("p a d -> p (a d)"), xt))
                ve.wait_ge(s["w0f_loaded"], i * 16 + 32)
                st.done(ve.tensor_copy(w0_hi[:, ds(i * WS, WS)], w0_raw[:, ds(i * WS, WS)]))
                st.wait()
                st.done(ve.tensor_tensor(w0_lo[:, ds(i * WS, WS)], w0_raw[:, ds(i * WS, WS)],
                                         w0_hi[:, ds(i * WS, WS)], ALU.subtract))
            st.end(NA)
            st.wait()
            ve.sem_inc(s["a_loop_done"], 1)

            def split_router(f, n, loads, bias):
                ve.wait_ge(s[f"sel{n}_loaded"], loads)
                parts = [tuple(f[f"rw_{k}"] for k in ("hi", "lo", "raw"))]
                if bias:
                    parts.append(tuple(f[f"bd_{k}"][0:KC] for k in ("hi", "lo", "raw")))
                for hi, lo, raw in parts:
                    st.done(ve.tensor_copy(hi, raw))
                st.done(ve.memset(f["lT"][0:64, :], 0.0))
                st.wait()
                for hi, lo, raw in parts:
                    st.done(ve.tensor_tensor(lo, raw, hi, ALU.subtract))
                st.done(ve.tensor_copy(f["cT"][0:64, :], f["lT"][0:64, :]))
                st.wait()
                ve.sem_inc(s["rw_split"], 1)

            def ffn(ph, f, chunks, hidden, gated, gate, steps, out_stats):
                last = {c: (hidden - c * P if (c + 1) * P > hidden else P) for c in range(chunks)}
                NL = E + 1 if gated else E
                with ve.Fori(0, NF) as i:
                    st.loop(i, steps)
                    ve.wait_ge(s[f"{ph}_xnT_psum"], ONE + i)
                    for t in range(FT):
                        st.done(normalise(f["xn"][:, t:t + 1, :], i * FT + t))
                    st.wait()
                    ve.sem_inc(s[f"{ph}_xn_ready"], 1)
                    ve.wait_ge(s[f"{ph}_xh_ready"], ONE + i * KT + KT)
                    for k in range(KT):
                        ve.tensor_tensor(f["xl"][:, k, :], bank[k][:, :], f["xh"][:, k, :], ALU.subtract).then_inc(
                            s[f"{ph}_xl_ready"], 1)
                    ve.wait_ge(s[f"{ph}_logitT_psum"], ONE + i + 1)
                    st.done(ve.tensor_copy(f["lg"][:, :, 0:NL], bank[6][:, 0:64].rearrange("p (t n) -> p t n", n=16)[:, :, 0:NL]))
                    st.wait()
                    ve.sem_inc(s["vector_passed"], 1)
                    for t in range(FT):
                        st.done(ve.max(f["m8"][:, t, :], f["lg"][:, t, 0:E]))
                    st.wait()
                    ve.sem_inc(s["vector_passed"], 1)
                    for t in range(FT):
                        st.done(ve.max_index(f["ix"][:, t, :].bitcast(U32), f["m8"][:, t, :], f["lg"][:, t, 0:E]))
                    st.done(ve.tensor_tensor(f["dl"][:, :, 0], f["m8"][:, :, 1], f["m8"][:, :, 0], ALU.subtract))
                    if gated:
                        st.done(ve.tensor_scalar(f["dl"][:, :, 1], f["lg"][:, :, E], -1.0, None, ALU.mult))
                    else:
                        st.done(ve.memset(f["dl"][:, :, 1], 0.0))
                    st.wait()
                    ve.sem_inc(s[f"{ph}_delta_ready"], 1)
                    st.done(ve.tensor_copy(f["ixf"], f["ix"][:, :, 0:2].bitcast(U32)))
                    ve.wait_ge(s[f"{ph}_exp_ready"], ONE + i + 1)
                    st.done(ve.tensor_scalar(f["wt"], f["ed"], 1.0, None, ALU.add))
                    st.wait()
                    st.done(ve.reciprocal(f["wt"], f["wt"]))
                    st.wait()
                    if gated:
                        st.done(ve.tensor_copy(f["comb"][:, :, E], f["wt"][:, :, 1]))
                    st.done(ve.tensor_tensor(f["ed"][:, :, 0], f["ed"][:, :, 0], f["wt"][:, :, 0], ALU.mult))
                    st.wait()
                    for t in range(FT):
                        st.done(ve.tensor_scalar(f["comb"][:, t, 0:E], iota8, f["ixf"][:, t, 0:1], f["wt"][:, t, 0:1],
                                                 ALU.is_equal, ALU.mult))
                        st.done(ve.tensor_scalar(f["c2"][:, t, :], iota8, f["ixf"][:, t, 1:2], f["ed"][:, t, 0:1],
                                                 ALU.is_equal, ALU.mult))
                    st.wait()
                    st.done(ve.tensor_tensor(f["comb"][:, :, 0:E], f["comb"][:, :, 0:E], f["c2"], ALU.add))
                    st.wait()
                    ve.sem_inc(s[f"{ph}_comb_ready"], 1)

                    def product(c):
                        if not gated:
                            return
                        M = last[c]
                        if c >= 3:
                            ve.wait_ge(s[f"{ph}_hl_ready"], ONE + i * chunks + c - 2)
                        ve.wait_ge(s[f"{ph}_silu"], ONE + i * chunks + c + 1)
                        ve.tensor_tensor(f["act"][c % 3][0:M, :], bank[2 + c % 2][0:M, :], f["s"][c % 2][0:M, :],
                                         ALU.mult).then_inc(s[f"{ph}_act_ready"], 1)

                    def scaled(c):
                        M = last[c]
                        ve.wait_ge(s[f"{ph}_cb_psum"], ONE + i * chunks + c + 1)
                        if gated:
                            ve.wait_ge(s[f"{ph}_act_ready"], ONE + i * chunks + c + 1)
                            ve.tensor_tensor(f["act"][c % 3][0:M, :], bank[4][0:M, :], f["act"][c % 3][0:M, :],
                                             ALU.mult).then_inc(s[f"{ph}_scaled"], 1)
                        else:
                            if c >= 3:
                                ve.wait_ge(s[f"{ph}_hl_ready"], ONE + i * chunks + c - 2)
                            ve.wait_ge(s[f"{ph}_silu"], ONE + i * chunks + c + 1)
                            ve.tensor_tensor(f["act"][c % 3][0:M, :], bank[4][0:M, :], f["s"][c % 2][0:M, :],
                                             ALU.mult).then_inc(s[f"{ph}_scaled"], 1)

                    def low(c):
                        M = last[c]
                        ve.wait_ge(s[f"{ph}_hh_ready"], ONE + i * chunks + c + 1)
                        ve.tensor_tensor(f["hl"][c % 3][0:M, :], f["act"][c % 3][0:M, :], f["hh"][c % 3][0:M, :],
                                         ALU.subtract).then_inc(s[f"{ph}_hl_ready"], 1)

                    product(0)
                    product(1)
                    ve.wait_ge(s[f"{ph}_combT_psum"], ONE + i + 1)
                    ve.wait_ge(s[f"{ph}_cTh_ready"], ONE + i + 1)
                    ve.tensor_tensor(f["cT"][LOW:LOW + NL, :], bank[6][0:NL, :], f["cT"][0:NL, :],
                                     ALU.subtract).then_inc(s[f"{ph}_cTl_ready"], 1)
                    for t in range(1, chunks + 2):
                        if 0 <= t - 1 < chunks:
                            scaled(t - 1)
                        if 2 <= t < chunks:
                            product(t)
                        if 0 <= t - 2 < chunks:
                            low(t - 2)
                    ve.wait_ge(s[f"{ph}_down_done"], ONE + i * chunks + chunks)
                    for u in range(2):
                        xt = x[:, ds(i * FT + 2 * u, 2), :].rearrange("p a d -> p (a d)")
                        st.done(ve.scalar_tensor_tensor(out=xt, in0=bank[5 + 2 * u][:, :], scalar=gates[:, gate:gate + 1], in1=xt,
                                                        op0=ALU.mult, op1=ALU.add))
                    st.wait()
                    ve.sem_inc(s[f"{ph}_resid"], 1)
                    if out_stats:
                        for t in range(FT):
                            st.done(ve.bn_stats(bn[:, ds(i * FT + t, 1), :].rearrange("p a d -> p (a d)"),
                                                x[:, ds(i * FT + t, 1), :].rearrange("p a d -> p (a d)")))
                st.end(NF)
                st.wait()
                ve.sem_inc(s[f"{ph}_loop_done"], 1)

            stats(1)
            split_router(f0, 0, 16, False)
            ffn("f0", f0, NC0, HID0, True, 1, 35, True)
            stats(2)
            ve.wait_ge(s["mask_loaded"], 16)
            st.done(ve.tensor_copy(maskrow[0:B, :], maskraw.bitcast(U8)[0:B, :]))
            st.wait()
            st.done(ve.tensor_reduce(validb[0:B, 0:1], maskrow[0:B, :], AX_X, ALU.max))
            st.wait()
            st.done(ve.tensor_copy(valid[0:B, :], validb[0:B, 0:1].broadcast_to([B, P])))
            st.done(ve.tensor_scalar(maskrow[0:B, :], maskrow[0:B, :], 1.0, -MASKED, ALU.subtract, ALU.mult))
            st.wait()
            ve.sem_inc(s["mask_ready"], 1)
            for h in range(H1):
                ve.wait_ge(s["scalar_steps"], h + 1)
                ve.tensor_tensor(m_lo[:, h].rearrange("p k c -> p (k c)"), bank[h % 2][:, 0:256],
                                 m_hi[:, h].rearrange("p k c -> p (k c)"), ALU.subtract).then_inc(s["m_copied"], 1)
            for c in range(H1 // 2):
                ve.wait_ge(s["scalar_steps"], H1 + c + 1)
                ve.tensor_tensor(n_lo[:, 2 * c:2 * c + 2, :].rearrange("p u n -> p (u n)"), bank[2 + c % 2][:, :],
                                 n_hi[:, 2 * c:2 * c + 2, :].rearrange("p u n -> p (u n)"), ALU.subtract).then_inc(s["n_copied"], 1)
            ve.wait_ge(s["valid_psum"], 1)
            st.done(ve.tensor_copy(validb, bank[0][:, 0:B]))
            st.wait()
            ve.sem_inc(s["valid_ready"], 1)
            ve.wait_ge(s["n_psum"], H1 // 2)
            st.done(ve.memset(ones_raw, 1.0))
            st.wait()
            ve.tensor_copy(ones, ones_raw).then_inc(s["ones_ready"], 1)
            ve.wait_ge(s["o1_loaded"], 48)
            st.done(ve.tensor_copy(w1_hi, w1_raw))
            st.wait()
            ve.tensor_tensor(w1_lo, w1_raw, w1_hi, ALU.subtract).then_inc(s["w1_split"], 1)
            NB = 4
            with ve.Fori(0, NA) as i:
                st.loop(i, 18)
                ve.wait_ge(s["b_xnT_psum"], ONE + i)
                st.done(normalise(xn_b[:, 0:1, :], i * 2))
                st.done(normalise(xn_b[:, 1:2, :], i * 2 + 1))
                st.wait()
                ve.sem_inc(s["b_xn_ready"], 1)
                ve.wait_ge(s["b_xh_ready"], ONE + i + 1)
                ve.tensor_tensor(xl_b.rearrange("p k t -> p (k t)"), bank[4][:, :],
                                 xh_b.rearrange("p k t -> p (k t)"), ALU.subtract).then_inc(s["b_xl_ready"], 1)
                ve.wait_ge(s["b_cxh"], ONE + i + 1)
                ve.tensor_copy(mrow[0:1, :], mrow_raw[0:1, :]).then_inc(s["b_mrow"], 1)
                m = ve.tensor_tensor(cx_lo, cx_raw, cx_hi, ALU.subtract)
                m.then_inc(s["b_cxl"], 1)

                def centre(b):
                    ve.wait_ge(s["b_scores"], ONE + i * NB + b + 1)
                    sc = bank[b % 2][:, :].rearrange("p (g k) -> p g k", g=G1)
                    st.done(ve.tensor_reduce(rm_b[:, b % 2, :], sc, AX_X, ALU.max))
                    if b >= 2:
                        ve.wait_ge(s["b_pT_psum"], ONE + i * NB + b - 1)
                    st.wait()
                    ve.tensor_tensor(probs_b[b % 2], sc, rm_b[:, b % 2, :].unsqueeze(2).broadcast_to([P, G1, S]),
                                     ALU.subtract).then_inc(s["b_centred"], 1)

                def weigh(b):
                    ve.wait_ge(s["b_exp"], ONE + i * NB + b + 1)
                    st.done(ve.tensor_reduce(rs_b[:, b % 2, :], probs_b[b % 2], AX_X, ALU.add))
                    st.wait()
                    st.done(ve.reciprocal(rs_b[:, b % 2, :], rs_b[:, b % 2, :]))
                    st.wait()
                    ve.tensor_scalar(rs_b[:, b % 2, :], rs_b[:, b % 2, :], validb[:, ds(i * NB + b, 1)], None,
                                     ALU.mult).then_inc(s["b_recip"], 1)

                def ptl(b):
                    ve.wait_ge(s["b_pTh"], ONE + i * NB + b + 1)
                    ve.tensor_tensor(pTl[b % 2], bank[2 + b % 2][:, :], pTh[b % 2], ALU.subtract).then_inc(s["b_pTl"], 1)

                def otl(b):
                    for par in range(2):
                        ve.wait_ge(s["b_oTh"], ONE + i * NB * 2 + 2 * b + par + 1)
                        ve.tensor_tensor(oTl[:, :, par, :, b * S:(b + 1) * S],
                                         bank[4 + par][:, :].rearrange("p (j u q) -> p j u q", j=4, u=2),
                                         oTh[:, :, par, :, b * S:(b + 1) * S], ALU.subtract).then_inc(s["b_oTl"], 1)

                def resid(t):
                    ve.wait_ge(s["b_y_psum"], ONE + i * 2 + t + 1)
                    xt = x[:, ds(i * 2 + t, 1), :].rearrange("p a d -> p (a d)")
                    st.done(ve.scalar_tensor_tensor(out=xt, in0=bank[6][:, 0:D], scalar=gates[:, 2:3], in1=xt,
                                                    op0=ALU.mult, op1=ALU.add))
                    st.wait()
                    ve.sem_inc(s["b_resid"], 1)
                    st.done(ve.bn_stats(bn[:, ds(i * 2 + t, 1), :].rearrange("p a d -> p (a d)"), xt))

                centre(0)
                centre(1)
                weigh(0)
                weigh(1)
                ptl(0)
                centre(2)
                ptl(1)
                otl(0)
                weigh(2)
                centre(3)
                otl(1)
                weigh(3)
                ptl(2)
                resid(0)
                ptl(3)
                otl(2)
                otl(3)
                resid(1)
            st.end(NA)
            st.wait()
            stats(3)
            split_router(f1, 1, 48, True)
            ffn("f1", f1, NC1, HID1, False, 3, 30, False)


def _layouts(v):
    f = np.float32
    c = np.ascontiguousarray

    def cols(w):
        return c(w.reshape(-1, P, w.shape[1]).transpose(1, 0, 2).reshape(P, -1))

    o = {}
    o["x"] = v["x"].reshape(T, D)
    o["ctx"] = v["ctx_1024"]
    o["ctxT"] = c(v["ctx_1024"].reshape(T, CD).T)
    fs = v["fside_BxSx2_0"].reshape(NT, 2, S, 2)
    d = np.arange(HD0)
    axis, half = d // 4, (d % 4) // 2
    o["pos"] = c(fs.transpose(1, 3, 0, 2)[:, axis].reshape(P, 256))
    freq = (ROPE_BASE ** (-(half.astype(f)) / f(2))).astype(f)
    sign = np.where(d % 2 == 0, -1.0, 1.0).astype(f)
    per = np.stack([freq * sign, freq, np.zeros(HD0, f), np.full(HD0, np.pi / 2, f)], 1)
    o["freq"] = c(np.broadcast_to(per[None, :, None, :], (2, HD0, 8, 4)).reshape(P, 4).astype(f))
    g = np.stack([v["g_xattn"][0], v["g_ffn"][0], v["g_xattn"][1], v["g_ffn"][1]])
    o["gates"] = c(np.broadcast_to(g[None, :], (P, 4)))
    o["ident"] = np.eye(P, dtype=f)
    p = np.arange(P)
    o["headmask"] = ((p[:, None] % 64) // 8 == np.arange(E)[None, :]).astype(f)
    o["ownbatch"] = ((p[:, None] // 16) % 2 == p[None, :] // 64).astype(f)
    o["iota8"] = c(np.broadcast_to(np.arange(E, dtype=f)[None, :], (P, E)))
    o["bout"] = c(np.broadcast_to(v["L0_xattn_bout"][None, :], (P, D)))
    o["bup"] = c(v["L1_ffn_bup"].T)
    o["mask"] = v["mask_BxS2_bf1"].view(np.uint8)
    o["wq0"] = cols(v["L0_xattn_Wq"])
    o["wk0"] = c(v["L0_xattn_Wkv"][:, :D])
    wv = v["L0_xattn_Wkv"][:, D:].reshape(CD, 16, 2, HD0)
    o["wv0"] = c(wv.transpose(0, 2, 1, 3).reshape(CD, 2 * P))
    wo = v["L0_xattn_Wout"].reshape(HG, 4, 1, 2, HD0, D)
    o["wo0"] = cols(np.broadcast_to(wo, (HG, 4, 2, 2, HD0, D)).reshape(HG * P, D))
    gu, pad = v["L0_ffn_gate_up_proj"], NC0 * P - HID0
    z = np.zeros((pad, D), f)
    gate = np.concatenate([gu[:, :I_MOE].reshape(-1, D), v["L0_ffn_sh_gate_w"], z])
    up = np.concatenate([gu[:, I_MOE:].reshape(-1, D), v["L0_ffn_sh_up_w"], z])
    down = np.concatenate([v["L0_ffn_down_proj"].transpose(0, 2, 1).reshape(-1, D), v["L0_ffn_sh_down_w"].T, z])
    o["w0"] = c(np.concatenate([cols(gate.T), cols(up.T), cols(down)], 1))
    rw = np.concatenate([v["L0_ffn_router_weight"], v["L0_ffn_shared_gate_w"], np.zeros((1, D), f)])
    o["rw0"] = cols(rw.T)
    unit = np.arange(NC0 * P)
    owner = np.where(unit < E * I_MOE, unit // I_MOE, E)
    sel = np.zeros((KC, NC0 * P), f)
    sel[owner, unit] = 1
    sel[LOW + owner, unit] = 1
    o["sel0"] = sel
    o["wq1"] = c(v["L1_xattn_Wq"].reshape(D, H1, P).transpose(2, 1, 0).reshape(P, -1))
    o["wk1"] = c(v["L1_xattn_Wk"].reshape(CD, G1, P).transpose(2, 1, 0).reshape(P, -1))
    o["wv1"] = c(v["L1_xattn_Wv"].reshape(CD, G1, P).transpose(2, 1, 0).reshape(P, -1))
    o["wo1"] = cols(v["L1_xattn_Wo"])
    o["w1"] = c(np.concatenate([cols(v["L1_ffn_Wup"].reshape(HID1, D).T),
                                cols(v["L1_ffn_Wdown"].transpose(0, 2, 1).reshape(HID1, D))], 1))
    o["rw1"] = cols(np.concatenate([v["L1_ffn_Wg1"], np.zeros((2, D), f)]).T)
    o["wg2"] = c(v["L1_ffn_Wg2"].T)
    unit = np.arange(HID1)
    sel = np.zeros((KC, HID1), f)
    sel[unit // P, unit] = 1
    sel[LOW + unit // P, unit] = 1
    o["sel1"] = sel
    bd = np.zeros((KC, D), f)
    bd[0:E] = v["L1_ffn_bdown"]
    bd[LOW:LOW + E] = v["L1_ffn_bdown"]
    o["bdown"] = bd
    return o


def kernel(**inputs):
    import concourse.bacc as _bacc
    from concourse.bass_utils import run_bass_kernel_spmd as _run

    arrays = _layouts({k: np.asarray(v) for k, v in inputs.items()})
    nc = _bacc.Bacc("TRN2", target_bir_lowering=False, num_devices=1)
    a = {k: nc.dram_tensor(f"in_{k}", w.shape, mybir.dt.from_np(w.dtype), kind="ExternalInput").ap()
         for k, w in arrays.items()}
    out = nc.dram_tensor("out_0", (T, D), F32, kind="ExternalOutput").ap()
    build(nc, a, out)
    r = _run(nc, [{f"in_{k}": w for k, w in arrays.items()}], core_ids=[0])
    return r.results[0]["out_0"].reshape(B, S, D)
```

```python
import concourse.bass as bass
from concourse import mybir
from contextlib import ExitStack
import numpy as np

F32 = mybir.dt.float32
FR = mybir.dt.float32r
I32 = mybir.dt.int32
U32 = mybir.dt.uint32
U8 = mybir.dt.uint8
ALU = mybir.AluOpType
ACT = mybir.ActivationFunctionType
AX_X = mybir.AxisListType.X
P = 128
ds = bass.ds

B, S, D = 64, 64, 256
CD = 128
T = B * S
NT = T // P
KT = D // P
H0, HD0 = 32, 8
HG = 4
H1, G1 = 16, 8
E = 8
I_MOE, I_SH = 176, 704
HID0 = E * I_MOE + I_SH
NC0 = -(-HID0 // P)
HID1 = 1024
NC1 = HID1 // P
LN_EPS = 1e-5
ROPE_BASE = 10000.0
MASKED = -(2.0 ** 100)
LOW = 32
KC = LOW + E + 1

START = 4
NA = 16
NF = 8
FT = NT // NF
SLOTS = {"f0": dict(norm=1, t0=3, t1=5, logits=7, back=9, weights=14),
         "f1": dict(norm=0, t0=1, t1=2, logits=3, back=4, weights=8)}
STEPS = {"a": 32, "b": 22, "f0": 78, "f1": 58}


def rounds(eng, n, body):
    body(0, first=True)
    with eng.Fori(1, n - 1) as i:
        body(i)
    body(n - 1, last=True)


def pairs(eng, n, body):
    with eng.Fori(0, n // 2 - 1) as j:
        for u in range(2):
            body(j * 2 + u, u, True)
    body(n - 2, 0, True)
    body(n - 1, 1, False)


class Steps:

    def __init__(self, eng, sem):
        self.eng, self.sem, self.base, self.n, self.per, self.i = eng, sem, 0, 0, None, 0

    def loop(self, i, per, first=0):
        self.base, self.n, self.per, self.i = self.base + self.n - first * per, 0, per, i

    def end(self, last):
        assert self.n == self.per, f"steps a round: {self.n}"
        self.base, self.n, self.per, self.i = self.base + last * self.per, 0, None, 0

    def done(self, ins):
        ins.then_inc(self.sem, 1)
        self.n += 1
        return self.value()

    def value(self):
        if self.per is None:
            return self.base + self.n
        return self.i * self.per + (self.base + self.n)

    def wait(self, value=None):
        self.eng.wait_ge(self.sem, self.value() if value is None else value)


def build(nc, a, out):
    with ExitStack() as ctx:
        def sem(name):
            return ctx.enter_context(nc.semaphore(name))

        FIRST = -(-nc.sbuf_base // 32) * 32
        WORDS = (nc.sbuf_top - FIRST) // 4

        class Region:

            def __init__(self, at):
                self.at = self.last = at

            def take(self, name, *shape, dtype=F32, over=False):
                n = int(np.prod(shape))
                at = self.last if over else self.at
                t = nc.alloc_sbuf_tensor_at(name, [P, n], dtype, offset=FIRST + 4 * at)
                self.last, self.at = at, max(self.at, at + -(-n // 8) * 8)
                assert self.at <= WORDS, (name, self.at, WORDS)
                v = t[:, :]
                if len(shape) == 1:
                    return v
                names = "abcdef"[:len(shape)]
                return v.rearrange(f"p ({' '.join(names)}) -> p {' '.join(names)}",
                                   **{k: m for k, m in zip(names, shape)})

            def split(self, name, *shape):
                raw = self.take(name + "_raw", *shape)
                lo = self.take(name + "_lo", *shape, dtype=FR, over=True)
                return self.take(name + "_hi", *shape, dtype=FR), lo, raw

            def halves(self, name, *shape):
                return self.take(name + "_hi", *shape, dtype=FR), self.take(name + "_lo", *shape, dtype=FR)

        keep = Region(0)
        x = keep.take("x", NT, D)
        ident = keep.take("ident", P)
        headmask = keep.take("headmask", E)
        ownbatch = keep.take("ownbatch", P)
        gates = keep.take("gates", 4)
        tiny = keep.take("freqs", 4)
        iota8 = keep.take("iota8", E)
        bn = keep.take("bn", 8, 6)
        mv = keep.take("mean_var", NT, 2)
        mv_new = keep.take("mean_var_new", FT, 2)
        sd = keep.take("sd", NT)
        rstd = keep.take("rstd", NT)
        nmr = keep.take("nmr", NT)
        gbout = keep.take("gbout", D)
        validb = keep.take("validb", B)
        bup = keep.take("bup", NC1)
        maskraw = keep.take("maskraw", S // 4)
        wide = keep.at
        w0 = Region(wide)
        W0N = (2 * KT * NC0 + 2 * NC0) * P
        w0_hi, w0_lo, w0_raw = w0.split("w0", W0N)
        local = w0.at

        def ffn0_view(w):
            n = KT * NC0 * P
            gate = w[:, 0:n].rearrange("p (k m) -> p k m", k=KT)
            up = w[:, n:2 * n].rearrange("p (k m) -> p k m", k=KT)
            down = w[:, 2 * n:].rearrange("p (c n) -> p c n", n=D)
            return gate, up, down

        w1 = Region(wide)
        m_hi, m_lo = w1.halves("m", H1, KT, P)
        n_hi, n_lo = w1.halves("n", H1, D)
        w1_hi, w1_lo, w1_raw = w1.split("w1", KT * HID1 + NC1 * D)
        valid = w1.take("valid", P)
        ctxT_b = w1.take("ctxT_b", 4, S)
        mrow_raw = w1.take("mrow_raw", 4 * S)
        mrow = w1.take("mrow", 4 * S, dtype=FR)
        ones_raw = w1.take("ones_raw", P)
        ones = w1.take("ones", P, dtype=FR)
        maskrow = w1.take("maskrow", S)
        assert w1.at <= w0.at

        def ffn1_view(w):
            return w[:, 0:KT * HID1].rearrange("p (k m) -> p k m", k=KT), \
                w[:, KT * HID1:].rearrange("p (c n) -> p c n", n=D)

        r = Region(local)
        cosT = r.take("cosT", NT, S)
        sinT = r.take("sinT", NT, S)
        wq0 = r.take("wq0", KT, D)
        wk0 = r.take("wk0", D)
        wv0 = r.take("wv0", 2, P)
        wo0 = r.take("wo0", HG, D)
        xn_a = r.take("xn_a", 2, D)
        xnT_a = r.take("xnT_a", KT, 2, P)
        ctxT_a = r.take("ctxT_a", 2, P)
        kw_a, qs_a, qw_a = (r.take(n, HG, 2, S) for n in ("kw_a", "qs_a", "qw_a"))
        q_bd = r.take("q_bd", HG, 2, 2, S)
        k_rot = r.take("k_rot", HG, 2, S)
        v_bd = r.take("v_bd", 2, 16, 2, 2, HD0)
        NK = 4
        k_hd = [r.take(f"k_hd{n}", E, S) for n in range(NK)]
        NP = 4
        probs_a = [r.take(f"probs_a{n}", E, S) for n in range(NP)]
        pT_a = [r.take(f"pT_a{n}", 4, P) for n in range(2)]
        oT_a = r.take("oT_a", 2, HG, P)
        rm_a = r.take("rm_a", 2, E)
        rs_a = r.take("rs_a", 4, E)
        pos, ang, turn, trig = (k_hd[n].rearrange("p a b -> p (a b)") for n in range(4))
        pos = pos[:, 0:256]

        def ffn_region(n, chunks):
            r = Region(local)
            f = {}
            f["sel"] = r.take(f"sel{n}", chunks, P, dtype=FR)
            f["xn"] = r.take(f"xn{n}", FT, D)
            f["xh"], f["xl"] = zip(*(r.halves(f"xT{n}{m}", KT, FT * P) for m in range(2)))
            f["s"] = [r.take(f"s{n}{m}", FT * P) for m in range(2)]
            f["act"] = [r.take(f"act{n}{m}", FT * P) for m in range(3)]
            f["hh"] = [r.take(f"hh{n}{m}", FT * P, dtype=FR) for m in range(3)]
            f["hl"] = [r.take(f"hl{n}{m}", FT * P, dtype=FR) for m in range(3)]
            f["cT"] = [r.take(f"cT{n}{m}", FT * P, dtype=FR) for m in range(2)]
            for k, shape in (("lT", (FT * P,)), ("lg", (FT, E + 1)), ("m8", (FT, E)), ("ix", (FT, E)), ("ixf", (FT, 2)),
                             ("dl", (FT, 2)), ("ed", (FT, 2)), ("wt", (FT, 2)), ("w2", (FT, 1)), ("comb", (FT, E + 1)), ("c2", (FT, E)),
                             ("wg2", (E,))):
                f[k] = r.take(f"{k}{n}", *shape)
            f["rw_hi"], f["rw_lo"], f["rw_raw"] = r.split(f"rw{n}", KT, E + 2)
            f["bd_hi"], f["bd_lo"], f["bd_raw"] = r.split(f"bd{n}", D)
            return f, r

        f0, r0 = ffn_region(0, NC0)
        f1, _ = ffn_region(1, NC1)

        r = Region(local)
        q1_raw = r.take("q1_raw", H1, D)
        k1_raw = r.take("k1_raw", G1, CD)
        o1_raw = r.take("o1_raw", H1, D)
        v1_raw = r.take("v1_raw", G1, CD)
        r = Region(local)
        xn_b = r.take("xn_b", 2, D)
        xh_b, xl_b = r.halves("xT_b", KT, 2 * P)
        qT = r.take("qT", 4, H1, S)
        cx_hi, cx_lo, cx_raw = r.split("cx", 4, CD)
        probs_b = [r.take(f"probs_b{n}", G1, S) for n in range(4)]
        pTh, pTl = r.halves("pT_b", 4 * P)
        oTh, oTl = r.halves("oT_b", 2, 4, 2, 2, P)
        rm_b = w1.take("rm_b", 2, G1)
        rs_b = w1.take("rs_b", 4, G1)
        assert w1.at <= w0.at

        bank = [ctx.enter_context(nc.psum_tensor(f"bank{n}", [P, 512], F32)) for n in range(8)]

        tab = {k: nc.dram_tensor(f"{k}_table", (16, NT * S), F32).ap() for k in ("cos", "sin")}

        biases = nc.dram_tensor("mask_biases", (1, B * S), F32).ap()

        names = """x_loaded const_loaded w0x_loaded w0f_loaded pos_loaded tables_stored tables_loaded
        gates_ready sd_wanted sd_ready zeros_ready gbout_ready trig_wanted trig_ready
        a_xn_ready a_xnT_psum a_xnT_ready a_ctx_loaded a_q_psum a_k_psum a_v_psum a_q_read a_k_read w0_hi a_bias
        a_v_ready a_k_ready a_q_ready a_khd_ready a_scores a_centred a_exp a_recip a_probs a_pT_psum a_pT_ready
        a_o_psum a_oT_ready a_y_psum a_resid a_loop_done
        sel0_loaded sel1_loaded sel0_cast sel1_cast w1_loaded o1_loaded m_psum m_copied n_psum n_copied w1_split rw_split
        mask_loaded mask_ready biases_stored valid_psum valid_ready ones_ready
        b_xn_ready b_xnT_psum b_xh_ready b_xl_ready b_ctx_loaded b_cx_loaded b_q_psum b_q_ready b_cxh b_cxl b_scores b_centred
        b_exp b_recip b_probs b_pT_psum b_pTh b_pTl b_o_psum b_oTh b_oTl b_y_psum b_resid b_mrow
        vector_steps scalar_steps out_stored vector_passed tensor_passed""".split()
        s = {n: sem(n) for n in names}
        for ph in ("f0", "f1"):
            for n in """xn_ready xnT_psum xh_ready xl_ready logit_psum logit_copied logitT_psum delta_ready exp_ready
                    comb_ready combT_psum cTh_ready cTl_ready gu_psum silu act_ready scaled cb_psum hh_ready hl_ready
                    down_done resid loop_done""".split():
                s[f"{ph}_{n}"] = sem(f"{ph}_{n}")

        started = dict(
            tensor="""a_xnT_psum a_q_psum a_k_psum a_v_psum a_scores a_pT_psum a_o_psum a_y_psum
                b_xnT_psum b_q_psum b_scores b_pT_psum b_o_psum b_y_psum
                f_xnT_psum f_logit_psum f_logitT_psum f_combT_psum f_gu_psum f_cb_psum f_down_done""",
            scalar="""a_xnT_ready a_v_ready a_exp a_pT_ready w0_hi
                b_xh_ready b_cxh b_q_ready b_exp b_pTh b_oTh
                f_xh_ready f_logit_copied f_exp_ready f_silu f_cTh_ready f_hh_ready""",
            gpsimd="a_khd_ready a_probs a_bias b_probs",
            vector="""a_xn_ready a_k_ready a_q_ready a_q_read a_k_read a_centred a_recip a_oT_ready a_resid
                b_xn_ready b_xl_ready b_cxl b_mrow b_centred b_recip b_pTl b_oTl b_resid
                f_xn_ready f_xl_ready f_delta_ready f_comb_ready f_cTl_ready f_act_ready f_scaled f_hl_ready f_resid""")

        def start(eng, name):
            for n in started[name].split():
                for ph in ("f0", "f1") if n.startswith("f_") else (None,):
                    eng.sem_inc(s[n if ph is None else ph + n[1:]], START)

        block = ctx.enter_context(nc.Block())

        @block.sync
        def _(sp):
            sp.sem_inc(s["w0f_loaded"], 16)
            xs = a["x"].rearrange("(t p) d -> p t d", p=P)
            sp.dma_start(pos, a["pos"]).then_inc(s["pos_loaded"], 16)
            for n, (dst, src) in enumerate(((tiny[:, 0:4], "freq"), (gates, "gates"), (ident, "ident"), (headmask, "headmask"),
                                            (ownbatch, "ownbatch"), (iota8, "iota8"), (gbout, "bout"), (bup, "bup"))):
                sp.dma_start(dst, a[src]).then_inc(s["const_loaded"], 16)
            for n in range(4):
                sp.dma_start(x[:, 8 * n:8 * n + 8, :], xs[:, 8 * n:8 * n + 8, :]).then_inc(s["x_loaded"], 16)
            for dst, src in ((wq0.rearrange("p k n -> p (k n)"), "wq0"), (wk0, "wk0"),
                             (wv0.rearrange("p k n -> p (k n)"), "wv0"), (wo0.rearrange("p k n -> p (k n)"), "wo0")):
                sp.dma_start(dst, a[src]).then_inc(s["w0x_loaded"], 16)
            sp.dma_start(maskraw.bitcast(U8)[0:B, :], a["mask"]).then_inc(s["mask_loaded"], 16)
            for n, k in enumerate(("sin", "cos")):
                sp.wait_ge(s["trig_ready"], n + 1)
                sp.dma_start(tab[k].rearrange("r (g c) -> (r g) c", c=256), trig[:, 256 * n:256 * n + 256]).then_inc(
                    s["tables_stored"], 16)
            sp.wait_ge(s["tables_stored"], 32)
            for k, dst in (("cos", cosT), ("sin", sinT)):
                for b in range(2):
                    for h in range(8):
                        sp.dma_start(dst[64 * b + 8 * h:64 * b + 8 * h + 8, :, :].rearrange("p t c -> p (t c)"),
                                     tab[k][8 * b:8 * b + 8, :]).then_inc(s["tables_loaded"], 16)
            with sp.Fori(0, NA) as i:
                sp.wait_ge(s["a_v_psum"], START + i)
                sp.dma_start(ctxT_a.rearrange("p a b -> p (a b)"), a["ctxT"][:, ds(i * 256, 256)]).then_inc(s["a_ctx_loaded"], 16)
                sp.wait_ge(s["w0f_loaded"], i * 16 + 16)
                sp.dma_start(w0_raw[:, ds(i * (W0N // NA), W0N // NA)], a["w0"][:, ds(i * (W0N // NA), W0N // NA)]).then_inc(
                    s["w0f_loaded"], 16)
            sp.wait_ge(s["a_loop_done"], 3)
            sp.dma_start(f0["rw_raw"].rearrange("p k m -> p (k m)"), a["rw0"]).then_inc(s["sel0_loaded"], 16)
            sp.wait_ge(s["f0_loop_done"], 2)
            for dst, src in ((q1_raw, "wq1"), (k1_raw, "wk1")):
                sp.dma_start(dst.rearrange("p k n -> p (k n)"), a[src]).then_inc(s["w1_loaded"], 16)
            sp.dma_start(o1_raw.rearrange("p k n -> p (k n)"), a["wo1"]).then_inc(s["o1_loaded"], 16)
            sp.dma_start(v1_raw.rearrange("p k n -> p (k n)"), a["wv1"]).then_inc(s["o1_loaded"], 16)
            sp.dma_start(w1_raw, a["w1"]).then_inc(s["o1_loaded"], 16)
            sp.wait_ge(s["n_psum"], H1 // 2)
            sp.wait_ge(s["mask_ready"], 1)
            sp.dma_start(biases.rearrange("a (b k) -> (a b) k", b=B), maskrow[0:B, :]).then_inc(s["biases_stored"], 16)
            sp.wait_ge(s["biases_stored"], 16)
            with sp.Fori(0, NA) as i:
                sp.wait_ge(s["b_scores"], START + i * 4)
                sp.dma_start(ctxT_b.rearrange("p a b -> p (a b)"), a["ctxT"][:, ds(i * 256, 256)]).then_inc(s["b_ctx_loaded"], 16)
                sp.dma_start(mrow_raw[0:1, :], biases[:, ds(i * 256, 256)]).then_inc(s["b_ctx_loaded"], 16)
                sp.wait_ge(s["b_o_psum"], START + i * 8)
                for half in range(2):
                    sp.dma_start(cx_raw[64 * half:64 * half + 64, :, :],
                                 a["ctx"][ds(i * 4, 4), :, :].rearrange("b k c -> k b c")).then_inc(s["b_cx_loaded"], 16)
            sp.wait_ge(s["b_resid"], START + NA * 2)
            sp.dma_start(f1["rw_raw"].rearrange("p k m -> p (k m)"), a["rw1"]).then_inc(s["sel1_loaded"], 16)
            sp.dma_start(f1["wg2"][0:E, :], a["wg2"]).then_inc(s["sel1_loaded"], 16)
            sp.dma_start(f1["bd_raw"][0:KC, :], a["bdown"]).then_inc(s["sel1_loaded"], 16)
            os_ = out.rearrange("(t p) d -> p t d", p=P)
            with sp.Fori(0, NF) as i:
                sp.wait_ge(s["f1_resid"], START + i + 1)
                sp.dma_start(os_[:, ds(i * FT, FT), :], x[:, ds(i * FT, FT), :]).then_inc(s["out_stored"], 16)
            sp.wait_ge(s["out_stored"], 16 * NF)
            for n, v in (("const_loaded", 128), ("tables_loaded", 512), ("w0f_loaded", 16 * NA + 16), ("x_loaded", 64)):
                sp.wait_ge(s[n], v)

        @block.tensor
        def _(pe):
            start(pe, "tensor")

            def split3(dst, lhs, rhs, start, stop):
                (lh, ll), (rh, rl) = lhs, rhs
                pe.matmul(dst, lh, rh, start=start, stop=False, skip_group_check=True)
                pe.matmul(dst, ll, rh, start=False, stop=False, skip_group_check=True)
                return pe.matmul(dst, lh, rl, start=False, stop=stop, skip_group_check=True)

            pe.wait_ge(s["const_loaded"], 128)
            pe.wait_ge(s["w0x_loaded"], 64)
            pe.wait_ge(s["zeros_ready"], 2)
            NS = 8

            def turn_x(i):
                pe.wait_ge(s["a_xn_ready"], START + i + 1)
                pe.wait_ge(s["a_v_ready"], START + i * 4)
                trb = bank[6][:, :].rearrange("p (k t c) -> p k t c", k=KT, t=2)
                for t in range(2):
                    for k in range(KT):
                        m = pe.transpose(trb[:, k, t, :], xn_a[:, t, k * P:(k + 1) * P], ident)
                m.then_inc(s["a_xnT_psum"], 1)

            def queries(i):
                pe.wait_ge(s["a_xnT_ready"], START + i + 1)
                pe.wait_ge(s["a_q_read"], START + i)
                qb = bank[7][:, :].rearrange("p (g t k) -> p g t k", g=HG, t=2)
                for b in range(2):
                    for g in range(HG):
                        for k in range(KT):
                            m = pe.matmul(qb[64 * b:64 * b + 64, g], wq0[:, k, 64 * g:64 * g + 64],
                                          xnT_a[:, k, :, 64 * b:64 * b + 64], start=(k == 0), stop=(k == KT - 1))
                m.then_inc(s["a_q_psum"], 1)

            def keys(i):
                pe.wait_ge(s["a_ctx_loaded"], i * 16 + 16)
                pe.wait_ge(s["a_xnT_ready"], START + i + 1)
                kb = bank[6][:, :].rearrange("p (g t k) -> p g t k", g=HG, t=2)
                for b in range(2):
                    for g in range(HG):
                        m = pe.matmul(kb[64 * b:64 * b + 64, g], wk0[:, 64 * g:64 * g + 64], ctxT_a[:, :, 64 * b:64 * b + 64],
                                      start=True, stop=True)
                m.then_inc(s["a_k_psum"], 1)

            def values(i):
                pe.wait_ge(s["a_k_read"], START + i + 1)
                vb = bank[6][:, :].rearrange("p (b n) -> p b n", b=4)
                for par in range(2):
                    for b in range(4):
                        m = pe.matmul(vb[64 * par:64 * par + 64, b], ctxT_a[:, b // 2, 64 * (b % 2):64 * (b % 2) + 64],
                                      wv0[:, par, :], start=True, stop=True)
                m.then_inc(s["a_v_psum"], 1)

            def scores0(i, n):
                pe.wait_ge(s["a_khd_ready"], START + i * NS + n + 1)
                if n == 0:
                    pe.wait_ge(s["a_q_ready"], START + i + 1)
                pe.wait_ge(s["a_centred"], START + i * NS + n - 1)
                pe.matmul(bank[n % 2][:, :], q_bd[:, n % 4, n // 4].rearrange("p b q -> p (b q)"),
                          k_hd[n % NK].rearrange("p h k -> p (h k)"), start=True, stop=True).then_inc(s["a_scores"], 1)

            def turn_probs(i, n):
                pe.wait_ge(s["a_probs"], START + i * NS + n + 1)
                pe.wait_ge(s["a_pT_ready"], START + i * NS + n - 1)
                for j in range(4):
                    m = pe.transpose(bank[2 + n % 2][:, j * P:(j + 1) * P],
                                     probs_a[n % NP].rearrange("p h k -> p (h k)")[:, j * P:(j + 1) * P], ident)
                m.then_inc(s["a_pT_psum"], 1)

            def outputs0(i, n):
                pe.wait_ge(s["a_pT_ready"], START + i * NS + n + 1)
                if n == 0:
                    pe.wait_ge(s["a_v_ready"], START + i * 4 + 4)
                pe.wait_ge(s["a_oT_ready"], START + i * NS + n)
                for j in range(4):
                    m = pe.matmul(bank[4][32 * j:32 * j + 32, 0:P],
                                  v_bd[:, n // 4, 4 * (n % 4) + j].rearrange("p b r d -> p (b r d)"),
                                  pT_a[n % 2][:, j, :], start=True, stop=True)
                m.then_inc(s["a_o_psum"], 1)

            def project0(i, n):
                pe.wait_ge(s["a_oT_ready"], START + i * NS + n + 1)
                if n % 4 == 0:
                    pe.wait_ge(s["a_resid"], START + i * 2 + n // 4)
                m = pe.matmul(bank[5][:, 0:D], oT_a[:, n // 4, n % 4, :], wo0[:, n % 4, :],
                              start=(n % 4 == 0), stop=(n % 4 == 3))
                if n % 4 == 3:
                    m.then_inc(s["a_y_psum"], 1)

            def late(i, t, lag, step, first):
                if t >= lag:
                    step(i, t - lag)
                elif not first:
                    step(i - 1, t - lag + NS)

            def attend0(i, first=False, last=False):
                for t in range(NS + 4 if last else NS):
                    if t < NS:
                        scores0(i, t)
                    for lag, step in ((2, turn_probs), (3, outputs0), (4, project0)):
                        if t - lag < NS:
                            late(i, t, lag, step, first)
                    if not last:
                        if t == 3:
                            turn_x(i + 1)
                        if t == 4:
                            queries(i + 1)
                        if t == 5:
                            keys(i + 1)
                        if t == 7:
                            values(i + 1)

            turn_x(0)
            queries(0)
            keys(0)
            values(0)
            rounds(pe, NA, attend0)
            pe.wait_ge(s["a_resid"], START + NA * 2)
            pe.sem_inc(s["a_loop_done"], 1)

            def ffn(ph, f, chunks, hidden, gate, up, down, rows_last):
                gated = gate is not None
                last = {c: (hidden - c * P if (c + 1) * P > hidden else P) for c in range(chunks)}
                NL = E + 1 if gated else E

                def turn(i, u, k):
                    pe.wait_ge(s[f"{ph}_xn_ready"], START + i + 1)
                    if k == 0:
                        pe.wait_ge(s[f"{ph}_cTl_ready"], START + i)
                    else:
                        pe.wait_ge(s[f"{ph}_xl_ready"], START + i * KT + k)
                    for t in range(FT):
                        m = pe.transpose(bank[6][:, t * P:(t + 1) * P], f["xn"][:, t, k * P:(k + 1) * P], ident)
                    m.then_inc(s[f"{ph}_xnT_psum"], 1)

                def logits(i, u):
                    pe.wait_ge(s[f"{ph}_xh_ready"], START + i * KT + KT)
                    pe.wait_ge(s[f"{ph}_xl_ready"], START + i * KT + KT)
                    for k in range(KT):
                        m = split3(bank[6][0:NL, :], (f["rw_hi"][:, k, 0:NL], f["rw_lo"][:, k, 0:NL]),
                                   (f["xh"][u][:, k, :], f["xl"][u][:, k, :]), k == 0, k == KT - 1)
                    m.then_inc(s[f"{ph}_logit_psum"], 1)

                def logits_back(i, u):
                    pe.wait_ge(s[f"{ph}_logit_copied"], START + i + 1)
                    pe.sem_inc(s["tensor_passed"], 1)
                    for t in range(FT):
                        cols = f["lT"][0:NL, t * P:(t + 1) * P]
                        if gated:
                            m = pe.transpose(bank[6][:, t * 16:t * 16 + NL], cols, ident[0:NL, 0:NL])
                        else:
                            m = pe.matmul(bank[6][:, t * 16:t * 16 + NL], cols, f["wg2"][0:E, :], start=True, stop=True)
                    m.then_inc(s[f"{ph}_logitT_psum"], 1)

                def turn_weights(i, u):
                    pe.wait_ge(s[f"{ph}_comb_ready"], START + i + 1)
                    for t in range(FT):
                        m = pe.transpose(bank[6][0:NL, t * P:(t + 1) * P], f["comb"][:, t, 0:NL], ident)
                    m.then_inc(s[f"{ph}_combT_psum"], 1)

                def gate_up(i, u, c):
                    M = last[c]
                    cols = slice(c * P, c * P + M)
                    pe.wait_ge(s[f"{ph}_silu"], START + i * chunks + c - 1)
                    if gated:
                        pe.wait_ge(s[f"{ph}_act_ready"], START + i * chunks + c - 1)
                    for w, b in ((gate, 0), (up, 2)) if gated else ((up, 0),):
                        for k in range(KT):
                            m = split3(bank[b + c % 2][0:M, :], (w[0][:, k, cols], w[1][:, k, cols]),
                                       (f["xh"][u][:, k, :], f["xl"][u][:, k, :]), k == 0, k == KT - 1)
                    m.then_inc(s[f"{ph}_gu_psum"], 1)

                def spread(i, u, c):
                    if c == 0:
                        pe.wait_ge(s[f"{ph}_cTh_ready"], START + i + 1)
                        pe.wait_ge(s[f"{ph}_cTl_ready"], START + i + 1)
                    pe.wait_ge(s[f"{ph}_scaled"], START + i * chunks + c)
                    M = last[c]
                    pe.sem_inc(s["tensor_passed"], 1)
                    pe.matmul(bank[4][0:M, :], f["sel"][0:KC, c, 0:M], f["cT"][u][0:KC, :],
                              start=True, stop=True, skip_group_check=True).then_inc(s[f"{ph}_cb_psum"], 1)

                def down_part(i, u, c):
                    M = last[c]
                    pe.wait_ge(s[f"{ph}_hh_ready"], START + i * chunks + c + 1)
                    pe.wait_ge(s[f"{ph}_hl_ready"], START + i * chunks + c + 1)
                    if c == 0:
                        pe.wait_ge(s[f"{ph}_resid"], START + i)
                    for t in range(FT):
                        y = bank[5 + 2 * (t // 2)][:, (t % 2) * D:(t % 2 + 1) * D]
                        if c == 0 and not gated:
                            cols = f["cT"][u][0:KC, t * P:(t + 1) * P]
                            pe.matmul(y, cols, f["bd_hi"][0:KC, :], start=(t % 2 == 0), stop=False, skip_group_check=True)
                            pe.matmul(y, cols, f["bd_lo"][0:KC, :], start=False, stop=False, skip_group_check=True)
                        m = split3(y, (f["hh"][c % 3][0:M, t * P:(t + 1) * P], f["hl"][c % 3][0:M, t * P:(t + 1) * P]),
                                   (down[0][0:M, c, :], down[1][0:M, c, :]),
                                   gated and c == 0 and t % 2 == 0, c == chunks - 1)
                    m.then_inc(s[f"{ph}_down_done"], 1)

                def block_(i, u, more):
                    at = SLOTS[ph]
                    for t in range(chunks + 3):
                        if t < chunks:
                            gate_up(i, u, t)
                        if 0 <= t - 1 < chunks:
                            spread(i, u, t - 1)
                        if more:
                            if t == at["t0"]:
                                turn(i + 1, 1 - u, 0)
                            if t == at["t1"]:
                                turn(i + 1, 1 - u, 1)
                            if t == at["logits"]:
                                logits(i + 1, 1 - u)
                            if t == at["back"]:
                                logits_back(i + 1, 1 - u)
                            if t == at["weights"]:
                                turn_weights(i + 1, 1 - u)
                        if 0 <= t - 3 < chunks:
                            down_part(i, u, t - 3)

                turn(0, 0, 0)
                turn(0, 0, 1)
                logits(0, 0)
                logits_back(0, 0)
                turn_weights(0, 0)
                pairs(pe, NF, block_)
                pe.wait_ge(s[f"{ph}_resid"], START + NF)
                pe.sem_inc(s[f"{ph}_loop_done"], 1)

            pe.wait_ge(s["sel0_cast"], 16)
            pe.wait_ge(s["rw_split"], 1)
            hi, lo = ffn0_view(w0_hi), ffn0_view(w0_lo)
            ffn("f0", f0, NC0, HID0, (hi[0], lo[0]), (hi[1], lo[1]), (hi[2], lo[2]), None)

            pe.wait_ge(s["w1_loaded"], 32)
            for h in range(H1):
                if h >= 2:
                    pe.wait_ge(s["m_copied"], h - 1)
                for k in range(KT):
                    m = pe.matmul(bank[h % 2][:, k * P:(k + 1) * P], q1_raw[:, h, k * P:(k + 1) * P], k1_raw[:, h // 2, :],
                                  start=True, stop=True)
                m.then_inc(s["m_psum"], 1)
            pe.wait_ge(s["o1_loaded"], 48)
            for c in range(H1 // 2):
                if c >= 2:
                    pe.wait_ge(s["n_copied"], c - 1)
                for u in range(2):
                    m = pe.matmul(bank[2 + c % 2][:, u * D:(u + 1) * D], v1_raw[:, c, :], o1_raw[:, 2 * c + u, :],
                                  start=True, stop=True)
                m.then_inc(s["n_psum"], 1)
            pe.wait_ge(s["mask_ready"], 1)
            pe.wait_ge(s["m_copied"], H1)
            pe.matmul(bank[0][:, 0:B], valid[0:B, :], ident[0:B, 0:B], start=True, stop=True).then_inc(s["valid_psum"], 1)
            pe.wait_ge(s["valid_ready"], 1)
            pe.wait_ge(s["n_copied"], H1 // 2)
            pe.wait_ge(s["ones_ready"], 1)
            NB = 4

            def turn_x1(i, first=False):
                pe.wait_ge(s["b_xn_ready"], START + i + 1)
                if not first:
                    pe.wait_ge(s["b_pTh"], START + (i - 1) * NB)
                    pe.wait_ge(s["b_pTl"], START + (i - 1) * NB)
                trb = bank[2][:, :].rearrange("p (k t c) -> p k t c", k=KT, t=2)
                for t in range(2):
                    for k in range(KT):
                        m = pe.transpose(trb[:, k, t, :], xn_b[:, t, k * P:(k + 1) * P], ident)
                m.then_inc(s["b_xnT_psum"], 1)

            def queries1(i, c):
                if c == 0:
                    pe.wait_ge(s["b_xh_ready"], START + i + 1)
                    pe.wait_ge(s["b_xl_ready"], START + i + 1)
                pe.wait_ge(s["b_q_ready"], START + i * 8 + c - 1)
                for u in range(2):
                    for k in range(KT):
                        m = split3(bank[6 + c % 2][:, u * 256:(u + 1) * 256], (m_hi[:, 2 * c + u, k, :], m_lo[:, 2 * c + u, k, :]),
                                   (xh_b[:, k, :], xl_b[:, k, :]), u == 0 and k == 0, k == KT - 1)
                m.then_inc(s["b_q_psum"], 1)

            def scores1(i, b):
                if b == 0:
                    pe.wait_ge(s["b_mrow"], START + i + 1)
                    pe.wait_ge(s["b_q_ready"], START + i * 8 + 8)
                    pe.wait_ge(s["b_ctx_loaded"], i * 32 + 32)
                pe.wait_ge(s["b_centred"], START + i * NB + b - 1)
                pe.matmul(bank[b % 2][:, :].rearrange("p (g k) -> p g k", g=G1), ones[0:1, :],
                          mrow[0:1, b * S:(b + 1) * S].unsqueeze(1).broadcast_to([1, G1, S]),
                          start=True, stop=False, skip_group_check=True)
                for g in range(G1):
                    m = pe.matmul(bank[b % 2][:, g * S:(g + 1) * S], qT[:, b, 2 * g:2 * g + 2, :].rearrange("p h q -> p (h q)"),
                                  ctxT_b[:, b, :], start=False, stop=(g == G1 - 1), skip_group_check=True)
                m.then_inc(s["b_scores"], 1)

            def turn_probs1(i, b):
                pe.wait_ge(s["b_probs"], START + i * NB + b + 1)
                if b == 0:
                    pe.wait_ge(s["b_xh_ready"], START + i + 1)
                    pe.wait_ge(s["b_xl_ready"], START + i + 1)
                pe.wait_ge(s["b_pTh"], START + i * NB + b)
                pe.wait_ge(s["b_pTl"], START + i * NB + b)
                for j in range(4):
                    m = pe.transpose(bank[2][:, j * P:(j + 1) * P],
                                     probs_b[b].rearrange("p g k -> p (g k)")[:, j * P:(j + 1) * P], ident)
                m.then_inc(s["b_pT_psum"], 1)

            def outputs1(i, b):
                pe.wait_ge(s["b_pTh"], START + i * NB + b + 1)
                pe.wait_ge(s["b_pTl"], START + i * NB + b + 1)
                if b == 0:
                    pe.wait_ge(s["b_cxh"], START + i + 1)
                    pe.wait_ge(s["b_cxl"], START + i + 1)
                for par in range(2):
                    pe.wait_ge(s["b_oTh"], START + i * NB * 2 + 2 * b - 1 + par)
                    pe.wait_ge(s["b_oTl"], START + i * NB * 2 + 2 * b - 1 + par)
                    rows = slice(64 * par, 64 * par + 64)
                    split3(bank[4 + par][:, :], (cx_hi[rows, b, :], cx_lo[rows, b, :]), (pTh[rows, :], pTl[rows, :]),
                           True, True).then_inc(s["b_o_psum"], 1)

            def project1(i, t, half):
                if half == 0:
                    pe.wait_ge(s["b_oTh"], START + i * NB * 2 + 4 * t + 4)
                    pe.wait_ge(s["b_oTl"], START + i * NB * 2 + 4 * t + 4)
                    pe.wait_ge(s["b_resid"], START + i * 2 + t)
                for h in range(8 * half, 8 * half + 8):
                    j, par, u = h // 4, (h // 2) % 2, h % 2
                    m = split3(bank[3][:, 0:D], (oTh[:, t, j, par, u, :], oTl[:, t, j, par, u, :]),
                               (n_hi[:, h, :], n_lo[:, h, :]), h == 0, h == H1 - 1)
                if half == 1:
                    m.then_inc(s["b_y_psum"], 1)

            def attend1(i, first=False, last=False):
                scores1(i, 0)
                scores1(i, 1)
                if not first:
                    project1(i - 1, 1, 0)
                scores1(i, 2)
                if not first:
                    project1(i - 1, 1, 1)
                scores1(i, 3)
                if not last:
                    turn_x1(i + 1)

                def next_queries(*cs):
                    if not last:
                        for c in cs:
                            queries1(i + 1, c)

                next_queries(0, 1)
                turn_probs1(i, 0)
                next_queries(2)
                outputs1(i, 0)
                next_queries(3)
                turn_probs1(i, 1)
                next_queries(4)
                outputs1(i, 1)
                turn_probs1(i, 2)
                next_queries(5)
                project1(i, 0, 0)
                outputs1(i, 2)
                turn_probs1(i, 3)
                project1(i, 0, 1)
                next_queries(6, 7)
                outputs1(i, 3)

            turn_x1(0, first=True)
            for c in range(H1 // 2):
                queries1(0, c)
            rounds(pe, NA, attend1)
            project1(NA - 1, 1, 0)
            project1(NA - 1, 1, 1)
            pe.wait_ge(s["b_resid"], START + NA * 2)
            pe.wait_ge(s["sel1_cast"], 16)
            pe.wait_ge(s["sel1_loaded"], 48)
            pe.wait_ge(s["rw_split"], 2)
            pe.wait_ge(s["w1_split"], 1)
            hi, lo = ffn1_view(w1_hi), ffn1_view(w1_lo)
            ffn("f1", f1, NC1, HID1, None, (hi[0], lo[0]), (hi[1], lo[1]), None)

        @block.scalar
        def _(act):
            start(act, "scalar")
            act.wait_ge(s["const_loaded"], 128)
            act.activation(gates, gates, ACT.Tanh).then_inc(s["gates_ready"], 1)
            for n in range(2):
                act.wait_ge(s["trig_wanted"], n + 1)
                act.activation(trig[:, 256 * n:256 * n + 256], ang[:, 256 * n:256 * n + 256], ACT.Sin).then_inc(s["trig_ready"], 1)

            def root(n):
                act.wait_ge(s["sd_wanted"], n + 1)
                act.activation(sd, sd, ACT.Sqrt).then_inc(s["sd_ready"], 1)

            root(0)
            NS = 8
            SCALE0 = float(HD0) ** -0.5
            act.wait_ge(s["zeros_ready"], 2)
            WS = W0N // NA

            def xT_copy(i):
                act.wait_ge(s["a_xnT_psum"], START + i + 1)
                act.wait_ge(s["a_q_psum"], START + i)
                act.activation(xnT_a.rearrange("p k t c -> p (k t c)"), bank[6][:, :], ACT.Copy).then_inc(s["a_xnT_ready"], 1)

            def v_copy(i):
                act.wait_ge(s["a_v_psum"], START + i + 1)
                act.wait_ge(s["a_o_psum"], START + i * NS)
                vb = bank[6][:, :].rearrange("p (t b j d) -> p t b j d", t=2, b=2, j=16)
                for par in range(2):
                    for t in range(2):
                        rows = slice(64 * par, 64 * par + 64)
                        act.activation(v_bd[rows, t, :, :, par, :].rearrange("p j b d -> p b j d"), vb[rows, t],
                                       ACT.Copy).then_inc(s["a_v_ready"], 1)

            def pT_copy(i, n):
                act.wait_ge(s["a_pT_psum"], START + i * NS + n + 1)
                act.wait_ge(s["a_o_psum"], START + i * NS + n - 1)
                act.activation(pT_a[n % 2].rearrange("p j c -> p (j c)"), bank[2 + n % 2][:, :], ACT.Copy).then_inc(
                    s["a_pT_ready"], 1)

            def attend0(i, first=False, last=False):
                for t in range(NS + 2 if last else NS):
                    if t < NS:
                        act.wait_ge(s["a_centred"], START + i * NS + t + 1)
                        act.activation(probs_a[t % NP], probs_a[t % NP], ACT.Exp, scale=SCALE0).then_inc(s["a_exp"], 1)
                    if t >= 2:
                        pT_copy(i, t - 2)
                    elif not first:
                        pT_copy(i - 1, t - 2 + NS)
                    if t == 2:
                        v_copy(i)
                    if t == 3 and not last:
                        xT_copy(i + 1)
                    if t == 5:
                        act.wait_ge(s["w0f_loaded"], i * 16 + 32)
                        act.activation(w0_hi[:, ds(i * WS, WS)], w0_raw[:, ds(i * WS, WS)], ACT.Copy).then_inc(s["w0_hi"], 1)

            xT_copy(0)
            rounds(act, NA, attend0)

            def ffn(ph, f, chunks, hidden, gated):
                last = {c: (hidden - c * P if (c + 1) * P > hidden else P) for c in range(chunks)}
                NL = E + 1 if gated else E

                def xT_high(i, u, k):
                    act.wait_ge(s[f"{ph}_xnT_psum"], START + i * KT + k + 1)
                    act.activation(f["xh"][u][:, k, :], bank[6][:, :], ACT.Copy).then_inc(s[f"{ph}_xh_ready"], 1)

                def logits_copy(i, u):
                    act.wait_ge(s[f"{ph}_logit_psum"], START + i + 1)
                    act.activation(f["lT"][0:NL, :], bank[6][0:NL, :], ACT.Copy if gated else ACT.Tanh).then_inc(
                        s[f"{ph}_logit_copied"], 1)

                def halves(i, u):
                    act.wait_ge(s[f"{ph}_delta_ready"], START + i + 1)
                    act.activation(f["ed"], f["dl"], ACT.Tanh, scale=0.5).then_inc(s[f"{ph}_exp_ready"], 1)

                def weights_high(i, u):
                    act.wait_ge(s[f"{ph}_combT_psum"], START + i + 1)
                    act.activation(f["cT"][u][0:NL, :], bank[6][0:NL, :], ACT.Copy).then_inc(s[f"{ph}_cTh_ready"], 1)

                def silu(i, c):
                    M = last[c]
                    act.wait_ge(s[f"{ph}_gu_psum"], START + i * chunks + c + 1)
                    act.wait_ge(s[f"{ph}_act_ready" if gated else f"{ph}_scaled"], START + i * chunks + c - 1)
                    act.activation(f["s"][c % 2][0:M, :], bank[c % 2][0:M, :], ACT.Silu,
                                   **({} if gated else {"bias": bup[:, c:c + 1]})).then_inc(s[f"{ph}_silu"], 1)

                def high(i, c):
                    M = last[c]
                    act.wait_ge(s[f"{ph}_scaled"], START + i * chunks + c + 1)
                    act.wait_ge(s[f"{ph}_down_done"], START + i * chunks + (c - 2 if c >= 3 else 0))
                    act.activation(f["hh"][c % 3][0:M, :], f["act"][c % 3][0:M, :], ACT.Copy).then_inc(
                        s[f"{ph}_hh_ready"], 1)

                def block_(i, u, more):
                    at = SLOTS[ph]
                    for t in range(chunks + 1):
                        if t < chunks:
                            silu(i, t)
                        if t >= 1:
                            high(i, t - 1)
                        if more:
                            if t == at["t0"]:
                                xT_high(i + 1, 1 - u, 0)
                            if t == at["t1"]:
                                xT_high(i + 1, 1 - u, 1)
                            if t == at["logits"]:
                                logits_copy(i + 1, 1 - u)
                            if t == at["back"]:
                                halves(i + 1, 1 - u)
                            if t == at["weights"]:
                                weights_high(i + 1, 1 - u)

                xT_high(0, 0, 0)
                xT_high(0, 0, 1)
                logits_copy(0, 0)
                halves(0, 0)
                weights_high(0, 0)
                pairs(act, NF, block_)

            root(1)
            ffn("f0", f0, NC0, HID0, True)
            root(2)
            for h in range(H1):
                act.wait_ge(s["m_psum"], h + 1)
                act.activation(m_hi[:, h].rearrange("p k c -> p (k c)"), bank[h % 2][:, 0:256], ACT.Copy).then_inc(
                    s["scalar_steps"], 1)
            for c in range(H1 // 2):
                act.wait_ge(s["n_psum"], c + 1)
                act.activation(n_hi[:, 2 * c:2 * c + 2, :].rearrange("p u n -> p (u n)"), bank[2 + c % 2][:, :],
                               ACT.Copy).then_inc(s["scalar_steps"], 1)
            NB = 4
            SCALE1 = float(CD) ** -0.5

            def xT_high1(i):
                act.wait_ge(s["b_xnT_psum"], START + i + 1)
                act.wait_ge(s["b_q_psum"], START + i * 8)
                act.activation(xh_b.rearrange("p k t -> p (k t)"), bank[2][:, :], ACT.Copy).then_inc(s["b_xh_ready"], 1)

            def q_copy(i, c):
                act.wait_ge(s["b_q_psum"], START + i * 8 + c + 1)
                act.wait_ge(s["b_scores"], START + i * NB)
                act.activation(qT[:, :, 2 * c:2 * c + 2, :].rearrange("p b h q -> p h b q"),
                               bank[6 + c % 2][:, :].rearrange("p (h b q) -> p h b q", h=2, b=4), ACT.Copy).then_inc(
                    s["b_q_ready"], 1)

            def attend1(i, first=False, last=False):
                def expo(b):
                    act.wait_ge(s["b_centred"], START + i * NB + b + 1)
                    act.activation(probs_b[b], probs_b[b], ACT.Exp, scale=SCALE1).then_inc(s["b_exp"], 1)

                def pth(b):
                    act.wait_ge(s["b_pT_psum"], START + i * NB + b + 1)
                    act.wait_ge(s["b_o_psum"], START + i * NB * 2 + 2 * b)
                    act.activation(pTh, bank[2][:, :], ACT.Copy).then_inc(s["b_pTh"], 1)

                def oth(b):
                    if b % 2 == 0:
                        act.wait_ge(s["b_y_psum"], START + i * 2 + b // 2)
                    for par in range(2):
                        act.wait_ge(s["b_o_psum"], START + i * NB * 2 + 2 * b + par + 1)
                        act.activation(oTh[:, b // 2, :, par, :, (b % 2) * S:(b % 2 + 1) * S],
                                       bank[4 + par][:, :].rearrange("p (j u q) -> p j u q", j=4, u=2), ACT.Copy).then_inc(
                            s["b_oTh"], 1)

                def next_q(*cs):
                    if not last:
                        for c in cs:
                            q_copy(i + 1, c)

                expo(0)
                expo(1)
                act.wait_ge(s["b_cx_loaded"], i * 32 + 32)
                act.wait_ge(s["b_o_psum"], START + i * 8)
                act.activation(cx_hi, cx_raw, ACT.Copy).then_inc(s["b_cxh"], 1)
                expo(2)
                expo(3)
                if not last:
                    xT_high1(i + 1)
                next_q(0, 1)
                pth(0)
                next_q(2)
                oth(0)
                next_q(3)
                pth(1)
                next_q(4)
                oth(1)
                pth(2)
                next_q(5)
                oth(2)
                pth(3)
                next_q(6, 7)
                oth(3)

            xT_high1(0)
            for c in range(H1 // 2):
                q_copy(0, c)
            rounds(act, NA, attend1)
            root(3)
            ffn("f1", f1, NC1, HID1, False)

        @block.gpsimd
        def _(pool):
            start(pool, "gpsimd")
            pool.memset(v_bd, 0.0).then_inc(s["zeros_ready"], 1)
            pool.wait_ge(s["const_loaded"], 128)
            NS = 8

            def heads(i, n):
                if n == 0:
                    pool.wait_ge(s["a_k_ready"], START + i + 1)
                pool.wait_ge(s["a_scores"], START + i * NS + n - NK + 1)
                pool.tensor_tensor(k_hd[n % NK], k_rot[:, n % 4, n // 4, :].unsqueeze(1).broadcast_to([P, E, S]),
                                   headmask.unsqueeze(2).broadcast_to([P, E, S]), ALU.mult).then_inc(s["a_khd_ready"], 1)

            def bias(i):
                pool.wait_ge(s["a_xn_ready"], START + i + 1)
                pool.tensor_tensor(x[:, ds(i * 2, 2), :], x[:, ds(i * 2, 2), :],
                                   gbout.unsqueeze(1).broadcast_to([P, 2, D]), ALU.add).then_inc(s["a_bias"], 1)

            def attend0(i, first=False, last=False):
                for n in range(NS):
                    pool.wait_ge(s["a_recip"], START + i * NS + n + 1)
                    pool.tensor_tensor(probs_a[n % NP], probs_a[n % NP], rs_a[:, n % 4, :].unsqueeze(2).broadcast_to([P, E, S]),
                                       ALU.mult).then_inc(s["a_probs"], 1)
                    if n + NK < NS:
                        heads(i, n + NK)
                    elif not last:
                        heads(i + 1, n + NK - NS)
                    if n == 1 and not last:
                        bias(i + 1)

            pool.wait_ge(s["gbout_ready"], 1)
            for n in range(NK):
                heads(0, n)
            bias(0)
            rounds(pool, NA, attend0)
            pool.sem_inc(s["a_loop_done"], 1)
            pool.wait_ge(s["a_loop_done"], 3)
            pool.dma_start(f0["sel"][0:KC].rearrange("p c m -> p (c m)"), a["sel0"]).then_inc(s["sel0_cast"], 16)
            NB = 4
            with pool.Fori(0, NA) as i:
                for b in range(NB):
                    pool.wait_ge(s["b_recip"], START + i * NB + b + 1)
                    pool.tensor_tensor(probs_b[b], probs_b[b], rs_b[:, b, :].unsqueeze(2).broadcast_to([P, G1, S]),
                                       ALU.mult).then_inc(s["b_probs"], 1)
            pool.wait_ge(s["b_resid"], START + NA * 2)
            pool.dma_start(f1["sel"][0:KC].rearrange("p c m -> p (c m)"), a["sel1"]).then_inc(s["sel1_cast"], 16)

        @block.vector
        def _(ve):
            start(ve, "vector")
            st = Steps(ve, s["vector_steps"])

            TWO_PI, PI = float(2 * np.pi), 3.14159250
            ROUND = 1.5 * 2.0 ** 23
            ve.wait_ge(s["pos_loaded"], 16)
            ve.wait_ge(s["const_loaded"], 128)
            for n in range(2):
                w = slice(256 * n, 256 * n + 256)
                st.done(ve.tensor_scalar(ang[:, w], pos, tiny[:, n:n + 1], tiny[:, 2 + n:3 + n], ALU.mult, ALU.add))
                st.wait()
                st.done(ve.tensor_scalar(turn[:, w], ang[:, w], 1.0 / TWO_PI, ROUND, ALU.mult, ALU.add))
                st.wait()
                st.done(ve.tensor_scalar(turn[:, w], turn[:, w], ROUND, -TWO_PI, ALU.subtract, ALU.mult))
                st.wait()
                st.done(ve.tensor_tensor(ang[:, w], ang[:, w], turn[:, w], ALU.add))
                st.wait()
                ve.tensor_scalar(ang[:, w], ang[:, w], PI, -PI, ALU.min, ALU.max).then_inc(s["trig_wanted"], 1)
            ve.memset(q_bd, 0.0).then_inc(s["zeros_ready"], 1)
            ve.wait_ge(s["gates_ready"], 1)
            ve.tensor_scalar(gbout, gbout, gates[:, 0:1], None, ALU.mult).then_inc(s["gbout_ready"], 1)

            for n in range(4):
                ve.wait_ge(s["x_loaded"], 64)
                for t in range(8 * n, 8 * n + 8):
                    st.done(ve.bn_stats(bn[:, t % 8, :], x[:, t, :]))
                st.wait()
                for t in range(8 * n, 8 * n + 8):
                    st.done(ve.bn_aggr(mv[:, t, :], bn[:, t % 8, :]))
                st.wait()

            def moments(tile, count):
                for t in range(count):
                    st.done(ve.bn_stats(bn[:, t, :],
                                        x[:, ds(tile + t, 1), :].rearrange("p a d -> p (a d)")))
                st.wait()
                ve.sem_inc(s["vector_passed"], 1)
                for t in range(count):
                    st.done(ve.bn_aggr(mv_new[:, t, :], bn[:, t, :]))
                st.wait()
                st.done(ve.tensor_copy(mv[:, ds(tile, count), :], mv_new[:, 0:count, :]))

            def stats(n):
                ve.tensor_scalar(sd, mv[:, :, 1], LN_EPS, None, ALU.add).then_inc(s["sd_wanted"], 1)
                ve.wait_ge(s["sd_ready"], n + 1)
                st.done(ve.reciprocal(rstd, sd))
                st.wait()
                st.done(ve.scalar_tensor_tensor(out=nmr, in0=mv[:, :, 0], scalar=-1.0, in1=rstd, op0=ALU.mult, op1=ALU.mult))
                st.wait()

            def normalise(dst, tile):
                return ve.tensor_scalar(dst, x[:, ds(tile, 1), :], rstd[:, ds(tile, 1)], nmr[:, ds(tile, 1)], ALU.mult, ALU.add)

            stats(0)
            NS = 8
            WS = W0N // NA

            def norm0(i):
                ve.wait_ge(s["a_xnT_psum"], START + i)
                st.done(normalise(xn_a[:, 0:1, :], i * 2))
                st.done(normalise(xn_a[:, 1:2, :], i * 2 + 1))
                st.wait()
                ve.sem_inc(s["a_xn_ready"], 1)

            def rope(i, src, psum, here, swapped, read):
                ve.wait_ge(s[psum], START + i + 1)
                ve.sem_inc(s["vector_passed"], 1)
                st.done(ve.stream_shuffle(swapped.rearrange("p g t k -> p (g t k)"), src[:, :], [j ^ 1 for j in range(32)]))
                sv = src[:, :].rearrange("p (g t k) -> p g (t k)", g=HG, t=2)
                c, sn = (w[:, ds(i * 2, 2), :].rearrange("p t k -> p (t k)").unsqueeze(1).broadcast_to([P, HG, 2 * S])
                         for w in (cosT, sinT))
                hv, wv = (w.rearrange("p g t k -> p g (t k)") for w in (here, swapped))
                ve.tensor_tensor(hv, sv, c, ALU.mult).then_inc(s[read], 1)
                st.wait()
                st.done(ve.tensor_tensor(wv, wv, sn, ALU.mult))

            def keys(i):
                ve.wait_ge(s["a_khd_ready"], START + i * NS)
                rope(i, bank[6], "a_k_psum", k_rot, kw_a, "a_k_read")
                st.wait()
                ve.wait_ge(s["a_k_read"], START + i + 1)
                ve.tensor_tensor(k_rot, k_rot, kw_a, ALU.add).then_inc(s["a_k_ready"], 1)

            def queries_in(i):
                ve.wait_ge(s["a_scores"], START + i * NS)
                ve.wait_ge(s["a_q_read"], START + i + 1)
                st.wait()
                for b in range(2):
                    rows = slice(64 * b, 64 * b + 64)
                    m = ve.tensor_tensor(q_bd[rows, :, :, b, :], qs_a[rows], qw_a[rows], ALU.add)
                    if b == 0:
                        st.done(m)
                m.then_inc(s["a_q_ready"], 1)

            def centre0(i, n):
                ve.wait_ge(s["a_scores"], START + i * NS + n + 1)
                sc = bank[n % 2][:, :].rearrange("p (h k) -> p h k", h=E)
                st.done(ve.tensor_reduce(rm_a[:, n % 2, :], sc, AX_X, ALU.max))
                ve.wait_ge(s["a_pT_psum"], START + i * NS + n - NP + 1)
                st.wait()
                ve.tensor_tensor(probs_a[n % NP], sc, rm_a[:, n % 2, :].unsqueeze(2).broadcast_to([P, E, S]),
                                 ALU.subtract).then_inc(s["a_centred"], 1)

            def weigh0(i, n):
                ve.wait_ge(s["a_exp"], START + i * NS + n + 1)
                st.done(ve.tensor_reduce(rs_a[:, n % 4, :], probs_a[n % NP], AX_X, ALU.add))
                st.wait()
                ve.reciprocal(rs_a[:, n % 4, :], rs_a[:, n % 4, :]).then_inc(s["a_recip"], 1)

            def own0(i, n):
                ve.wait_ge(s["a_o_psum"], START + i * NS + n + 1)
                ve.tensor_tensor(oT_a[:, n // 4, n % 4, :], bank[4][:, 0:P], ownbatch, ALU.mult).then_inc(s["a_oT_ready"], 1)

            def resid0(i, n):
                if n % 4 != 3:
                    return
                u = n // 4
                ve.wait_ge(s["a_bias"], START + i + 1)
                ve.wait_ge(s["a_y_psum"], START + i * 2 + u + 1)
                xt = x[:, ds(i * 2 + u, 1), :].rearrange("p a d -> p (a d)")
                st.done(ve.scalar_tensor_tensor(out=xt, in0=bank[5][:, 0:D], scalar=gates[:, 0:1], in1=xt,
                                                op0=ALU.mult, op1=ALU.add))
                st.wait()
                ve.sem_inc(s["a_resid"], 1)
                moments(i * 2 + u, 1)

            def late(i, t, lag, step, first):
                if t >= lag:
                    step(i, t - lag)
                elif not first:
                    step(i - 1, t - lag + NS)

            def attend0(i, first=False, last=False):
                queries_in(i)
                for t in range(NS + 5 if last else NS):
                    if t < NS:
                        centre0(i, t)
                    for lag, step in ((1, weigh0), (3, own0), (4, resid0)):
                        if t - lag < NS:
                            late(i, t, lag, step, first)
                    if not last:
                        if t == 0:
                            norm0(i + 1)
                        if t == 5:
                            rope(i + 1, bank[7], "a_q_psum", qs_a, qw_a, "a_q_read")
                        if t == 6:
                            keys(i + 1)
                    if t == 7:
                        ve.wait_ge(s["w0_hi"], START + i + 1)
                        st.done(ve.tensor_tensor(w0_lo[:, ds(i * WS, WS)], w0_raw[:, ds(i * WS, WS)],
                                                 w0_hi[:, ds(i * WS, WS)], ALU.subtract))

            norm0(0)
            ve.wait_ge(s["tables_loaded"], 512)
            rope(0, bank[7], "a_q_psum", qs_a, qw_a, "a_q_read")
            keys(0)
            attend0(0, first=True)
            with ve.Fori(1, NA - 1) as i:
                st.loop(i, STEPS["a"], 1)
                attend0(i)
            st.end(NA - 1)
            attend0(NA - 1, last=True)
            st.wait()
            ve.sem_inc(s["a_loop_done"], 1)

            def split_router(f, n, loads, bias):
                ve.wait_ge(s[f"sel{n}_loaded"], loads)
                parts = [tuple(f[f"rw_{k}"] for k in ("hi", "lo", "raw"))]
                if bias:
                    parts.append(tuple(f[f"bd_{k}"][0:KC] for k in ("hi", "lo", "raw")))
                for hi, lo, raw in parts:
                    st.done(ve.tensor_copy(hi, raw))
                st.done(ve.memset(f["lT"][0:64, :], 0.0))
                st.wait()
                for hi, lo, raw in parts:
                    st.done(ve.tensor_tensor(lo, raw, hi, ALU.subtract))
                for cT in f["cT"]:
                    st.done(ve.tensor_copy(cT[0:64, :], f["lT"][0:64, :]))
                st.wait()
                ve.sem_inc(s["rw_split"], 1)

            def ffn(ph, f, chunks, hidden, gated, gate, out_stats):
                last = {c: (hidden - c * P if (c + 1) * P > hidden else P) for c in range(chunks)}
                NL = E + 1 if gated else E

                def norm(i, u):
                    ve.wait_ge(s[f"{ph}_xnT_psum"], START + i * KT)
                    for t in range(FT):
                        st.done(normalise(f["xn"][:, t:t + 1, :], i * FT + t))
                    st.wait()
                    ve.sem_inc(s[f"{ph}_xn_ready"], 1)

                def xT_low(i, u, k):
                    ve.wait_ge(s[f"{ph}_xh_ready"], START + i * KT + k + 1)
                    ve.tensor_tensor(f["xl"][u][:, k, :], bank[6][:, :], f["xh"][u][:, k, :], ALU.subtract).then_inc(
                        s[f"{ph}_xl_ready"], 1)

                def largest(i, u):
                    ve.wait_ge(s[f"{ph}_logitT_psum"], START + i + 1)
                    st.done(ve.tensor_copy(f["lg"][:, :, 0:NL], bank[6][:, 0:64].rearrange("p (t n) -> p t n", n=16)[:, :, 0:NL]))
                    st.wait()
                    ve.sem_inc(s["vector_passed"], 1)
                    for t in range(FT):
                        st.done(ve.max(f["m8"][:, t, :], f["lg"][:, t, 0:E]))
                    st.wait()
                    ve.sem_inc(s["vector_passed"], 1)
                    for t in range(FT):
                        st.done(ve.max_index(f["ix"][:, t, :].bitcast(U32), f["m8"][:, t, :], f["lg"][:, t, 0:E]))
                    st.done(ve.tensor_tensor(f["dl"][:, :, 0], f["m8"][:, :, 0], f["m8"][:, :, 1], ALU.subtract))
                    if gated:
                        st.done(ve.tensor_copy(f["dl"][:, :, 1], f["lg"][:, :, E]))
                    else:
                        st.done(ve.memset(f["dl"][:, :, 1], 0.0))
                    st.wait()
                    ve.sem_inc(s[f"{ph}_delta_ready"], 1)
                    st.done(ve.tensor_copy(f["ixf"], f["ix"][:, :, 0:2].bitcast(U32)))

                def weights(i, u):
                    ve.wait_ge(s[f"{ph}_exp_ready"], START + i + 1)
                    st.done(ve.tensor_scalar(f["wt"], f["ed"], 0.5, 0.5, ALU.mult, ALU.add))
                    st.done(ve.tensor_scalar(f["w2"], f["ed"][:, :, 0:1], -0.5, 0.5, ALU.mult, ALU.add))
                    st.wait()
                    if gated:
                        st.done(ve.tensor_copy(f["comb"][:, :, E], f["wt"][:, :, 1]))
                    for t in range(FT):
                        st.done(ve.tensor_scalar(f["comb"][:, t, 0:E], iota8, f["ixf"][:, t, 0:1], f["wt"][:, t, 0:1],
                                                 ALU.is_equal, ALU.mult))
                        st.done(ve.tensor_scalar(f["c2"][:, t, :], iota8, f["ixf"][:, t, 1:2], f["w2"][:, t, 0:1],
                                                 ALU.is_equal, ALU.mult))
                    st.wait()
                    st.done(ve.tensor_tensor(f["comb"][:, :, 0:E], f["comb"][:, :, 0:E], f["c2"], ALU.add))
                    st.wait()
                    ve.sem_inc(s[f"{ph}_comb_ready"], 1)

                def weights_low(i, u):
                    ve.wait_ge(s[f"{ph}_cTh_ready"], START + i + 1)
                    ve.tensor_tensor(f["cT"][u][LOW:LOW + NL, :], bank[6][0:NL, :], f["cT"][u][0:NL, :],
                                     ALU.subtract).then_inc(s[f"{ph}_cTl_ready"], 1)

                def product(i, c):
                    if not gated:
                        return
                    M = last[c]
                    if c >= 3:
                        ve.wait_ge(s[f"{ph}_hl_ready"], START + i * chunks + c - 2)
                    ve.wait_ge(s[f"{ph}_silu"], START + i * chunks + c + 1)
                    ve.tensor_tensor(f["act"][c % 3][0:M, :], bank[2 + c % 2][0:M, :], f["s"][c % 2][0:M, :],
                                     ALU.mult).then_inc(s[f"{ph}_act_ready"], 1)

                def scaled(i, c):
                    M = last[c]
                    ve.wait_ge(s[f"{ph}_cb_psum"], START + i * chunks + c + 1)
                    if gated:
                        ve.wait_ge(s[f"{ph}_act_ready"], START + i * chunks + c + 1)
                        other = f["act"][c % 3]
                    else:
                        if c >= 3:
                            ve.wait_ge(s[f"{ph}_hl_ready"], START + i * chunks + c - 2)
                        ve.wait_ge(s[f"{ph}_silu"], START + i * chunks + c + 1)
                        other = f["s"][c % 2]
                    ve.tensor_tensor(f["act"][c % 3][0:M, :], bank[4][0:M, :], other[0:M, :],
                                     ALU.mult).then_inc(s[f"{ph}_scaled"], 1)

                def low(i, c):
                    M = last[c]
                    ve.wait_ge(s[f"{ph}_hh_ready"], START + i * chunks + c + 1)
                    ve.tensor_tensor(f["hl"][c % 3][0:M, :], f["act"][c % 3][0:M, :], f["hh"][c % 3][0:M, :],
                                     ALU.subtract).then_inc(s[f"{ph}_hl_ready"], 1)

                def block_(i, u, more):
                    at = SLOTS[ph]
                    for t in range(chunks + 2):
                        if 0 <= t - 1 < chunks:
                            scaled(i, t - 1)
                        if t < chunks:
                            product(i, t)
                        if 0 <= t - 2 < chunks:
                            low(i, t - 2)
                        if more:
                            if t == at["norm"]:
                                norm(i + 1, 1 - u)
                            if t == at["t0"]:
                                xT_low(i + 1, 1 - u, 0)
                            if t == at["t1"]:
                                xT_low(i + 1, 1 - u, 1)
                            if t == at["back"]:
                                largest(i + 1, 1 - u)
                                weights(i + 1, 1 - u)
                            if t == at["weights"]:
                                weights_low(i + 1, 1 - u)
                    ve.wait_ge(s[f"{ph}_down_done"], START + i * chunks + chunks)
                    for y in range(2):
                        xt = x[:, ds(i * FT + 2 * y, 2), :].rearrange("p a d -> p (a d)")
                        st.done(ve.scalar_tensor_tensor(out=xt, in0=bank[5 + 2 * y][:, :], scalar=gates[:, gate:gate + 1], in1=xt,
                                                        op0=ALU.mult, op1=ALU.add))
                    st.wait()
                    ve.sem_inc(s[f"{ph}_resid"], 1)
                    if out_stats:
                        moments(i * FT, FT)

                norm(0, 0)
                xT_low(0, 0, 0)
                xT_low(0, 0, 1)
                largest(0, 0)
                weights(0, 0)
                weights_low(0, 0)
                with ve.Fori(0, NF // 2 - 1) as j:
                    st.loop(j, STEPS[ph])
                    for u in range(2):
                        block_(j * 2 + u, u, True)
                st.end(NF // 2 - 1)
                block_(NF - 2, 0, True)
                block_(NF - 1, 1, False)
                st.wait()
                ve.sem_inc(s[f"{ph}_loop_done"], 1)

            stats(1)
            split_router(f0, 0, 16, False)
            ffn("f0", f0, NC0, HID0, True, 1, True)
            stats(2)
            ve.wait_ge(s["mask_loaded"], 16)
            st.done(ve.tensor_copy(maskrow[0:B, :], maskraw.bitcast(U8)[0:B, :]))
            st.wait()
            st.done(ve.tensor_reduce(validb[0:B, 0:1], maskrow[0:B, :], AX_X, ALU.max))
            st.wait()
            st.done(ve.tensor_copy(valid[0:B, :], validb[0:B, 0:1].broadcast_to([B, P])))
            st.done(ve.tensor_scalar(maskrow[0:B, :], maskrow[0:B, :], 1.0, -MASKED, ALU.subtract, ALU.mult))
            st.wait()
            ve.sem_inc(s["mask_ready"], 1)
            for h in range(H1):
                ve.wait_ge(s["scalar_steps"], h + 1)
                ve.tensor_tensor(m_lo[:, h].rearrange("p k c -> p (k c)"), bank[h % 2][:, 0:256],
                                 m_hi[:, h].rearrange("p k c -> p (k c)"), ALU.subtract).then_inc(s["m_copied"], 1)
            for c in range(H1 // 2):
                ve.wait_ge(s["scalar_steps"], H1 + c + 1)
                ve.tensor_tensor(n_lo[:, 2 * c:2 * c + 2, :].rearrange("p u n -> p (u n)"), bank[2 + c % 2][:, :],
                                 n_hi[:, 2 * c:2 * c + 2, :].rearrange("p u n -> p (u n)"), ALU.subtract).then_inc(s["n_copied"], 1)
            ve.wait_ge(s["valid_psum"], 1)
            st.done(ve.tensor_copy(validb, bank[0][:, 0:B]))
            st.wait()
            ve.sem_inc(s["valid_ready"], 1)
            ve.wait_ge(s["n_psum"], H1 // 2)
            st.done(ve.memset(ones_raw, 1.0))
            st.wait()
            ve.tensor_copy(ones, ones_raw).then_inc(s["ones_ready"], 1)
            ve.wait_ge(s["o1_loaded"], 48)
            st.done(ve.tensor_copy(w1_hi, w1_raw))
            st.wait()
            ve.tensor_tensor(w1_lo, w1_raw, w1_hi, ALU.subtract).then_inc(s["w1_split"], 1)
            NB = 4

            def norm1(i):
                ve.wait_ge(s["b_xnT_psum"], START + i)
                st.done(normalise(xn_b[:, 0:1, :], i * 2))
                st.done(normalise(xn_b[:, 1:2, :], i * 2 + 1))
                st.wait()
                ve.sem_inc(s["b_xn_ready"], 1)

            def xT_low1(i):
                ve.wait_ge(s["b_xh_ready"], START + i + 1)
                ve.tensor_tensor(xl_b.rearrange("p k t -> p (k t)"), bank[2][:, :],
                                 xh_b.rearrange("p k t -> p (k t)"), ALU.subtract).then_inc(s["b_xl_ready"], 1)

            def resid1(i, t):
                ve.wait_ge(s["b_y_psum"], START + i * 2 + t + 1)
                xt = x[:, ds(i * 2 + t, 1), :].rearrange("p a d -> p (a d)")
                st.done(ve.scalar_tensor_tensor(out=xt, in0=bank[3][:, 0:D], scalar=gates[:, 2:3], in1=xt,
                                                op0=ALU.mult, op1=ALU.add))
                st.wait()
                ve.sem_inc(s["b_resid"], 1)
                moments(i * 2 + t, 1)

            def attend1(i, first=False, last=False):
                def centre(b):
                    ve.wait_ge(s["b_scores"], START + i * NB + b + 1)
                    sc = bank[b % 2][:, :].rearrange("p (g k) -> p g k", g=G1)
                    st.done(ve.tensor_reduce(rm_b[:, b % 2, :], sc, AX_X, ALU.max))
                    ve.wait_ge(s["b_pT_psum"], START + i * NB)
                    st.wait()
                    ve.tensor_tensor(probs_b[b], sc, rm_b[:, b % 2, :].unsqueeze(2).broadcast_to([P, G1, S]),
                                     ALU.subtract).then_inc(s["b_centred"], 1)

                def weigh(b):
                    ve.wait_ge(s["b_exp"], START + i * NB + b + 1)
                    st.done(ve.tensor_reduce(rs_b[:, b, :], probs_b[b], AX_X, ALU.add))
                    st.wait()
                    st.done(ve.reciprocal(rs_b[:, b, :], rs_b[:, b, :]))
                    st.wait()
                    ve.tensor_scalar(rs_b[:, b, :], rs_b[:, b, :], validb[:, ds(i * NB + b, 1)], None,
                                     ALU.mult).then_inc(s["b_recip"], 1)

                def ptl(b):
                    ve.wait_ge(s["b_pTh"], START + i * NB + b + 1)
                    ve.tensor_tensor(pTl, bank[2][:, :], pTh, ALU.subtract).then_inc(s["b_pTl"], 1)

                def otl(b):
                    for par in range(2):
                        ve.wait_ge(s["b_oTh"], START + i * NB * 2 + 2 * b + par + 1)
                        cols = slice((b % 2) * S, (b % 2 + 1) * S)
                        ve.tensor_tensor(oTl[:, b // 2, :, par, :, cols],
                                         bank[4 + par][:, :].rearrange("p (j u q) -> p j u q", j=4, u=2),
                                         oTh[:, b // 2, :, par, :, cols], ALU.subtract).then_inc(s["b_oTl"], 1)

                ve.wait_ge(s["b_ctx_loaded"], i * 32 + 32)
                ve.tensor_copy(mrow[0:1, :], mrow_raw[0:1, :]).then_inc(s["b_mrow"], 1)
                if not last:
                    norm1(i + 1)
                centre(0)
                centre(1)
                weigh(0)
                centre(2)
                weigh(1)
                centre(3)
                if not first:
                    resid1(i - 1, 1)
                if not last:
                    xT_low1(i + 1)
                weigh(2)
                weigh(3)
                ve.wait_ge(s["b_cxh"], START + i + 1)
                ve.tensor_tensor(cx_lo, cx_raw, cx_hi, ALU.subtract).then_inc(s["b_cxl"], 1)
                ptl(0)
                otl(0)
                ptl(1)
                otl(1)
                ptl(2)
                otl(2)
                ptl(3)
                resid1(i, 0)
                otl(3)

            norm1(0)
            xT_low1(0)
            attend1(0, first=True)
            with ve.Fori(1, NA - 1) as i:
                st.loop(i, STEPS["b"], 1)
                attend1(i)
            st.end(NA - 1)
            attend1(NA - 1, last=True)
            resid1(NA - 1, 1)
            st.wait()
            stats(3)
            split_router(f1, 1, 48, True)
            ffn("f1", f1, NC1, HID1, False, 3, False)


def _layouts(v):
    f = np.float32
    c = np.ascontiguousarray

    def cols(w):
        return c(w.reshape(-1, P, w.shape[1]).transpose(1, 0, 2).reshape(P, -1))

    o = {}
    o["x"] = v["x"].reshape(T, D)
    o["ctx"] = v["ctx_1024"]
    o["ctxT"] = c(v["ctx_1024"].reshape(T, CD).T)
    fs = v["fside_BxSx2_0"].reshape(NT, 2, S, 2)
    d = np.arange(HD0)
    axis, half = d // 4, (d % 4) // 2
    o["pos"] = c(fs.transpose(1, 3, 0, 2)[:, axis].reshape(P, 256))
    freq = (ROPE_BASE ** (-(half.astype(f)) / f(2))).astype(f)
    sign = np.where(d % 2 == 0, -1.0, 1.0).astype(f)
    per = np.stack([freq * sign, freq, np.zeros(HD0, f), np.full(HD0, np.pi / 2, f)], 1)
    o["freq"] = c(np.broadcast_to(per[None, :, None, :], (2, HD0, 8, 4)).reshape(P, 4).astype(f))
    g = np.stack([v["g_xattn"][0], v["g_ffn"][0], v["g_xattn"][1], v["g_ffn"][1]])
    o["gates"] = c(np.broadcast_to(g[None, :], (P, 4)))
    o["ident"] = np.eye(P, dtype=f)
    p = np.arange(P)
    o["headmask"] = ((p[:, None] % 64) // 8 == np.arange(E)[None, :]).astype(f)
    o["ownbatch"] = ((p[:, None] // 16) % 2 == p[None, :] // 64).astype(f)
    o["iota8"] = c(np.broadcast_to(np.arange(E, dtype=f)[None, :], (P, E)))
    o["bout"] = c(np.broadcast_to(v["L0_xattn_bout"][None, :], (P, D)))
    o["bup"] = c(v["L1_ffn_bup"].T)
    o["mask"] = v["mask_BxS2_bf1"].view(np.uint8)
    o["wq0"] = cols(v["L0_xattn_Wq"])
    o["wk0"] = c(v["L0_xattn_Wkv"][:, :D])
    wv = v["L0_xattn_Wkv"][:, D:].reshape(CD, 16, 2, HD0)
    o["wv0"] = c(wv.transpose(0, 2, 1, 3).reshape(CD, 2 * P))
    wo = v["L0_xattn_Wout"].reshape(HG, 4, 1, 2, HD0, D)
    o["wo0"] = cols(np.broadcast_to(wo, (HG, 4, 2, 2, HD0, D)).reshape(HG * P, D))
    gu, pad = v["L0_ffn_gate_up_proj"], NC0 * P - HID0
    z = np.zeros((pad, D), f)
    gate = np.concatenate([gu[:, :I_MOE].reshape(-1, D), v["L0_ffn_sh_gate_w"], z])
    up = np.concatenate([gu[:, I_MOE:].reshape(-1, D), v["L0_ffn_sh_up_w"], z])
    down = np.concatenate([v["L0_ffn_down_proj"].transpose(0, 2, 1).reshape(-1, D), v["L0_ffn_sh_down_w"].T, z])
    o["w0"] = c(np.concatenate([cols(gate.T), cols(up.T), cols(down)], 1))
    rw = np.concatenate([v["L0_ffn_router_weight"], v["L0_ffn_shared_gate_w"], np.zeros((1, D), f)])
    o["rw0"] = cols(rw.T)
    unit = np.arange(NC0 * P)
    owner = np.where(unit < E * I_MOE, unit // I_MOE, E)
    sel = np.zeros((KC, NC0 * P), f)
    sel[owner, unit] = 1
    sel[LOW + owner, unit] = 1
    o["sel0"] = sel
    o["wq1"] = c(v["L1_xattn_Wq"].reshape(D, H1, P).transpose(2, 1, 0).reshape(P, -1))
    o["wk1"] = c(v["L1_xattn_Wk"].reshape(CD, G1, P).transpose(2, 1, 0).reshape(P, -1))
    o["wv1"] = c(v["L1_xattn_Wv"].reshape(CD, G1, P).transpose(2, 1, 0).reshape(P, -1))
    o["wo1"] = cols(v["L1_xattn_Wo"])
    o["w1"] = c(np.concatenate([cols(v["L1_ffn_Wup"].reshape(HID1, D).T),
                                cols(v["L1_ffn_Wdown"].transpose(0, 2, 1).reshape(HID1, D))], 1))
    o["rw1"] = cols(np.concatenate([v["L1_ffn_Wg1"], np.zeros((2, D), f)]).T)
    o["wg2"] = c(v["L1_ffn_Wg2"].T)
    unit = np.arange(HID1)
    sel = np.zeros((KC, HID1), f)
    sel[unit // P, unit] = 1
    sel[LOW + unit // P, unit] = 1
    o["sel1"] = sel
    bd = np.zeros((KC, D), f)
    bd[0:E] = v["L1_ffn_bdown"]
    bd[LOW:LOW + E] = v["L1_ffn_bdown"]
    o["bdown"] = bd
    return o


def kernel(**inputs):
    import concourse.bacc as _bacc
    from concourse.bass_utils import run_bass_kernel_spmd as _run

    arrays = _layouts({k: np.asarray(v) for k, v in inputs.items()})
    nc = _bacc.Bacc("TRN2", target_bir_lowering=False, num_devices=1)
    a = {k: nc.dram_tensor(f"in_{k}", w.shape, mybir.dt.from_np(w.dtype), kind="ExternalInput").ap()
         for k, w in arrays.items()}
    out = nc.dram_tensor("out_0", (T, D), F32, kind="ExternalOutput").ap()
    build(nc, a, out)
    r = _run(nc, [{f"in_{k}": w for k, w in arrays.items()}], core_ids=[0])
    return r.results[0]["out_0"].reshape(B, S, D)
```

```python
import concourse.bass as bass
from concourse import mybir
from contextlib import ExitStack
import numpy as np

F32 = mybir.dt.float32
FR = mybir.dt.float32r
I32 = mybir.dt.int32
U32 = mybir.dt.uint32
U8 = mybir.dt.uint8
ALU = mybir.AluOpType
ACT = mybir.ActivationFunctionType
AX_X = mybir.AxisListType.X
P = 128
ds = bass.ds

B, S, D = 64, 64, 256
CD = 128
T = B * S
NT = T // P
KT = D // P
H0, HD0 = 32, 8
HG = 4
H1, G1 = 16, 8
E = 8
I_MOE, I_SH = 176, 704
HID0 = E * I_MOE + I_SH
NC0 = -(-HID0 // P)
HID1 = 1024
NC1 = HID1 // P
LN_EPS = 1e-5
ROPE_BASE = 10000.0
MASKED = -(2.0 ** 100)
LOW = 32
KC = LOW + E + 1

START = 4
NA = 16
NF = 8
FT = NT // NF
SLOTS = {"f0": dict(norm=1, t0=3, t1=5, logits=7, back=9, largest=9, weigh=10, weights=14),
         "f1": dict(norm=0, t0=1, t1=3, logits=4, back=5, largest=5, weigh=6, weights=8)}
STEPS = {"a": 24, "b": 19, "f0": 78, "f1": 58}


def rounds(eng, n, body):
    body(0, first=True)
    with eng.Fori(1, n - 1) as i:
        body(i)
    body(n - 1, last=True)


def pairs(eng, n, body):
    with eng.Fori(0, n // 2 - 1) as j:
        for u in range(2):
            body(j * 2 + u, u, True)
    body(n - 2, 0, True)
    body(n - 1, 1, False)


class Steps:

    def __init__(self, eng, sem):
        self.eng, self.sem, self.base, self.n, self.per, self.i = eng, sem, 0, 0, None, 0

    def loop(self, i, per, first=0):
        self.base, self.n, self.per, self.i = self.base + self.n - first * per, 0, per, i

    def end(self, last):
        assert self.n == self.per, f"steps a round: {self.n}"
        self.base, self.n, self.per, self.i = self.base + last * self.per, 0, None, 0

    def done(self, ins):
        ins.then_inc(self.sem, 1)
        self.n += 1
        return self.value()

    def value(self):
        if self.per is None:
            return self.base + self.n
        return self.i * self.per + (self.base + self.n)

    def wait(self, value=None):
        self.eng.wait_ge(self.sem, self.value() if value is None else value)


def build(nc, a, out):
    with ExitStack() as ctx:
        def sem(name):
            return ctx.enter_context(nc.semaphore(name))

        FIRST = -(-nc.sbuf_base // 32) * 32
        WORDS = (nc.sbuf_top - FIRST) // 4

        class Region:

            def __init__(self, at):
                self.at = self.last = at

            def take(self, name, *shape, dtype=F32, over=False):
                n = int(np.prod(shape))
                at = self.last if over else self.at
                t = nc.alloc_sbuf_tensor_at(name, [P, n], dtype, offset=FIRST + 4 * at)
                self.last, self.at = at, max(self.at, at + -(-n // 8) * 8)
                assert self.at <= WORDS, (name, self.at, WORDS)
                v = t[:, :]
                if len(shape) == 1:
                    return v
                names = "abcdef"[:len(shape)]
                return v.rearrange(f"p ({' '.join(names)}) -> p {' '.join(names)}",
                                   **{k: m for k, m in zip(names, shape)})

            def split(self, name, *shape):
                raw = self.take(name + "_raw", *shape)
                lo = self.take(name + "_lo", *shape, dtype=FR, over=True)
                return self.take(name + "_hi", *shape, dtype=FR), lo, raw

            def halves(self, name, *shape):
                return self.take(name + "_hi", *shape, dtype=FR), self.take(name + "_lo", *shape, dtype=FR)

        keep = Region(0)
        x = keep.take("x", NT, D)
        ident = keep.take("ident", P)
        headmask = keep.take("headmask", E)
        ownbatch = keep.take("ownbatch", P)
        gates = keep.take("gates", 4)
        tiny = keep.take("freqs", 4)
        iota8 = keep.take("iota8", E)
        bn = keep.take("bn", 8, 6)
        mv = keep.take("mean_var", NT, 2)
        mv_new = keep.take("mean_var_new", FT, 2)
        sd = keep.take("sd", NT)
        rstd = keep.take("rstd", NT)
        nmr = keep.take("nmr", NT)
        gbout = keep.take("gbout", D)
        validb = keep.take("validb", B)
        bup = keep.take("bup", NC1)
        maskraw = keep.take("maskraw", S // 4)
        wide = keep.at
        w0 = Region(wide)
        W0N = (2 * KT * NC0 + 2 * NC0) * P
        w0_hi, w0_lo, w0_raw = w0.split("w0", W0N)
        local = w0.at

        def ffn0_view(w):
            n = KT * NC0 * P
            gate = w[:, 0:n].rearrange("p (k m) -> p k m", k=KT)
            up = w[:, n:2 * n].rearrange("p (k m) -> p k m", k=KT)
            down = w[:, 2 * n:].rearrange("p (c n) -> p c n", n=D)
            return gate, up, down

        w1 = Region(wide)
        m_hi, m_lo = w1.halves("m", H1, KT, P)
        n_hi, n_lo = w1.halves("n", H1, D)
        w1_hi, w1_lo, w1_raw = w1.split("w1", KT * HID1 + NC1 * D)
        valid = w1.take("valid", P)
        ctxT_b = w1.take("ctxT_b", 4, S)
        mrow_raw = w1.take("mrow_raw", 4 * S)
        mrow = w1.take("mrow", 4 * S, dtype=FR)
        ones_raw = w1.take("ones_raw", P)
        ones = w1.take("ones", P, dtype=FR)
        maskrow = w1.take("maskrow", S)
        assert w1.at <= w0.at

        def ffn1_view(w):
            return w[:, 0:KT * HID1].rearrange("p (k m) -> p k m", k=KT), \
                w[:, KT * HID1:].rearrange("p (c n) -> p c n", n=D)

        r = Region(local)
        cosT = r.take("cosT", NT, S)
        sinT = r.take("sinT", NT, S)
        wq0 = r.take("wq0", KT, D)
        wk0 = r.take("wk0", D)
        wv0 = r.take("wv0", 2, P)
        wo0 = r.take("wo0", HG, D)
        xnT_a = r.take("xnT_a", KT, 2, P)
        ctxT_a = r.take("ctxT_a", 2, P)
        qs_a, qw_a, ks_a, kw_a = (r.take(n, HG, 2, S) for n in ("qs_a", "qw_a", "ks_a", "kw_a"))
        xn_a = qs_a.rearrange("p g t k -> p (g t k)").rearrange("p (t d) -> p t d", t=2)
        q_bd = r.take("q_bd", HG, 2, 2, S)
        k_rot = r.take("k_rot", HG, 2, S)
        v_bd = r.take("v_bd", 2, 16, 2, 2, HD0)
        NK = 4
        k_hd = [r.take(f"k_hd{n}", E, S) for n in range(NK)]
        NP = 4
        probs_a = [r.take(f"probs_a{n}", E, S) for n in range(NP)]
        pT_a = [r.take(f"pT_a{n}", 4, P) for n in range(2)]
        oT_a = r.take("oT_a", 2, HG, P)
        rm_a = r.take("rm_a", 2, E)
        rs_a = r.take("rs_a", 4, E)
        pos, ang, turn, trig = (k_hd[n].rearrange("p a b -> p (a b)") for n in range(4))
        pos = pos[:, 0:256]

        def ffn_region(n, chunks):
            r = Region(local)
            f = {}
            f["sel"] = r.take(f"sel{n}", chunks, P, dtype=FR)
            f["xn"] = r.take(f"xn{n}", FT, D)
            f["xh"], f["xl"] = zip(*(r.halves(f"xT{n}{m}", KT, FT * P) for m in range(2)))
            f["s"] = [r.take(f"s{n}{m}", FT * P) for m in range(2)]
            f["act"] = [r.take(f"act{n}{m}", FT * P) for m in range(3)]
            f["hh"] = [r.take(f"hh{n}{m}", FT * P, dtype=FR) for m in range(3)]
            f["hl"] = [r.take(f"hl{n}{m}", FT * P, dtype=FR) for m in range(3)]
            f["cT"] = [r.take(f"cT{n}{m}", FT * P, dtype=FR) for m in range(2)]
            for k, shape in (("lT", (FT * P,)), ("lg", (FT, E + 1)), ("m8", (FT, E)), ("ix", (FT, E)), ("ixf", (FT, 2)),
                             ("dl", (FT, 2)), ("ed", (FT, 2)), ("wt", (FT, 2)), ("w2", (FT, 1)), ("comb", (FT, E + 1)), ("c2", (FT, E)),
                             ("wg2", (E,))):
                f[k] = r.take(f"{k}{n}", *shape)
            f["rw_hi"], f["rw_lo"], f["rw_raw"] = r.split(f"rw{n}", KT, E + 2)
            f["bd_hi"], f["bd_lo"], f["bd_raw"] = r.split(f"bd{n}", D)
            return f, r

        f0, r0 = ffn_region(0, NC0)
        f1, _ = ffn_region(1, NC1)

        r = Region(local)
        q1_raw = r.take("q1_raw", H1, D)
        k1_raw = r.take("k1_raw", G1, CD)
        o1_raw = r.take("o1_raw", H1, D)
        v1_raw = r.take("v1_raw", G1, CD)
        r = Region(local)
        xn_b = r.take("xn_b", 2, D)
        xh_b, xl_b = r.halves("xT_b", KT, 2 * P)
        qT = r.take("qT", 4, H1, S)
        cx_hi, cx_lo, cx_raw = r.split("cx", 4, CD)
        probs_b = [r.take(f"probs_b{n}", G1, S) for n in range(4)]
        pTh, pTl = r.halves("pT_b", 4 * P)
        oTh, oTl = r.halves("oT_b", 2, 4, 2, 2, P)
        rm_b = w1.take("rm_b", 2, G1)
        rs_b = w1.take("rs_b", 4, G1)
        assert w1.at <= w0.at

        bank = [ctx.enter_context(nc.psum_tensor(f"bank{n}", [P, 512], F32)) for n in range(8)]

        tab = {k: nc.dram_tensor(f"{k}_table", (16, NT * S), F32).ap() for k in ("cos", "sin")}

        biases = nc.dram_tensor("mask_biases", (1, B * S), F32).ap()

        names = """x0_loaded x1_loaded x2_loaded x3_loaded const_loaded w0x_loaded w0f_loaded pos_loaded tables_stored tables_loaded
        gates_ready sd_wanted sd_ready zeros_ready gbout_ready trig_wanted trig_ready
        a_xn_ready a_xnT_psum a_xnT_ready a_ctx_loaded a_q_psum a_k_psum a_v_psum a_q_read a_k_read w0_hi a_bias
        a_v_ready a_k_ready a_q_sum a_q_swapped a_k_swapped a_q_turned a_k_turned a_q_ready a_khd_ready a_scores a_centred a_exp a_recip a_probs a_pT_psum a_pT_ready
        a_o_psum a_oT_ready a_y_psum a_resid a_loop_done
        sel0_loaded sel1_loaded sel0_cast sel1_cast w1_loaded o1_loaded m_psum m_copied n_psum n_copied w0_split w1_split rw_split
        mask_loaded mask_ready biases_stored valid_psum valid_ready ones_ready
        b_xn_ready b_xnT_psum b_xh_ready b_xl_ready b_ctx_loaded b_cx_loaded b_q_psum b_q_ready b_cxh b_cxl b_scores b_centred
        b_exp b_recip b_probs b_pT_psum b_pTh b_pTl b_o_psum b_oTh b_oTl b_y_psum b_resid b_mrow
        vector_steps scalar_steps out_stored vector_passed tensor_passed pool_passed""".split()
        s = {n: sem(n) for n in names}
        for ph in ("f0", "f1"):
            for n in """xn_ready xnT_psum xh_ready xl_ready logit_psum logit_copied logitT_psum delta_ready exp_ready
                    comb_ready combT_psum cTh_ready cTl_ready gu_psum silu act_ready scaled cb_psum hh_ready hl_ready
                    down_done resid loop_done""".split():
                s[f"{ph}_{n}"] = sem(f"{ph}_{n}")

        started = dict(
            tensor="""a_xnT_psum a_q_psum a_k_psum a_v_psum a_scores a_pT_psum a_o_psum a_y_psum
                b_xnT_psum b_q_psum b_scores b_pT_psum b_o_psum b_y_psum
                f_xnT_psum f_logit_psum f_logitT_psum f_combT_psum f_gu_psum f_cb_psum f_down_done""",
            scalar="""a_q_ready a_oT_ready a_xnT_ready a_v_ready a_exp a_pT_ready w0_hi
                b_xh_ready b_cxh b_q_ready b_exp b_pTh b_oTh
                f_xh_ready f_logit_copied f_exp_ready f_silu f_cTh_ready f_hh_ready""",
            gpsimd="a_q_turned a_k_turned a_khd_ready a_probs a_bias b_probs",
            vector="""a_xn_ready a_k_ready a_q_sum a_q_swapped a_k_swapped a_q_read a_k_read a_centred a_recip a_resid
                b_xn_ready b_xl_ready b_cxl b_mrow b_centred b_recip b_pTl b_oTl b_resid
                f_xn_ready f_xl_ready f_delta_ready f_comb_ready f_cTl_ready f_act_ready f_scaled f_hl_ready f_resid""")

        def start(eng, name):
            for n in started[name].split():
                for ph in ("f0", "f1") if n.startswith("f_") else (None,):
                    eng.sem_inc(s[n if ph is None else ph + n[1:]], START)

        def angles(table, i):
            return table[:, ds(i * 2, 2), :].rearrange("p t k -> p (t k)").unsqueeze(1).broadcast_to([P, HG, 2 * S])

        block = ctx.enter_context(nc.Block())

        @block.sync
        def _(sp):
            sp.sem_inc(s["w0f_loaded"], 16)
            xs = a["x"].rearrange("(t p) d -> p t d", p=P)
            sp.dma_start(pos, a["pos"]).then_inc(s["pos_loaded"], 16)
            for n, (dst, src) in enumerate(((tiny[:, 0:4], "freq"), (gates, "gates"), (ident, "ident"), (headmask, "headmask"),
                                            (ownbatch, "ownbatch"), (iota8, "iota8"), (gbout, "bout"), (bup, "bup"))):
                sp.dma_start(dst, a[src]).then_inc(s["const_loaded"], 16)
            def load_x(n):
                sp.dma_start(x[:, 8 * n:8 * n + 8, :], xs[:, 8 * n:8 * n + 8, :]).then_inc(s[f"x{n}_loaded"], 16)

            load_x(0)
            load_x(1)
            for n, k in enumerate(("sin", "cos")):
                sp.wait_ge(s["trig_ready"], n + 1)
                sp.dma_start(tab[k].rearrange("r (g c) -> (r g) c", c=256), trig[:, 256 * n:256 * n + 256]).then_inc(
                    s["tables_stored"], 16)
                load_x(2 + n)
            for dst, src in ((wq0.rearrange("p k n -> p (k n)"), "wq0"), (wk0, "wk0"),
                             (wv0.rearrange("p k n -> p (k n)"), "wv0"), (wo0.rearrange("p k n -> p (k n)"), "wo0")):
                sp.dma_start(dst, a[src]).then_inc(s["w0x_loaded"], 16)
            sp.dma_start(maskraw.bitcast(U8)[0:B, :], a["mask"]).then_inc(s["mask_loaded"], 16)
            sp.wait_ge(s["tables_stored"], 32)
            for k, dst in (("cos", cosT), ("sin", sinT)):
                for b in range(2):
                    sp.dma_start(dst[64 * b:64 * b + 64, :, :].rearrange("p t c -> p (t c)"),
                                 tab[k][8 * b:8 * b + 8, :].unsqueeze(0).broadcast_to([8, 8, NT * S])).then_inc(
                        s["tables_loaded"], 16)
            with sp.Fori(0, NA) as i:
                sp.wait_ge(s["a_v_psum"], START + i)
                sp.dma_start(ctxT_a.rearrange("p a b -> p (a b)"), a["ctxT"][:, ds(i * 256, 256)]).then_inc(s["a_ctx_loaded"], 16)
                sp.wait_ge(s["w0f_loaded"], i * 16 + 16)
                sp.dma_start(w0_raw[:, ds(i * (W0N // NA), W0N // NA)], a["w0"][:, ds(i * (W0N // NA), W0N // NA)]).then_inc(
                    s["w0f_loaded"], 16)
            sp.wait_ge(s["a_loop_done"], 3)
            sp.dma_start(f0["rw_raw"].rearrange("p k m -> p (k m)"), a["rw0"]).then_inc(s["sel0_loaded"], 16)
            sp.wait_ge(s["f0_loop_done"], 2)
            for dst, src in ((q1_raw, "wq1"), (k1_raw, "wk1")):
                sp.dma_start(dst.rearrange("p k n -> p (k n)"), a[src]).then_inc(s["w1_loaded"], 16)
            sp.dma_start(o1_raw.rearrange("p k n -> p (k n)"), a["wo1"]).then_inc(s["o1_loaded"], 16)
            sp.dma_start(v1_raw.rearrange("p k n -> p (k n)"), a["wv1"]).then_inc(s["o1_loaded"], 16)
            sp.dma_start(w1_raw, a["w1"]).then_inc(s["o1_loaded"], 16)
            sp.wait_ge(s["n_psum"], H1 // 2)
            sp.wait_ge(s["mask_ready"], 1)
            sp.dma_start(biases.rearrange("a (b k) -> (a b) k", b=B), maskrow[0:B, :]).then_inc(s["biases_stored"], 16)
            sp.wait_ge(s["biases_stored"], 16)
            with sp.Fori(0, NA) as i:
                sp.wait_ge(s["b_scores"], START + i * 4)
                sp.dma_start(ctxT_b.rearrange("p a b -> p (a b)"), a["ctxT"][:, ds(i * 256, 256)]).then_inc(s["b_ctx_loaded"], 16)
                sp.dma_start(mrow_raw[0:1, :], biases[:, ds(i * 256, 256)]).then_inc(s["b_ctx_loaded"], 16)
                sp.wait_ge(s["b_o_psum"], START + i * 8)
                for half in range(2):
                    sp.dma_start(cx_raw[64 * half:64 * half + 64, :, :],
                                 a["ctx"][ds(i * 4, 4), :, :].rearrange("b k c -> k b c")).then_inc(s["b_cx_loaded"], 16)
            sp.wait_ge(s["b_resid"], START + NA * 2)
            sp.dma_start(f1["rw_raw"].rearrange("p k m -> p (k m)"), a["rw1"]).then_inc(s["sel1_loaded"], 16)
            sp.dma_start(f1["wg2"][0:E, :], a["wg2"]).then_inc(s["sel1_loaded"], 16)
            sp.dma_start(f1["bd_raw"][0:KC, :], a["bdown"]).then_inc(s["sel1_loaded"], 16)
            os_ = out.rearrange("(t p) d -> p t d", p=P)
            with sp.Fori(0, NF) as i:
                sp.wait_ge(s["f1_resid"], START + i + 1)
                sp.dma_start(os_[:, ds(i * FT, FT), :], x[:, ds(i * FT, FT), :]).then_inc(s["out_stored"], 16)
            sp.wait_ge(s["out_stored"], 16 * NF)
            for n, v in (("const_loaded", 128), ("tables_loaded", 64), ("w0f_loaded", 16 * NA + 16), ("x0_loaded", 16), ("x1_loaded", 16), ("x2_loaded", 16), ("x3_loaded", 16)):
                sp.wait_ge(s[n], v)

        @block.tensor
        def _(pe):
            start(pe, "tensor")

            def split3(dst, lhs, rhs, start, stop):
                (lh, ll), (rh, rl) = lhs, rhs
                pe.matmul(dst, lh, rh, start=start, stop=False, skip_group_check=True)
                pe.matmul(dst, ll, rh, start=False, stop=False, skip_group_check=True)
                return pe.matmul(dst, lh, rl, start=False, stop=stop, skip_group_check=True)

            pe.wait_ge(s["const_loaded"], 128)
            pe.wait_ge(s["w0x_loaded"], 64)
            pe.wait_ge(s["zeros_ready"], 2)
            NS = 8

            def turn_x(i):
                pe.wait_ge(s["a_xn_ready"], START + i + 1)
                pe.wait_ge(s["a_k_read"], START + i + 1)
                trb = bank[7][:, :].rearrange("p (k t c) -> p k t c", k=KT, t=2)
                for t in range(2):
                    for k in range(KT):
                        m = pe.transpose(trb[:, k, t, :], xn_a[:, t, k * P:(k + 1) * P], ident)
                m.then_inc(s["a_xnT_psum"], 1)

            def queries(i, b):
                pe.wait_ge(s["a_xnT_ready"], START + i + 1)
                qb = bank[7][:, :].rearrange("p (g t k) -> p g t k", g=HG, t=2)
                for g in range(HG):
                    for k in range(KT):
                        m = pe.matmul(qb[64 * b:64 * b + 64, g], wq0[:, k, 64 * g:64 * g + 64],
                                      xnT_a[:, k, :, 64 * b:64 * b + 64], start=(k == 0), stop=(k == KT - 1))
                if b == 1:
                    m.then_inc(s["a_q_psum"], 1)

            def keys(i):
                pe.wait_ge(s["a_ctx_loaded"], i * 16 + 16)
                pe.wait_ge(s["a_q_read"], START + i)
                kb = bank[7][:, :].rearrange("p (g t k) -> p g t k", g=HG, t=2)
                for b in range(2):
                    for g in range(HG):
                        m = pe.matmul(kb[64 * b:64 * b + 64, g], wk0[:, 64 * g:64 * g + 64], ctxT_a[:, :, 64 * b:64 * b + 64],
                                      start=True, stop=True)
                m.then_inc(s["a_k_psum"], 1)

            def values(i):
                pe.wait_ge(s["a_v_ready"], START + i * 4)
                vb = bank[6][:, :].rearrange("p (b n) -> p b n", b=4)
                for par in range(2):
                    for b in range(4):
                        m = pe.matmul(vb[64 * par:64 * par + 64, b], ctxT_a[:, b // 2, 64 * (b % 2):64 * (b % 2) + 64],
                                      wv0[:, par, :], start=True, stop=True)
                m.then_inc(s["a_v_psum"], 1)

            def scores0(i, n):
                pe.wait_ge(s["a_khd_ready"], START + i * NS + n + 1)
                if n % 4 == 0:
                    pe.wait_ge(s["a_q_ready"], START + i * 4 + 2 + n // 2)
                pe.wait_ge(s["a_centred"], START + i * NS + n - 1)
                pe.matmul(bank[n % 2][:, :], q_bd[:, n % 4, n // 4].rearrange("p b q -> p (b q)"),
                          k_hd[n % NK].rearrange("p h k -> p (h k)"), start=True, stop=True).then_inc(s["a_scores"], 1)

            def turn_probs(i, n):
                pe.wait_ge(s["a_probs"], START + i * NS + n + 1)
                pe.wait_ge(s["a_pT_ready"], START + i * NS + n - 1)
                for j in range(4):
                    m = pe.transpose(bank[2 + n % 2][:, j * P:(j + 1) * P],
                                     probs_a[n % NP].rearrange("p h k -> p (h k)")[:, j * P:(j + 1) * P], ident)
                m.then_inc(s["a_pT_psum"], 1)

            def outputs0(i, n):
                pe.wait_ge(s["a_pT_ready"], START + i * NS + n + 1)
                if n % 4 == 0:
                    pe.wait_ge(s["a_v_ready"], START + i * 4 + 2 + n // 2)
                pe.wait_ge(s["a_oT_ready"], START + i * NS * 2 + n * 2)
                for j in range(4):
                    m = pe.matmul(bank[4][32 * j:32 * j + 32, 0:P],
                                  v_bd[:, n // 4, 4 * (n % 4) + j].rearrange("p b r d -> p (b r d)"),
                                  pT_a[n % 2][:, j, :], start=True, stop=True)
                m.then_inc(s["a_o_psum"], 1)

            def project0(i, n):
                pe.wait_ge(s["a_oT_ready"], START + i * NS * 2 + n * 2 + 2)
                if n % 4 == 0:
                    pe.wait_ge(s["a_resid"], START + i * 2 + n // 4)
                m = pe.matmul(bank[5][:, 0:D], oT_a[:, n // 4, n % 4, :], wo0[:, n % 4, :],
                              start=(n % 4 == 0), stop=(n % 4 == 3))
                if n % 4 == 3:
                    m.then_inc(s["a_y_psum"], 1)

            def late(i, t, lag, step, first):
                if t >= lag:
                    step(i, t - lag)
                elif not first:
                    step(i - 1, t - lag + NS)

            def attend0(i, first=False, last=False):
                for t in range(NS + 5 if last else NS):
                    if t + 1 < NS:
                        scores0(i, t + 1)
                    for lag, step in ((3, turn_probs), (4, outputs0), (5, project0)):
                        if t - lag < NS:
                            late(i, t, lag, step, first)
                    if not last:
                        if t == 0:
                            keys(i + 1)
                        if t == 1:
                            turn_x(i + 1)
                        if t in (2, 3):
                            queries(i + 1, t - 2)
                        if t == 6:
                            values(i + 1)
                        if t == 7:
                            scores0(i + 1, 0)

            keys(0)
            turn_x(0)
            queries(0, 0)
            queries(0, 1)
            values(0)
            scores0(0, 0)
            rounds(pe, NA, attend0)
            pe.wait_ge(s["a_resid"], START + NA * 2)
            pe.sem_inc(s["a_loop_done"], 1)

            def ffn(ph, f, chunks, hidden, gate, up, down, rows_last):
                gated = gate is not None
                last = {c: (hidden - c * P if (c + 1) * P > hidden else P) for c in range(chunks)}
                NL = E + 1 if gated else E

                def turn(i, u, k):
                    pe.wait_ge(s[f"{ph}_xn_ready"], START + i + 1)
                    if k == 0:
                        pe.wait_ge(s[f"{ph}_cTl_ready"], START + i)
                    else:
                        pe.wait_ge(s[f"{ph}_xl_ready"], START + i * KT + k)
                    for t in range(FT):
                        m = pe.transpose(bank[6][:, t * P:(t + 1) * P], f["xn"][:, t, k * P:(k + 1) * P], ident)
                    m.then_inc(s[f"{ph}_xnT_psum"], 1)

                def logits(i, u):
                    pe.wait_ge(s[f"{ph}_xh_ready"], START + i * KT + KT)
                    pe.wait_ge(s[f"{ph}_xl_ready"], START + i * KT + KT)
                    for k in range(KT):
                        m = split3(bank[6][0:NL, :], (f["rw_hi"][:, k, 0:NL], f["rw_lo"][:, k, 0:NL]),
                                   (f["xh"][u][:, k, :], f["xl"][u][:, k, :]), k == 0, k == KT - 1)
                    m.then_inc(s[f"{ph}_logit_psum"], 1)

                def logits_back(i, u):
                    pe.wait_ge(s[f"{ph}_logit_copied"], START + i + 1)
                    pe.sem_inc(s["tensor_passed"], 1)
                    for t in range(FT):
                        cols = f["lT"][0:NL, t * P:(t + 1) * P]
                        if gated:
                            m = pe.transpose(bank[6][:, t * 16:t * 16 + NL], cols, ident[0:NL, 0:NL])
                        else:
                            m = pe.matmul(bank[6][:, t * 16:t * 16 + NL], cols, f["wg2"][0:E, :], start=True, stop=True)
                    m.then_inc(s[f"{ph}_logitT_psum"], 1)

                def turn_weights(i, u):
                    pe.wait_ge(s[f"{ph}_comb_ready"], START + i + 1)
                    for t in range(FT):
                        m = pe.transpose(bank[6][0:NL, t * P:(t + 1) * P], f["comb"][:, t, 0:NL], ident)
                    m.then_inc(s[f"{ph}_combT_psum"], 1)

                def gate_up(i, u, c):
                    M = last[c]
                    cols = slice(c * P, c * P + M)
                    pe.wait_ge(s[f"{ph}_silu"], START + i * chunks + c - 1)
                    if gated:
                        pe.wait_ge(s[f"{ph}_act_ready"], START + i * chunks + c - 1)
                    for w, b in ((gate, 0), (up, 2)) if gated else ((up, 0),):
                        for k in range(KT):
                            m = split3(bank[b + c % 2][0:M, :], (w[0][:, k, cols], w[1][:, k, cols]),
                                       (f["xh"][u][:, k, :], f["xl"][u][:, k, :]), k == 0, k == KT - 1)
                    m.then_inc(s[f"{ph}_gu_psum"], 1)

                def spread(i, u, c):
                    if c == 0:
                        pe.wait_ge(s[f"{ph}_cTh_ready"], START + i + 1)
                        pe.wait_ge(s[f"{ph}_cTl_ready"], START + i + 1)
                    pe.wait_ge(s[f"{ph}_scaled"], START + i * chunks + c)
                    M = last[c]
                    pe.sem_inc(s["tensor_passed"], 1)
                    pe.matmul(bank[4][0:M, :], f["sel"][0:KC, c, 0:M], f["cT"][u][0:KC, :],
                              start=True, stop=True, skip_group_check=True).then_inc(s[f"{ph}_cb_psum"], 1)

                def down_part(i, u, c):
                    M = last[c]
                    pe.wait_ge(s[f"{ph}_hh_ready"], START + i * chunks + c + 1)
                    pe.wait_ge(s[f"{ph}_hl_ready"], START + i * chunks + c + 1)
                    if c == 0:
                        pe.wait_ge(s[f"{ph}_resid"], START + i)
                    for t in range(FT):
                        y = bank[5 + 2 * (t // 2)][:, (t % 2) * D:(t % 2 + 1) * D]
                        if c == 0 and not gated:
                            cols = f["cT"][u][0:KC, t * P:(t + 1) * P]
                            pe.matmul(y, cols, f["bd_hi"][0:KC, :], start=(t % 2 == 0), stop=False, skip_group_check=True)
                            pe.matmul(y, cols, f["bd_lo"][0:KC, :], start=False, stop=False, skip_group_check=True)
                        m = split3(y, (f["hh"][c % 3][0:M, t * P:(t + 1) * P], f["hl"][c % 3][0:M, t * P:(t + 1) * P]),
                                   (down[0][0:M, c, :], down[1][0:M, c, :]),
                                   gated and c == 0 and t % 2 == 0, c == chunks - 1)
                    m.then_inc(s[f"{ph}_down_done"], 1)

                def block_(i, u, more):
                    at = SLOTS[ph]
                    for t in range(chunks + 3):
                        if t < chunks:
                            gate_up(i, u, t)
                        if 0 <= t - 1 < chunks:
                            spread(i, u, t - 1)
                        if more:
                            if t == at["t0"]:
                                turn(i + 1, 1 - u, 0)
                            if t == at["t1"]:
                                turn(i + 1, 1 - u, 1)
                            if t == at["logits"]:
                                logits(i + 1, 1 - u)
                            if t == at["back"]:
                                logits_back(i + 1, 1 - u)
                            if t == at["weights"]:
                                turn_weights(i + 1, 1 - u)
                        if 0 <= t - 3 < chunks:
                            down_part(i, u, t - 3)

                turn(0, 0, 0)
                turn(0, 0, 1)
                logits(0, 0)
                logits_back(0, 0)
                turn_weights(0, 0)
                pairs(pe, NF, block_)
                pe.wait_ge(s[f"{ph}_resid"], START + NF)
                pe.sem_inc(s[f"{ph}_loop_done"], 1)

            pe.wait_ge(s["sel0_cast"], 16)
            pe.wait_ge(s["w0_split"], NA)
            pe.wait_ge(s["rw_split"], 1)
            hi, lo = ffn0_view(w0_hi), ffn0_view(w0_lo)
            ffn("f0", f0, NC0, HID0, (hi[0], lo[0]), (hi[1], lo[1]), (hi[2], lo[2]), None)

            pe.wait_ge(s["w1_loaded"], 32)
            for h in range(H1):
                if h >= 2:
                    pe.wait_ge(s["m_copied"], h - 1)
                for k in range(KT):
                    m = pe.matmul(bank[h % 2][:, k * P:(k + 1) * P], q1_raw[:, h, k * P:(k + 1) * P], k1_raw[:, h // 2, :],
                                  start=True, stop=True)
                m.then_inc(s["m_psum"], 1)
            pe.wait_ge(s["o1_loaded"], 48)
            for c in range(H1 // 2):
                if c >= 2:
                    pe.wait_ge(s["n_copied"], c - 1)
                for u in range(2):
                    m = pe.matmul(bank[2 + c % 2][:, u * D:(u + 1) * D], v1_raw[:, c, :], o1_raw[:, 2 * c + u, :],
                                  start=True, stop=True)
                m.then_inc(s["n_psum"], 1)
            pe.wait_ge(s["mask_ready"], 1)
            pe.wait_ge(s["m_copied"], H1)
            pe.matmul(bank[0][:, 0:B], valid[0:B, :], ident[0:B, 0:B], start=True, stop=True).then_inc(s["valid_psum"], 1)
            pe.wait_ge(s["valid_ready"], 1)
            pe.wait_ge(s["n_copied"], H1 // 2)
            pe.wait_ge(s["ones_ready"], 1)
            NB = 4

            def turn_x1(i, first=False):
                pe.wait_ge(s["b_xn_ready"], START + i + 1)
                if not first:
                    pe.wait_ge(s["b_pTh"], START + (i - 1) * NB)
                    pe.wait_ge(s["b_pTl"], START + (i - 1) * NB)
                trb = bank[2][:, :].rearrange("p (k t c) -> p k t c", k=KT, t=2)
                for t in range(2):
                    for k in range(KT):
                        m = pe.transpose(trb[:, k, t, :], xn_b[:, t, k * P:(k + 1) * P], ident)
                m.then_inc(s["b_xnT_psum"], 1)

            def queries1(i, c):
                if c == 0:
                    pe.wait_ge(s["b_xh_ready"], START + i + 1)
                    pe.wait_ge(s["b_xl_ready"], START + i + 1)
                pe.wait_ge(s["b_q_ready"], START + i * 8 + c - 1)
                for u in range(2):
                    for k in range(KT):
                        m = split3(bank[6 + c % 2][:, u * 256:(u + 1) * 256], (m_hi[:, 2 * c + u, k, :], m_lo[:, 2 * c + u, k, :]),
                                   (xh_b[:, k, :], xl_b[:, k, :]), u == 0 and k == 0, k == KT - 1)
                m.then_inc(s["b_q_psum"], 1)

            def scores1(i, b):
                if b == 0:
                    pe.wait_ge(s["b_mrow"], START + i + 1)
                    pe.wait_ge(s["b_q_ready"], START + i * 8 + 8)
                    pe.wait_ge(s["b_ctx_loaded"], i * 32 + 32)
                pe.wait_ge(s["b_centred"], START + i * NB + b - 1)
                pe.matmul(bank[b % 2][:, :].rearrange("p (g k) -> p g k", g=G1), ones[0:1, :],
                          mrow[0:1, b * S:(b + 1) * S].unsqueeze(1).broadcast_to([1, G1, S]),
                          start=True, stop=False, skip_group_check=True)
                for g in range(G1):
                    m = pe.matmul(bank[b % 2][:, g * S:(g + 1) * S], qT[:, b, 2 * g:2 * g + 2, :].rearrange("p h q -> p (h q)"),
                                  ctxT_b[:, b, :], start=False, stop=(g == G1 - 1), skip_group_check=True)
                m.then_inc(s["b_scores"], 1)

            def turn_probs1(i, b, last):
                pe.wait_ge(s["b_probs"], START + i * NB + b + 1)
                pe.wait_ge(s["b_pTh"], START + i * NB + b)
                pe.wait_ge(s["b_pTl"], START + i * NB + b)
                if b == 0:
                    pe.wait_ge(s["b_xh_ready"], START + i + (1 if last else 2))
                    pe.wait_ge(s["b_xl_ready"], START + i + (1 if last else 2))
                for j in range(4):
                    m = pe.transpose(bank[2][:, j * P:(j + 1) * P],
                                     probs_b[b].rearrange("p g k -> p (g k)")[:, j * P:(j + 1) * P], ident)
                m.then_inc(s["b_pT_psum"], 1)

            def outputs1(i, b):
                pe.wait_ge(s["b_pTh"], START + i * NB + b + 1)
                pe.wait_ge(s["b_pTl"], START + i * NB + b + 1)
                if b == 0:
                    pe.wait_ge(s["b_cxh"], START + i + 1)
                    pe.wait_ge(s["b_cxl"], START + i + 1)
                for par in range(2):
                    pe.wait_ge(s["b_oTh"], START + i * NB * 2 + 2 * b - 1 + par)
                    pe.wait_ge(s["b_oTl"], START + i * NB * 2 + 2 * b - 1 + par)
                    rows = slice(64 * par, 64 * par + 64)
                    split3(bank[4 + par][:, :], (cx_hi[rows, b, :], cx_lo[rows, b, :]), (pTh[rows, :], pTl[rows, :]),
                           True, True).then_inc(s["b_o_psum"], 1)

            def project1(i, t, half):
                if half == 0:
                    pe.wait_ge(s["b_oTh"], START + i * NB * 2 + 4 * t + 4)
                    pe.wait_ge(s["b_oTl"], START + i * NB * 2 + 4 * t + 4)
                    pe.wait_ge(s["b_resid"], START + i * 2 + t)
                for h in range(8 * half, 8 * half + 8):
                    j, par, u = h // 4, (h // 2) % 2, h % 2
                    m = split3(bank[3][:, 0:D], (oTh[:, t, j, par, u, :], oTl[:, t, j, par, u, :]),
                               (n_hi[:, h, :], n_lo[:, h, :]), h == 0, h == H1 - 1)
                if half == 1:
                    m.then_inc(s["b_y_psum"], 1)

            def attend1(i, first=False, last=False):
                def rest(step, *args):
                    if not first:
                        step(i - 1, *args)

                def ahead(step, *args):
                    if not last:
                        step(i + 1, *args)

                scores1(i, 0)
                rest(outputs1, 3)
                rest(project1, 0, 1)
                scores1(i, 1)
                rest(project1, 1, 0)
                scores1(i, 2)
                ahead(turn_x1)
                rest(project1, 1, 1)
                ahead(queries1, 0)
                scores1(i, 3)
                turn_probs1(i, 0, last)
                ahead(queries1, 1)
                ahead(queries1, 2)
                outputs1(i, 0)
                turn_probs1(i, 1, last)
                ahead(queries1, 3)
                ahead(queries1, 4)
                outputs1(i, 1)
                turn_probs1(i, 2, last)
                ahead(queries1, 5)
                ahead(queries1, 6)
                outputs1(i, 2)
                turn_probs1(i, 3, last)
                ahead(queries1, 7)
                project1(i, 0, 0)

            turn_x1(0, first=True)
            for c in range(H1 // 2):
                queries1(0, c)
            rounds(pe, NA, attend1)
            outputs1(NA - 1, 3)
            project1(NA - 1, 0, 1)
            project1(NA - 1, 1, 0)
            project1(NA - 1, 1, 1)
            pe.wait_ge(s["b_resid"], START + NA * 2)
            pe.wait_ge(s["sel1_cast"], 16)
            pe.wait_ge(s["sel1_loaded"], 48)
            pe.wait_ge(s["rw_split"], 2)
            pe.wait_ge(s["w1_split"], 1)
            hi, lo = ffn1_view(w1_hi), ffn1_view(w1_lo)
            ffn("f1", f1, NC1, HID1, None, (hi[0], lo[0]), (hi[1], lo[1]), None)

        @block.scalar
        def _(act):
            start(act, "scalar")
            act.wait_ge(s["const_loaded"], 128)
            act.activation(gates, gates, ACT.Tanh).then_inc(s["gates_ready"], 1)
            for n in range(2):
                act.wait_ge(s["trig_wanted"], n + 1)
                act.activation(trig[:, 256 * n:256 * n + 256], ang[:, 256 * n:256 * n + 256], ACT.Sin).then_inc(s["trig_ready"], 1)

            def root(n):
                act.wait_ge(s["sd_wanted"], n + 1)
                act.activation(sd, sd, ACT.Sqrt).then_inc(s["sd_ready"], 1)

            root(0)
            NS = 8
            SCALE0 = float(HD0) ** -0.5
            act.wait_ge(s["zeros_ready"], 2)
            WS = W0N // NA

            def xT_copy(i):
                act.wait_ge(s["a_xnT_psum"], START + i + 1)
                act.wait_ge(s["a_q_psum"], START + i)
                act.activation(xnT_a.rearrange("p k t c -> p (k t c)"), bank[7][:, :], ACT.Copy).then_inc(s["a_xnT_ready"], 1)

            def v_copy(i, t, first=False):
                if t == 0:
                    act.wait_ge(s["a_v_psum"], START + i + 1)
                if not first:
                    act.wait_ge(s["a_o_psum"], START + i * NS - 4 + 4 * t)
                vb = bank[6][:, :].rearrange("p (t b j d) -> p t b j d", t=2, b=2, j=16)
                for par in range(2):
                    rows = slice(64 * par, 64 * par + 64)
                    act.activation(v_bd[rows, t, :, :, par, :].rearrange("p j b d -> p b j d"), vb[rows, t],
                                   ACT.Copy).then_inc(s["a_v_ready"], 1)

            def q_copy(i, t, first=False):
                if t == 0:
                    act.wait_ge(s["a_q_sum"], START + i + 1)
                if not first:
                    act.wait_ge(s["a_scores"], START + i * NS - 4 + 4 * t)
                for b in range(2):
                    rows = slice(64 * b, 64 * b + 64)
                    act.activation(q_bd[rows, :, t, b, :], qs_a[rows, :, t, :], ACT.Copy).then_inc(s["a_q_ready"], 1)

            def pT_copy(i, n):
                act.wait_ge(s["a_pT_psum"], START + i * NS + n + 1)
                act.wait_ge(s["a_o_psum"], START + i * NS + n - 1)
                act.activation(pT_a[n % 2].rearrange("p j c -> p (j c)"), bank[2 + n % 2][:, :], ACT.Copy).then_inc(
                    s["a_pT_ready"], 1)

            def own(i, n):
                act.wait_ge(s["a_o_psum"], START + i * NS + n + 1)
                for b in range(2):
                    c = slice(64 * b, 64 * b + 64)
                    act.activation(oT_a[:, n // 4, n % 4, c], bank[4][:, c], ACT.Copy, scale=ownbatch[:, 64 * b:64 * b + 1]).then_inc(
                        s["a_oT_ready"], 1)

            def attend0(i, first=False, last=False):
                for t in range(NS + 5 if last else NS):
                    if t >= 5:
                        own(i, t - 5)
                    elif not first:
                        own(i - 1, t - 5 + NS)
                    if t < NS:
                        act.wait_ge(s["a_centred"], START + i * NS + t + 1)
                        act.activation(probs_a[t % NP], probs_a[t % NP], ACT.Exp, scale=SCALE0).then_inc(s["a_exp"], 1)
                    if t >= 3:
                        if t - 3 < NS:
                            pT_copy(i, t - 3)
                    elif not first:
                        pT_copy(i - 1, t - 3 + NS)
                    if t == 0:
                        v_copy(i, 0, first)
                    if t == 4:
                        v_copy(i, 1, first)
                    if not last:
                        if t == 1:
                            xT_copy(i + 1)
                        if t == 6:
                            q_copy(i + 1, 0)
                        if t == 7:
                            q_copy(i + 1, 1)
                    if t == 5:
                        act.wait_ge(s["w0f_loaded"], i * 16 + 32)
                        act.activation(w0_hi[:, ds(i * WS, WS)], w0_raw[:, ds(i * WS, WS)], ACT.Copy).then_inc(s["w0_hi"], 1)

            xT_copy(0)
            q_copy(0, 0, first=True)
            q_copy(0, 1, first=True)
            rounds(act, NA, attend0)

            def ffn(ph, f, chunks, hidden, gated):
                last = {c: (hidden - c * P if (c + 1) * P > hidden else P) for c in range(chunks)}
                NL = E + 1 if gated else E

                def xT_high(i, u, k):
                    act.wait_ge(s[f"{ph}_xnT_psum"], START + i * KT + k + 1)
                    act.activation(f["xh"][u][:, k, :], bank[6][:, :], ACT.Copy).then_inc(s[f"{ph}_xh_ready"], 1)

                def logits_copy(i, u):
                    act.wait_ge(s[f"{ph}_logit_psum"], START + i + 1)
                    act.activation(f["lT"][0:NL, :], bank[6][0:NL, :], ACT.Copy if gated else ACT.Tanh).then_inc(
                        s[f"{ph}_logit_copied"], 1)

                def halves(i, u):
                    act.wait_ge(s[f"{ph}_delta_ready"], START + i + 1)
                    act.activation(f["ed"], f["dl"], ACT.Tanh, scale=0.5).then_inc(s[f"{ph}_exp_ready"], 1)

                def weights_high(i, u):
                    act.wait_ge(s[f"{ph}_combT_psum"], START + i + 1)
                    act.activation(f["cT"][u][0:NL, :], bank[6][0:NL, :], ACT.Copy).then_inc(s[f"{ph}_cTh_ready"], 1)

                def silu(i, c):
                    M = last[c]
                    act.wait_ge(s[f"{ph}_gu_psum"], START + i * chunks + c + 1)
                    act.wait_ge(s[f"{ph}_act_ready" if gated else f"{ph}_scaled"], START + i * chunks + c - 1)
                    act.activation(f["s"][c % 2][0:M, :], bank[c % 2][0:M, :], ACT.Silu,
                                   **({} if gated else {"bias": bup[:, c:c + 1]})).then_inc(s[f"{ph}_silu"], 1)

                def high(i, c):
                    M = last[c]
                    act.wait_ge(s[f"{ph}_scaled"], START + i * chunks + c + 1)
                    act.wait_ge(s[f"{ph}_down_done"], START + i * chunks + (c - 2 if c >= 3 else 0))
                    act.activation(f["hh"][c % 3][0:M, :], f["act"][c % 3][0:M, :], ACT.Copy).then_inc(
                        s[f"{ph}_hh_ready"], 1)

                def block_(i, u, more):
                    at = SLOTS[ph]
                    for t in range(chunks + 2):
                        if t < chunks:
                            silu(i, t)
                        if 1 <= t <= chunks:
                            high(i, t - 1)
                        if more:
                            if t == at["t0"]:
                                xT_high(i + 1, 1 - u, 0)
                            if t == at["t1"]:
                                xT_high(i + 1, 1 - u, 1)
                            if t == at["logits"]:
                                logits_copy(i + 1, 1 - u)
                            if t == at["weigh"]:
                                halves(i + 1, 1 - u)
                            if t == at["weights"]:
                                weights_high(i + 1, 1 - u)

                xT_high(0, 0, 0)
                xT_high(0, 0, 1)
                logits_copy(0, 0)
                halves(0, 0)
                weights_high(0, 0)
                pairs(act, NF, block_)

            root(1)
            ffn("f0", f0, NC0, HID0, True)
            root(2)
            for h in range(H1):
                act.wait_ge(s["m_psum"], h + 1)
                act.activation(m_hi[:, h].rearrange("p k c -> p (k c)"), bank[h % 2][:, 0:256], ACT.Copy).then_inc(
                    s["scalar_steps"], 1)
            for c in range(H1 // 2):
                act.wait_ge(s["n_psum"], c + 1)
                act.activation(n_hi[:, 2 * c:2 * c + 2, :].rearrange("p u n -> p (u n)"), bank[2 + c % 2][:, :],
                               ACT.Copy).then_inc(s["scalar_steps"], 1)
            NB = 4
            SCALE1 = float(CD) ** -0.5

            def xT_high1(i):
                act.wait_ge(s["b_xnT_psum"], START + i + 1)
                act.wait_ge(s["b_q_psum"], START + i * 8)
                act.activation(xh_b.rearrange("p k t -> p (k t)"), bank[2][:, :], ACT.Copy).then_inc(s["b_xh_ready"], 1)

            def q_copy(i, c):
                act.wait_ge(s["b_q_psum"], START + i * 8 + c + 1)
                act.wait_ge(s["b_scores"], START + i * NB)
                act.activation(qT[:, :, 2 * c:2 * c + 2, :].rearrange("p b h q -> p h b q"),
                               bank[6 + c % 2][:, :].rearrange("p (h b q) -> p h b q", h=2, b=4), ACT.Copy).then_inc(
                    s["b_q_ready"], 1)

            def pth(i, b):
                act.wait_ge(s["b_pT_psum"], START + i * NB + b + 1)
                act.wait_ge(s["b_o_psum"], START + i * NB * 2 + 2 * b)
                act.activation(pTh, bank[2][:, :], ACT.Copy).then_inc(s["b_pTh"], 1)

            def oth(i, b):
                if b % 2 == 0:
                    act.wait_ge(s["b_y_psum"], START + i * 2 + b // 2 - 1)
                for par in range(2):
                    act.wait_ge(s["b_o_psum"], START + i * NB * 2 + 2 * b + par + 1)
                    act.activation(oTh[:, b // 2, :, par, :, (b % 2) * S:(b % 2 + 1) * S],
                                   bank[4 + par][:, :].rearrange("p (j u q) -> p j u q", j=4, u=2), ACT.Copy).then_inc(
                        s["b_oTh"], 1)

            def attend1(i, first=False, last=False):
                def expo(b):
                    act.wait_ge(s["b_centred"], START + i * NB + b + 1)
                    act.activation(probs_b[b], probs_b[b], ACT.Exp, scale=SCALE1).then_inc(s["b_exp"], 1)

                def next_q(*cs):
                    if not last:
                        for c in cs:
                            q_copy(i + 1, c)

                expo(0)
                if not first:
                    oth(i - 1, 3)
                expo(1)
                act.wait_ge(s["b_cx_loaded"], i * 32 + 32)
                act.wait_ge(s["b_o_psum"], START + i * 8)
                act.activation(cx_hi, cx_raw, ACT.Copy).then_inc(s["b_cxh"], 1)
                expo(2)
                if not last:
                    xT_high1(i + 1)
                expo(3)
                next_q(0)
                pth(i, 0)
                next_q(1, 2)
                oth(i, 0)
                pth(i, 1)
                next_q(3, 4)
                oth(i, 1)
                pth(i, 2)
                next_q(5, 6)
                oth(i, 2)
                pth(i, 3)
                next_q(7)

            xT_high1(0)
            for c in range(H1 // 2):
                q_copy(0, c)
            rounds(act, NA, attend1)
            oth(NA - 1, 3)
            root(3)
            ffn("f1", f1, NC1, HID1, False)

        @block.gpsimd
        def _(pool):
            start(pool, "gpsimd")
            pool.memset(v_bd, 0.0).then_inc(s["zeros_ready"], 1)
            pool.wait_ge(s["const_loaded"], 128)
            NS = 8
            WS = W0N // NA
            AHEAD = 4

            def heads(i, n):
                if n == 0:
                    pool.wait_ge(s["a_k_ready"], START + i + 1)
                pool.wait_ge(s["a_scores"], START + i * NS + n - NK + 1)
                pool.tensor_tensor(k_hd[n % NK], k_rot[:, n % 4, n // 4, :].unsqueeze(1).broadcast_to([P, E, S]),
                                   headmask.unsqueeze(2).broadcast_to([P, E, S]), ALU.mult).then_inc(s["a_khd_ready"], 1)

            def bias(i):
                pool.wait_ge(s["a_xn_ready"], START + i + 1)
                pool.tensor_tensor(x[:, ds(i * 2, 2), :], x[:, ds(i * 2, 2), :],
                                   gbout.unsqueeze(1).broadcast_to([P, 2, D]), ALU.add).then_inc(s["a_bias"], 1)

            def sine(i, swapped, wanted, done):
                pool.wait_ge(s[wanted], START + i + 1)
                pool.sem_inc(s["pool_passed"], 1)
                w = swapped.rearrange("p g t k -> p g (t k)")
                pool.tensor_tensor(w, w, angles(sinT, i), ALU.mult).then_inc(s[done], 1)

            def attend0(i, first=False, last=False):
                for n in range(NS):
                    pool.wait_ge(s["a_recip"], START + i * NS + n + 1)
                    pool.tensor_tensor(probs_a[n % NP], probs_a[n % NP], rs_a[:, n % 4, :].unsqueeze(2).broadcast_to([P, E, S]),
                                       ALU.mult).then_inc(s["a_probs"], 1)
                    if n + AHEAD < NS:
                        heads(i, n + AHEAD)
                    elif not last:
                        heads(i + 1, n + AHEAD - NS)
                    if n == 1 and not last:
                        sine(i + 1, kw_a, "a_k_swapped", "a_k_turned")
                    if n == 4 and not last:
                        sine(i + 1, qw_a, "a_q_swapped", "a_q_turned")
                    if n == 2 and not last:
                        bias(i + 1)
                    if n == 6:
                        pool.wait_ge(s["w0_hi"], START + i + 1)
                        pool.tensor_tensor(w0_lo[:, ds(i * WS, WS)], w0_raw[:, ds(i * WS, WS)],
                                           w0_hi[:, ds(i * WS, WS)], ALU.subtract).then_inc(s["w0_split"], 1)

            pool.wait_ge(s["gbout_ready"], 1)
            pool.wait_ge(s["tables_loaded"], 64)
            sine(0, kw_a, "a_k_swapped", "a_k_turned")
            sine(0, qw_a, "a_q_swapped", "a_q_turned")
            for n in range(AHEAD):
                heads(0, n)
            bias(0)
            rounds(pool, NA, attend0)
            pool.sem_inc(s["a_loop_done"], 1)
            pool.wait_ge(s["a_loop_done"], 3)
            pool.dma_start(f0["sel"][0:KC].rearrange("p c m -> p (c m)"), a["sel0"]).then_inc(s["sel0_cast"], 16)
            NB = 4
            with pool.Fori(0, NA) as i:
                for b in range(NB):
                    pool.wait_ge(s["b_recip"], START + i * NB + b + 1)
                    pool.tensor_tensor(probs_b[b], probs_b[b], rs_b[:, b, :].unsqueeze(2).broadcast_to([P, G1, S]),
                                       ALU.mult).then_inc(s["b_probs"], 1)
            pool.wait_ge(s["b_resid"], START + NA * 2)
            pool.dma_start(f1["sel"][0:KC].rearrange("p c m -> p (c m)"), a["sel1"]).then_inc(s["sel1_cast"], 16)

        @block.vector
        def _(ve):
            start(ve, "vector")
            st = Steps(ve, s["vector_steps"])

            TWO_PI, PI = float(2 * np.pi), 3.14159250
            ROUND = 1.5 * 2.0 ** 23
            ve.wait_ge(s["pos_loaded"], 16)
            ve.wait_ge(s["const_loaded"], 128)
            for n in range(2):
                w = slice(256 * n, 256 * n + 256)
                st.done(ve.tensor_scalar(ang[:, w], pos, tiny[:, n:n + 1], tiny[:, 2 + n:3 + n], ALU.mult, ALU.add))
                st.wait()
                st.done(ve.tensor_scalar(turn[:, w], ang[:, w], 1.0 / TWO_PI, ROUND, ALU.mult, ALU.add))
                st.wait()
                st.done(ve.tensor_scalar(turn[:, w], turn[:, w], ROUND, -TWO_PI, ALU.subtract, ALU.mult))
                st.wait()
                st.done(ve.tensor_tensor(ang[:, w], ang[:, w], turn[:, w], ALU.add))
                st.wait()
                ve.tensor_scalar(ang[:, w], ang[:, w], PI, -PI, ALU.min, ALU.max).then_inc(s["trig_wanted"], 1)
            ve.memset(q_bd, 0.0).then_inc(s["zeros_ready"], 1)
            ve.wait_ge(s["gates_ready"], 1)
            ve.tensor_scalar(gbout, gbout, gates[:, 0:1], None, ALU.mult).then_inc(s["gbout_ready"], 1)

            for n in range(4):
                ve.wait_ge(s[f"x{n}_loaded"], 16)
                for t in range(8 * n, 8 * n + 8):
                    st.done(ve.bn_stats(bn[:, t % 8, :], x[:, t, :]))
                st.wait()
                for t in range(8 * n, 8 * n + 8):
                    st.done(ve.bn_aggr(mv[:, t, :], bn[:, t % 8, :]))
                st.wait()

            def moments(tile, count):
                for t in range(count):
                    st.done(ve.bn_stats(bn[:, t, :],
                                        x[:, ds(tile + t, 1), :].rearrange("p a d -> p (a d)")))
                st.wait()
                ve.sem_inc(s["vector_passed"], 1)
                for t in range(count):
                    st.done(ve.bn_aggr(mv_new[:, t, :], bn[:, t, :]))
                st.wait()
                st.done(ve.tensor_copy(mv[:, ds(tile, count), :], mv_new[:, 0:count, :]))

            def stats(n):
                ve.tensor_scalar(sd, mv[:, :, 1], LN_EPS, None, ALU.add).then_inc(s["sd_wanted"], 1)
                ve.wait_ge(s["sd_ready"], n + 1)
                st.done(ve.reciprocal(rstd, sd))
                st.wait()
                st.done(ve.scalar_tensor_tensor(out=nmr, in0=mv[:, :, 0], scalar=-1.0, in1=rstd, op0=ALU.mult, op1=ALU.mult))
                st.wait()

            def normalise(dst, tile):
                return ve.tensor_scalar(dst, x[:, ds(tile, 1), :], rstd[:, ds(tile, 1)], nmr[:, ds(tile, 1)], ALU.mult, ALU.add)

            stats(0)
            NS = 8

            def norm0(i):
                ve.wait_ge(s["a_q_ready"], START + i * 4)
                st.done(normalise(xn_a[:, 0:1, :], i * 2))
                st.done(normalise(xn_a[:, 1:2, :], i * 2 + 1))
                st.wait()
                ve.sem_inc(s["a_xn_ready"], 1)

            def rope(i, psum, here, swapped, read, wanted):
                ve.wait_ge(s[psum], START + i + 1)
                ve.sem_inc(s["vector_passed"], 1)
                ve.stream_shuffle(swapped.rearrange("p g t k -> p (g t k)"), bank[7][:, :], [j ^ 1 for j in range(32)]).then_inc(
                    s[wanted], 1)
                ve.tensor_tensor(here.rearrange("p g t k -> p g (t k)"), bank[7][:, :].rearrange("p (g c) -> p g c", g=HG),
                                 angles(cosT, i), ALU.mult).then_inc(s[read], 1)

            def queries(i):
                rope(i, "a_q_psum", qs_a, qw_a, "a_q_read", "a_q_swapped")

            def queries_in(i):
                ve.wait_ge(s["a_q_read"], START + i + 1)
                ve.wait_ge(s["a_q_turned"], START + i + 1)
                ve.tensor_tensor(qs_a, qs_a, qw_a, ALU.add).then_inc(s["a_q_sum"], 1)

            def keys(i):
                ve.wait_ge(s["a_k_ready"], START + i)
                rope(i, "a_k_psum", ks_a, kw_a, "a_k_read", "a_k_swapped")

            def keys_in(i):
                ve.wait_ge(s["a_khd_ready"], START + i * NS)
                ve.wait_ge(s["a_k_read"], START + i + 1)
                ve.wait_ge(s["a_k_turned"], START + i + 1)
                ve.tensor_tensor(k_rot, ks_a, kw_a, ALU.add).then_inc(s["a_k_ready"], 1)

            def largest0(i, n):
                ve.wait_ge(s["a_scores"], START + i * NS + n + 1)
                return st.done(ve.tensor_reduce(rm_a[:, n % 2, :], bank[n % 2][:, :].rearrange("p (h k) -> p h k", h=E),
                                                AX_X, ALU.max))

            def sums0(i, n):
                ve.wait_ge(s["a_exp"], START + i * NS + n + 1)
                st.done(ve.tensor_reduce(rs_a[:, n % 4, :], probs_a[n % NP], AX_X, ALU.add))

            def centre0(i, n, maximum):
                ve.wait_ge(s["a_pT_psum"], START + i * NS + n - NP + 1)
                st.wait(maximum)
                ve.tensor_tensor(probs_a[n % NP], bank[n % 2][:, :].rearrange("p (h k) -> p h k", h=E),
                                 rm_a[:, n % 2, :].unsqueeze(2).broadcast_to([P, E, S]), ALU.subtract).then_inc(s["a_centred"], 1)

            def recip0(i, n):
                st.wait()
                ve.reciprocal(rs_a[:, n % 4, :], rs_a[:, n % 4, :]).then_inc(s["a_recip"], 1)

            def resid0(i, n):
                if n % 4 == 3:
                    u = n // 4
                    ve.wait_ge(s["a_bias"], START + i + 1)
                    ve.wait_ge(s["a_y_psum"], START + i * 2 + u + 1)
                    xt = x[:, ds(i * 2 + u, 1), :].rearrange("p a d -> p (a d)")
                    ve.scalar_tensor_tensor(out=xt, in0=bank[5][:, 0:D], scalar=gates[:, 0:1], in1=xt,
                                            op0=ALU.mult, op1=ALU.add).then_inc(s["a_resid"], 1)

            def moments0(i, n):
                if n % 4 == 3:
                    ve.wait_ge(s["a_resid"], START + i * 2 + n // 4 + 1)
                    ve.sem_inc(s["vector_passed"], 1)
                    st.done(ve.bn_stats(bn[:, 0, :], x[:, ds(i * 2 + n // 4, 1), :].rearrange("p a d -> p (a d)")))

            def gathered0(i, n):
                if n % 4 == 3:
                    st.wait()
                    ve.sem_inc(s["vector_passed"], 1)
                    st.done(ve.bn_aggr(mv_new[:, 0, :], bn[:, 0, :]))

            def stored0(i, n):
                if n % 4 == 3:
                    st.wait()
                    st.done(ve.tensor_copy(mv[:, ds(i * 2 + n // 4, 1), :], mv_new[:, 0:1, :]))

            def late(i, t, lag, step, first):
                if t >= lag:
                    step(i, t - lag)
                elif not first:
                    step(i - 1, t - lag + NS)

            def attend0(i, first=False, last=False):
                for t in range(NS + 8 if last else NS):
                    if t < NS:
                        maximum = largest0(i, t)
                    if t - 1 < NS:
                        late(i, t, 1, sums0, first)
                    if t < NS:
                        centre0(i, t, maximum)
                    for lag, step in ((8, gathered0), (1, recip0), (6, resid0), (7, moments0), (8, stored0)):
                        if t - lag < NS:
                            late(i, t, lag, step, first)
                    if not last:
                        if t == 0:
                            norm0(i + 1)
                        if t == 1:
                            keys(i + 1)
                        if t == 4:
                            queries(i + 1)
                        if t == 5:
                            keys_in(i + 1)
                        if t == 6:
                            queries_in(i + 1)
            norm0(0)
            ve.wait_ge(s["tables_loaded"], 64)
            keys(0)
            queries(0)
            keys_in(0)
            queries_in(0)
            attend0(0, first=True)
            with ve.Fori(1, NA - 1) as i:
                st.loop(i, STEPS["a"], 1)
                attend0(i)
            st.end(NA - 1)
            attend0(NA - 1, last=True)
            st.wait()
            ve.sem_inc(s["a_loop_done"], 1)

            def split_router(f, n, loads, bias):
                ve.wait_ge(s[f"sel{n}_loaded"], loads)
                parts = [tuple(f[f"rw_{k}"] for k in ("hi", "lo", "raw"))]
                if bias:
                    parts.append(tuple(f[f"bd_{k}"][0:KC] for k in ("hi", "lo", "raw")))
                for hi, lo, raw in parts:
                    st.done(ve.tensor_copy(hi, raw))
                st.done(ve.memset(f["lT"][0:64, :], 0.0))
                st.wait()
                for hi, lo, raw in parts:
                    st.done(ve.tensor_tensor(lo, raw, hi, ALU.subtract))
                for cT in f["cT"]:
                    st.done(ve.tensor_copy(cT[0:64, :], f["lT"][0:64, :]))
                st.wait()
                ve.sem_inc(s["rw_split"], 1)

            def ffn(ph, f, chunks, hidden, gated, gate, out_stats):
                last = {c: (hidden - c * P if (c + 1) * P > hidden else P) for c in range(chunks)}
                NL = E + 1 if gated else E

                def norm(i, u):
                    ve.wait_ge(s[f"{ph}_xnT_psum"], START + i * KT)
                    for t in range(FT):
                        st.done(normalise(f["xn"][:, t:t + 1, :], i * FT + t))
                    st.wait()
                    ve.sem_inc(s[f"{ph}_xn_ready"], 1)

                def xT_low(i, u, k):
                    ve.wait_ge(s[f"{ph}_xh_ready"], START + i * KT + k + 1)
                    ve.tensor_tensor(f["xl"][u][:, k, :], bank[6][:, :], f["xh"][u][:, k, :], ALU.subtract).then_inc(
                        s[f"{ph}_xl_ready"], 1)

                def largest(i, u):
                    ve.wait_ge(s[f"{ph}_logitT_psum"], START + i + 1)
                    st.done(ve.tensor_copy(f["lg"][:, :, 0:NL], bank[6][:, 0:64].rearrange("p (t n) -> p t n", n=16)[:, :, 0:NL]))
                    st.wait()
                    ve.sem_inc(s["vector_passed"], 1)
                    for t in range(FT):
                        st.done(ve.max(f["m8"][:, t, :], f["lg"][:, t, 0:E]))
                    st.wait()
                    ve.sem_inc(s["vector_passed"], 1)
                    for t in range(FT):
                        st.done(ve.max_index(f["ix"][:, t, :].bitcast(U32), f["m8"][:, t, :], f["lg"][:, t, 0:E]))
                    st.done(ve.tensor_tensor(f["dl"][:, :, 0], f["m8"][:, :, 0], f["m8"][:, :, 1], ALU.subtract))
                    if gated:
                        st.done(ve.tensor_copy(f["dl"][:, :, 1], f["lg"][:, :, E]))
                    else:
                        st.done(ve.memset(f["dl"][:, :, 1], 0.0))
                    st.wait()
                    ve.sem_inc(s[f"{ph}_delta_ready"], 1)
                    st.done(ve.tensor_copy(f["ixf"], f["ix"][:, :, 0:2].bitcast(U32)))

                def weights(i, u):
                    ve.wait_ge(s[f"{ph}_exp_ready"], START + i + 1)
                    st.done(ve.tensor_scalar(f["wt"], f["ed"], 0.5, 0.5, ALU.mult, ALU.add))
                    st.done(ve.tensor_scalar(f["w2"], f["ed"][:, :, 0:1], -0.5, 0.5, ALU.mult, ALU.add))
                    st.wait()
                    if gated:
                        st.done(ve.tensor_copy(f["comb"][:, :, E], f["wt"][:, :, 1]))
                    for t in range(FT):
                        st.done(ve.tensor_scalar(f["comb"][:, t, 0:E], iota8, f["ixf"][:, t, 0:1], f["wt"][:, t, 0:1],
                                                 ALU.is_equal, ALU.mult))
                        st.done(ve.tensor_scalar(f["c2"][:, t, :], iota8, f["ixf"][:, t, 1:2], f["w2"][:, t, 0:1],
                                                 ALU.is_equal, ALU.mult))
                    st.wait()
                    st.done(ve.tensor_tensor(f["comb"][:, :, 0:E], f["comb"][:, :, 0:E], f["c2"], ALU.add))
                    st.wait()
                    ve.sem_inc(s[f"{ph}_comb_ready"], 1)

                def weights_low(i, u):
                    ve.wait_ge(s[f"{ph}_cTh_ready"], START + i + 1)
                    ve.tensor_tensor(f["cT"][u][LOW:LOW + NL, :], bank[6][0:NL, :], f["cT"][u][0:NL, :],
                                     ALU.subtract).then_inc(s[f"{ph}_cTl_ready"], 1)

                def product(i, c):
                    if not gated:
                        return
                    M = last[c]
                    if c >= 3:
                        ve.wait_ge(s[f"{ph}_hl_ready"], START + i * chunks + c - 2)
                    ve.wait_ge(s[f"{ph}_silu"], START + i * chunks + c + 1)
                    ve.tensor_tensor(f["act"][c % 3][0:M, :], bank[2 + c % 2][0:M, :], f["s"][c % 2][0:M, :],
                                     ALU.mult).then_inc(s[f"{ph}_act_ready"], 1)

                def scaled(i, c):
                    M = last[c]
                    ve.wait_ge(s[f"{ph}_cb_psum"], START + i * chunks + c + 1)
                    if gated:
                        ve.wait_ge(s[f"{ph}_act_ready"], START + i * chunks + c + 1)
                        other = f["act"][c % 3]
                    else:
                        if c >= 3:
                            ve.wait_ge(s[f"{ph}_hl_ready"], START + i * chunks + c - 2)
                        ve.wait_ge(s[f"{ph}_silu"], START + i * chunks + c + 1)
                        other = f["s"][c % 2]
                    ve.tensor_tensor(f["act"][c % 3][0:M, :], bank[4][0:M, :], other[0:M, :],
                                     ALU.mult).then_inc(s[f"{ph}_scaled"], 1)

                def low(i, c):
                    M = last[c]
                    ve.wait_ge(s[f"{ph}_hh_ready"], START + i * chunks + c + 1)
                    ve.tensor_tensor(f["hl"][c % 3][0:M, :], f["act"][c % 3][0:M, :], f["hh"][c % 3][0:M, :],
                                     ALU.subtract).then_inc(s[f"{ph}_hl_ready"], 1)

                def block_(i, u, more):
                    at = SLOTS[ph]
                    for t in range(chunks + 2):
                        if 0 <= t - 1 < chunks:
                            scaled(i, t - 1)
                        if t < chunks:
                            product(i, t)
                        if 0 <= t - 2 < chunks:
                            low(i, t - 2)
                        if more:
                            if t == at["norm"]:
                                norm(i + 1, 1 - u)
                            if t == at["t0"]:
                                xT_low(i + 1, 1 - u, 0)
                            if t == at["t1"]:
                                xT_low(i + 1, 1 - u, 1)
                            if t == at["largest"]:
                                largest(i + 1, 1 - u)
                            if t == at["weigh"]:
                                weights(i + 1, 1 - u)
                            if t == at["weights"]:
                                weights_low(i + 1, 1 - u)
                    ve.wait_ge(s[f"{ph}_down_done"], START + i * chunks + chunks)
                    for y in range(2):
                        xt = x[:, ds(i * FT + 2 * y, 2), :].rearrange("p a d -> p (a d)")
                        st.done(ve.scalar_tensor_tensor(out=xt, in0=bank[5 + 2 * y][:, :], scalar=gates[:, gate:gate + 1], in1=xt,
                                                        op0=ALU.mult, op1=ALU.add))
                    st.wait()
                    ve.sem_inc(s[f"{ph}_resid"], 1)
                    if out_stats:
                        moments(i * FT, FT)

                norm(0, 0)
                xT_low(0, 0, 0)
                xT_low(0, 0, 1)
                largest(0, 0)
                weights(0, 0)
                weights_low(0, 0)
                with ve.Fori(0, NF // 2 - 1) as j:
                    st.loop(j, STEPS[ph])
                    for u in range(2):
                        block_(j * 2 + u, u, True)
                st.end(NF // 2 - 1)
                block_(NF - 2, 0, True)
                block_(NF - 1, 1, False)
                st.wait()
                ve.sem_inc(s[f"{ph}_loop_done"], 1)

            stats(1)
            split_router(f0, 0, 16, False)
            ffn("f0", f0, NC0, HID0, True, 1, True)
            stats(2)
            ve.wait_ge(s["mask_loaded"], 16)
            st.done(ve.tensor_copy(maskrow[0:B, :], maskraw.bitcast(U8)[0:B, :]))
            st.wait()
            st.done(ve.tensor_reduce(validb[0:B, 0:1], maskrow[0:B, :], AX_X, ALU.max))
            st.wait()
            st.done(ve.tensor_copy(valid[0:B, :], validb[0:B, 0:1].broadcast_to([B, P])))
            st.done(ve.tensor_scalar(maskrow[0:B, :], maskrow[0:B, :], 1.0, -MASKED, ALU.subtract, ALU.mult))
            st.wait()
            ve.sem_inc(s["mask_ready"], 1)
            for h in range(H1):
                ve.wait_ge(s["scalar_steps"], h + 1)
                ve.tensor_tensor(m_lo[:, h].rearrange("p k c -> p (k c)"), bank[h % 2][:, 0:256],
                                 m_hi[:, h].rearrange("p k c -> p (k c)"), ALU.subtract).then_inc(s["m_copied"], 1)
            for c in range(H1 // 2):
                ve.wait_ge(s["scalar_steps"], H1 + c + 1)
                ve.tensor_tensor(n_lo[:, 2 * c:2 * c + 2, :].rearrange("p u n -> p (u n)"), bank[2 + c % 2][:, :],
                                 n_hi[:, 2 * c:2 * c + 2, :].rearrange("p u n -> p (u n)"), ALU.subtract).then_inc(s["n_copied"], 1)
            ve.wait_ge(s["valid_psum"], 1)
            st.done(ve.tensor_copy(validb, bank[0][:, 0:B]))
            st.wait()
            ve.sem_inc(s["valid_ready"], 1)
            ve.wait_ge(s["n_psum"], H1 // 2)
            st.done(ve.memset(ones_raw, 1.0))
            st.wait()
            ve.tensor_copy(ones, ones_raw).then_inc(s["ones_ready"], 1)
            ve.wait_ge(s["o1_loaded"], 48)
            st.done(ve.tensor_copy(w1_hi, w1_raw))
            st.wait()
            ve.tensor_tensor(w1_lo, w1_raw, w1_hi, ALU.subtract).then_inc(s["w1_split"], 1)
            NB = 4

            def norm1(i):
                ve.wait_ge(s["b_xnT_psum"], START + i)
                st.done(normalise(xn_b[:, 0:1, :], i * 2))
                st.done(normalise(xn_b[:, 1:2, :], i * 2 + 1))
                st.wait()
                ve.sem_inc(s["b_xn_ready"], 1)

            def xT_low1(i):
                ve.wait_ge(s["b_xh_ready"], START + i + 1)
                ve.tensor_tensor(xl_b.rearrange("p k t -> p (k t)"), bank[2][:, :],
                                 xh_b.rearrange("p k t -> p (k t)"), ALU.subtract).then_inc(s["b_xl_ready"], 1)

            def resid1(i, t):
                ve.wait_ge(s["b_y_psum"], START + i * 2 + t + 1)
                xt = x[:, ds(i * 2 + t, 1), :].rearrange("p a d -> p (a d)")
                ve.scalar_tensor_tensor(out=xt, in0=bank[3][:, 0:D], scalar=gates[:, 2:3], in1=xt,
                                        op0=ALU.mult, op1=ALU.add).then_inc(s["b_resid"], 1)

            def moments1(i):
                ve.wait_ge(s["b_resid"], START + i * 2 + 2)
                ve.sem_inc(s["vector_passed"], 1)
                moments(i * 2, 2)

            def mask_row(i):
                ve.wait_ge(s["b_ctx_loaded"], i * 32 + 32)
                ve.wait_ge(s["b_scores"], START + i * NB)
                ve.tensor_copy(mrow[0:1, :], mrow_raw[0:1, :]).then_inc(s["b_mrow"], 1)

            def ptl(i, b):
                ve.wait_ge(s["b_pTh"], START + i * NB + b + 1)
                ve.tensor_tensor(pTl, bank[2][:, :], pTh, ALU.subtract).then_inc(s["b_pTl"], 1)

            def otl(i, b):
                for par in range(2):
                    ve.wait_ge(s["b_oTh"], START + i * NB * 2 + 2 * b + par + 1)
                    cols = slice((b % 2) * S, (b % 2 + 1) * S)
                    ve.tensor_tensor(oTl[:, b // 2, :, par, :, cols],
                                     bank[4 + par][:, :].rearrange("p (j u q) -> p j u q", j=4, u=2),
                                     oTh[:, b // 2, :, par, :, cols], ALU.subtract).then_inc(s["b_oTl"], 1)

            def attend1(i, first=False, last=False):
                def centre(b):
                    ve.wait_ge(s["b_scores"], START + i * NB + b + 1)
                    sc = bank[b % 2][:, :].rearrange("p (g k) -> p g k", g=G1)
                    st.done(ve.tensor_reduce(rm_b[:, b % 2, :], sc, AX_X, ALU.max))
                    ve.wait_ge(s["b_pT_psum"], START + i * NB)
                    st.wait()
                    ve.tensor_tensor(probs_b[b], sc, rm_b[:, b % 2, :].unsqueeze(2).broadcast_to([P, G1, S]),
                                     ALU.subtract).then_inc(s["b_centred"], 1)

                def weigh(b):
                    ve.wait_ge(s["b_exp"], START + i * NB + b + 1)
                    st.done(ve.tensor_reduce(rs_b[:, b, :], probs_b[b], AX_X, ALU.add))
                    st.wait()
                    st.done(ve.reciprocal(rs_b[:, b, :], rs_b[:, b, :]))
                    st.wait()
                    ve.tensor_scalar(rs_b[:, b, :], rs_b[:, b, :], validb[:, ds(i * NB + b, 1)], None,
                                     ALU.mult).then_inc(s["b_recip"], 1)

                centre(0)
                if not first:
                    otl(i - 1, 3)
                    resid1(i - 1, 0)
                if not last:
                    norm1(i + 1)
                centre(1)
                weigh(0)
                centre(2)
                weigh(1)
                if not last:
                    xT_low1(i + 1)
                centre(3)
                ve.wait_ge(s["b_cxh"], START + i + 1)
                ve.tensor_tensor(cx_lo, cx_raw, cx_hi, ALU.subtract).then_inc(s["b_cxl"], 1)
                ptl(i, 0)
                weigh(2)
                weigh(3)
                otl(i, 0)
                ptl(i, 1)
                if not first:
                    resid1(i - 1, 1)
                    moments1(i - 1)
                otl(i, 1)
                ptl(i, 2)
                if not last:
                    mask_row(i + 1)
                otl(i, 2)
                ptl(i, 3)

            norm1(0)
            xT_low1(0)
            mask_row(0)
            attend1(0, first=True)
            with ve.Fori(1, NA - 1) as i:
                st.loop(i, STEPS["b"], 1)
                attend1(i)
            st.end(NA - 1)
            attend1(NA - 1, last=True)
            otl(NA - 1, 3)
            resid1(NA - 1, 0)
            resid1(NA - 1, 1)
            moments1(NA - 1)
            st.wait()
            stats(3)
            split_router(f1, 1, 48, True)
            ffn("f1", f1, NC1, HID1, False, 3, False)


def _layouts(v):
    f = np.float32
    c = np.ascontiguousarray

    def cols(w):
        return c(w.reshape(-1, P, w.shape[1]).transpose(1, 0, 2).reshape(P, -1))

    o = {}
    o["x"] = v["x"].reshape(T, D)
    o["ctx"] = v["ctx_1024"]
    o["ctxT"] = c(v["ctx_1024"].reshape(T, CD).T)
    fs = v["fside_BxSx2_0"].reshape(NT, 2, S, 2)
    d = np.arange(HD0)
    axis, half = d // 4, (d % 4) // 2
    o["pos"] = c(fs.transpose(1, 3, 0, 2)[:, axis].reshape(P, 256))
    freq = (ROPE_BASE ** (-(half.astype(f)) / f(2))).astype(f)
    sign = np.where(d % 2 == 0, -1.0, 1.0).astype(f)
    per = np.stack([freq * sign, freq, np.zeros(HD0, f), np.full(HD0, np.pi / 2, f)], 1)
    o["freq"] = c(np.broadcast_to(per[None, :, None, :], (2, HD0, 8, 4)).reshape(P, 4).astype(f))
    g = np.stack([v["g_xattn"][0], v["g_ffn"][0], v["g_xattn"][1], v["g_ffn"][1]])
    o["gates"] = c(np.broadcast_to(g[None, :], (P, 4)))
    o["ident"] = np.eye(P, dtype=f)
    p = np.arange(P)
    o["headmask"] = ((p[:, None] % 64) // 8 == np.arange(E)[None, :]).astype(f)
    o["ownbatch"] = ((p[:, None] // 16) % 2 == p[None, :] // 64).astype(f)
    o["iota8"] = c(np.broadcast_to(np.arange(E, dtype=f)[None, :], (P, E)))
    o["bout"] = c(np.broadcast_to(v["L0_xattn_bout"][None, :], (P, D)))
    o["bup"] = c(v["L1_ffn_bup"].T)
    o["mask"] = v["mask_BxS2_bf1"].view(np.uint8)
    o["wq0"] = cols(v["L0_xattn_Wq"])
    o["wk0"] = c(v["L0_xattn_Wkv"][:, :D])
    wv = v["L0_xattn_Wkv"][:, D:].reshape(CD, 16, 2, HD0)
    o["wv0"] = c(wv.transpose(0, 2, 1, 3).reshape(CD, 2 * P))
    wo = v["L0_xattn_Wout"].reshape(HG, 4, 1, 2, HD0, D)
    o["wo0"] = cols(np.broadcast_to(wo, (HG, 4, 2, 2, HD0, D)).reshape(HG * P, D))
    gu, pad = v["L0_ffn_gate_up_proj"], NC0 * P - HID0
    z = np.zeros((pad, D), f)
    gate = np.concatenate([gu[:, :I_MOE].reshape(-1, D), v["L0_ffn_sh_gate_w"], z])
    up = np.concatenate([gu[:, I_MOE:].reshape(-1, D), v["L0_ffn_sh_up_w"], z])
    down = np.concatenate([v["L0_ffn_down_proj"].transpose(0, 2, 1).reshape(-1, D), v["L0_ffn_sh_down_w"].T, z])
    o["w0"] = c(np.concatenate([cols(gate.T), cols(up.T), cols(down)], 1))
    rw = np.concatenate([v["L0_ffn_router_weight"], v["L0_ffn_shared_gate_w"], np.zeros((1, D), f)])
    o["rw0"] = cols(rw.T)
    unit = np.arange(NC0 * P)
    owner = np.where(unit < E * I_MOE, unit // I_MOE, E)
    sel = np.zeros((KC, NC0 * P), f)
    sel[owner, unit] = 1
    sel[LOW + owner, unit] = 1
    o["sel0"] = sel
    o["wq1"] = c(v["L1_xattn_Wq"].reshape(D, H1, P).transpose(2, 1, 0).reshape(P, -1))
    o["wk1"] = c(v["L1_xattn_Wk"].reshape(CD, G1, P).transpose(2, 1, 0).reshape(P, -1))
    o["wv1"] = c(v["L1_xattn_Wv"].reshape(CD, G1, P).transpose(2, 1, 0).reshape(P, -1))
    o["wo1"] = cols(v["L1_xattn_Wo"])
    o["w1"] = c(np.concatenate([cols(v["L1_ffn_Wup"].reshape(HID1, D).T),
                                cols(v["L1_ffn_Wdown"].transpose(0, 2, 1).reshape(HID1, D))], 1))
    o["rw1"] = cols(np.concatenate([v["L1_ffn_Wg1"], np.zeros((2, D), f)]).T)
    o["wg2"] = c(v["L1_ffn_Wg2"].T)
    unit = np.arange(HID1)
    sel = np.zeros((KC, HID1), f)
    sel[unit // P, unit] = 1
    sel[LOW + unit // P, unit] = 1
    o["sel1"] = sel
    bd = np.zeros((KC, D), f)
    bd[0:E] = v["L1_ffn_bdown"]
    bd[LOW:LOW + E] = v["L1_ffn_bdown"]
    o["bdown"] = bd
    return o


def kernel(**inputs):
    import concourse.bacc as _bacc
    from concourse.bass_utils import run_bass_kernel_spmd as _run

    arrays = _layouts({k: np.asarray(v) for k, v in inputs.items()})
    nc = _bacc.Bacc("TRN2", target_bir_lowering=False, num_devices=1)
    a = {k: nc.dram_tensor(f"in_{k}", w.shape, mybir.dt.from_np(w.dtype), kind="ExternalInput").ap()
         for k, w in arrays.items()}
    out = nc.dram_tensor("out_0", (T, D), F32, kind="ExternalOutput").ap()
    build(nc, a, out)
    r = _run(nc, [{f"in_{k}": w for k, w in arrays.items()}], core_ids=[0])
    return r.results[0]["out_0"].reshape(B, S, D)
```
